# Optimizing a Trainium2 kernel written in Bass

```python
import numpy as np
import jax
import jax.numpy as jnp

def _softmax(x, axis=-1):
    return jax.nn.softmax(x, axis=axis)

def _gelu(x):
    return jax.nn.gelu(x, approximate=True)

def _silu(x):
    return jax.nn.silu(x)

def _sigmoid(x):
    return jax.nn.sigmoid(x)

def _layernorm(x, axis=-1, eps=1e-05):
    m = jnp.mean(x, axis=axis, keepdims=True)
    v = jnp.var(x, axis=axis, keepdims=True)
    return (x - m) / jnp.sqrt(v + eps)

def _scatter_add(tgt, idx, src, axis=0):
    return tgt.at[idx].add(src)

def _segment_sum(src, seg, n):
    return jax.ops.segment_sum(src, seg, n)
kernel_name = 'mk_seq_preln_d2_jaxref_r8_d2776e'

def setup_inputs(seed: int=0):
    np.random.seed(seed)
    _w = jnp.asarray

    def _L0_attn_setup():
        import jax, jax.numpy as jnp
        import numpy as np
        EPS = 1e-06

        def _rmsnorm(x, w):
            ms = jnp.mean(jnp.square(x), axis=-1, keepdims=True)
            return x * jax.lax.rsqrt(ms + EPS) * w
        key = jax.random.key(seed)
        k1, k2, k3 = jax.random.split(key, 3)
        B, T, D = (4, 512, 128)
        d_inner = D
        x = jax.random.normal(k1, (B, T, D), dtype=jnp.float32)
        w_norm = jnp.ones((D,), dtype=jnp.float32)
        W_in = jax.random.normal(k2, (D, 3 * d_inner), dtype=jnp.float32) / np.sqrt(D)
        lambda_log = jnp.full((d_inner,), -0.5, dtype=jnp.float32)
        W_out = jax.random.normal(k3, (d_inner, D), dtype=jnp.float32) / np.sqrt(d_inner)
        return {'x': x, 'w_norm': w_norm, 'W_in': W_in, 'lambda_log': lambda_log, 'W_out': W_out}
    _L0_attn_in = _L0_attn_setup()

    def _L0_ffn_setup():
        import jax, jax.numpy as jnp
        import numpy as np
        R = 64
        key = jax.random.key(seed)
        k1, k2, k3 = jax.random.split(key, 3)
        B, S, D_IN, D_OUT = (8, 512, 128, 128)
        x = jax.random.normal(k1, (B, S, D_IN), dtype=jnp.float32)
        weight = jax.random.normal(k2, (D_OUT, D_IN), dtype=jnp.float32) * (1.0 / np.sqrt(D_IN))
        disha = jax.random.normal(k3, (R, D_OUT), dtype=jnp.float32) * 0.01
        return {'x': x, 'weight': weight, 'disha': disha}
    _L0_ffn_in = _L0_ffn_setup()

    def _L1_attn_setup():
        import jax, jax.numpy as jnp
        import numpy as np
        from jax import lax
        LN_EPS = 1e-05
        B, T, C = (4, 512, 128)

        def _layernorm(x, w, b):
            mu = jnp.mean(x, axis=-1, keepdims=True)
            var = jnp.mean((x - mu) ** 2, axis=-1, keepdims=True)
            return (x - mu) * lax.rsqrt(var + LN_EPS) * w + b
        key = jax.random.key(seed)
        ks = jax.random.split(key, 12)
        s = 1.0 / np.sqrt(C)
        return {'x': jax.random.normal(ks[0], (B, T, C), dtype=jnp.float32), 'time_mix_k': jax.random.uniform(ks[1], (C,), dtype=jnp.float32), 'time_mix_v': jax.random.uniform(ks[2], (C,), dtype=jnp.float32), 'time_mix_r': jax.random.uniform(ks[3], (C,), dtype=jnp.float32), 'time_decay': jnp.zeros((C,), dtype=jnp.float32), 'time_first': jnp.zeros((C,), dtype=jnp.float32), 'Wk': jax.random.uniform(ks[4], (C, C), jnp.float32, -s, s), 'Wv': jax.random.uniform(ks[5], (C, C), jnp.float32, -s, s), 'Wr': jax.random.uniform(ks[6], (C, C), jnp.float32, -s, s), 'Wo': jax.random.uniform(ks[7], (C, C), jnp.float32, -s, s), 'ln_w': jnp.ones((C,), dtype=jnp.float32), 'ln_b': jnp.zeros((C,), dtype=jnp.float32)}
    _L1_attn_in = _L1_attn_setup()

    def _L1_ffn_setup():
        import jax, jax.numpy as jnp
        import numpy as np
        EPS = 1e-05

        def _layernorm(x, w, b):
            mu = jnp.mean(x, axis=-1, keepdims=True)
            var = jnp.mean((x - mu) ** 2, axis=-1, keepdims=True)
            return (x - mu) * jax.lax.rsqrt(var + EPS) * w + b

        def _rope_tables(T, D, base=10000.0):
            inv_freq = 1.0 / base ** (jnp.arange(0, D, 2, dtype=jnp.float32) / D)
            t = jnp.arange(T, dtype=jnp.float32)
            freqs = jnp.einsum('i,j->ij', t, inv_freq)
            emb = jnp.concatenate([freqs, freqs], axis=-1)
            return (jnp.cos(emb), jnp.sin(emb))

        def _rotate_half(x):
            x1, x2 = (x[..., :x.shape[-1] // 2], x[..., x.shape[-1] // 2:])
            return jnp.concatenate([-x2, x1], axis=-1)

        def _attn(x, ln_w, ln_b, conv_w, attn_w, proj_w, n_head):
            B, T, C = x.shape
            D = C // n_head
            h = _layernorm(x, ln_w, ln_b)
            hc = jnp.transpose(h, (0, 2, 1))
            hc = jnp.pad(hc, ((0, 0), (0, 0), (2, 0)))
            hc = jax.lax.conv_general_dilated(hc, conv_w, window_strides=(1,), padding='VALID', dimension_numbers=('NCH', 'OIH', 'NCH'), feature_group_count=C)
            h = jnp.transpose(hc, (0, 2, 1))
            qkv = h @ attn_w
            q, k, v = jnp.split(qkv, 3, axis=-1)
            q = q.reshape(B, T, n_head, D)
            k = k.reshape(B, T, n_head, D)
            v = v.reshape(B, T, n_head, D)
            cos, sin = _rope_tables(T, D)
            cos = cos[None, :, None, :]
            sin = sin[None, :, None, :]
            q = q * cos + _rotate_half(q) * sin
            k = k * cos + _rotate_half(k) * sin
            scores = jnp.einsum('bqhd,bkhd->bhqk', q, k) / jnp.sqrt(jnp.float32(D))
            causal = jnp.tril(jnp.ones((T, T), dtype=bool))
            scores = jnp.where(causal, scores, jnp.float32(-1e+30))
            p = jax.nn.softmax(scores, axis=-1)
            y = jnp.einsum('bhqk,bkhd->bqhd', p, v).reshape(B, T, C)
            return y @ proj_w

        def _moe(x, ln_w, ln_b, router_w, expert_wv, expert_proj):
            h = _layernorm(x, ln_w, ln_b)
            logits = h @ router_w
            expert_idx = jnp.argmax(logits, axis=-1)
            E = router_w.shape[-1]
            out = jnp.zeros_like(x)
            for e in range(E):
                gv = h @ expert_wv[e]
                gate_raw, value = jnp.split(gv, 2, axis=-1)
                y = gate_raw * jax.nn.sigmoid(gate_raw) * value @ expert_proj[e]
                out = out + jnp.where((expert_idx == e)[..., None], y, 0.0)
            return out
        C, H, E, B, T = (128, 16, 4, 4, 128)
        Dff = 4 * C
        key = jax.random.key(seed)
        ks = jax.random.split(key, 8)
        s = 0.02
        return {'x': jax.random.normal(ks[0], (B, T, C), dtype=jnp.float32), 'ln1_w': jnp.ones((C,), jnp.float32), 'ln1_b': jnp.zeros((C,), jnp.float32), 'ln2_w': jnp.ones((C,), jnp.float32), 'ln2_b': jnp.zeros((C,), jnp.float32), 'conv_w': jax.random.normal(ks[1], (C, 1, 3), dtype=jnp.float32) * 0.1, 'attn_w': jax.random.normal(ks[2], (C, 3 * C), dtype=jnp.float32) * s, 'proj_w': jax.random.normal(ks[3], (C, C), dtype=jnp.float32) * s, 'router_w': jax.random.normal(ks[4], (C, E), dtype=jnp.float32) * s, 'expert_wv': jax.random.normal(ks[5], (E, C, 2 * Dff), dtype=jnp.float32) * s, 'expert_proj': jax.random.normal(ks[6], (E, Dff, C), dtype=jnp.float32) * s}
    _L1_ffn_in = _L1_ffn_setup()
    _d = {'L0_attn_x': _L0_attn_in['x'], 'L0_attn_w_norm': _L0_attn_in['w_norm'], 'L0_attn_W_in': _L0_attn_in['W_in'], 'L0_attn_lambda_log': _L0_attn_in['lambda_log'], 'L0_attn_W_out': _L0_attn_in['W_out'], 'L0_ffn_weight': _L0_ffn_in['weight'], 'L0_ffn_disha': _L0_ffn_in['disha'], 'L1_attn_time_mix_k': _L1_attn_in['time_mix_k'], 'L1_attn_time_mix_v': _L1_attn_in['time_mix_v'], 'L1_attn_time_mix_r': _L1_attn_in['time_mix_r'], 'L1_attn_time_decay': _L1_attn_in['time_decay'], 'L1_attn_time_first': _L1_attn_in['time_first'], 'L1_attn_Wk': _L1_attn_in['Wk'], 'L1_attn_Wv': _L1_attn_in['Wv'], 'L1_attn_Wr': _L1_attn_in['Wr'], 'L1_attn_Wo': _L1_attn_in['Wo'], 'L1_attn_ln_w': _L1_attn_in['ln_w'], 'L1_attn_ln_b': _L1_attn_in['ln_b'], 'L1_ffn_ln1_w': _L1_ffn_in['ln1_w'], 'L1_ffn_ln1_b': _L1_ffn_in['ln1_b'], 'L1_ffn_ln2_w': _L1_ffn_in['ln2_w'], 'L1_ffn_ln2_b': _L1_ffn_in['ln2_b'], 'L1_ffn_conv_w': _L1_ffn_in['conv_w'], 'L1_ffn_attn_w': _L1_ffn_in['attn_w'], 'L1_ffn_proj_w': _L1_ffn_in['proj_w'], 'L1_ffn_router_w': _L1_ffn_in['router_w'], 'L1_ffn_expert_wv': _L1_ffn_in['expert_wv'], 'L1_ffn_expert_proj': _L1_ffn_in['expert_proj']}
    _x0 = _d['L0_attn_x']
    _d['L0_attn_x'] = jax.random.normal(jax.random.fold_in(jax.random.key(seed), 1), (16, 256, 128), dtype=_x0.dtype)
    del _x0
    return _d

def reference(L0_attn_x, L0_attn_w_norm, L0_attn_W_in, L0_attn_lambda_log, L0_attn_W_out, L0_ffn_weight, L0_ffn_disha, L1_attn_time_mix_k, L1_attn_time_mix_v, L1_attn_time_mix_r, L1_attn_time_decay, L1_attn_time_first, L1_attn_Wk, L1_attn_Wv, L1_attn_Wr, L1_attn_Wo, L1_attn_ln_w, L1_attn_ln_b, L1_ffn_ln1_w, L1_ffn_ln1_b, L1_ffn_ln2_w, L1_ffn_ln2_b, L1_ffn_conv_w, L1_ffn_attn_w, L1_ffn_proj_w, L1_ffn_router_w, L1_ffn_expert_wv, L1_ffn_expert_proj):

    def _L0_attn_ref(x, w_norm, W_in, lambda_log, W_out):
        import jax, jax.numpy as jnp
        import numpy as np
        EPS = 1e-06

        def _rmsnorm(x, w):
            ms = jnp.mean(jnp.square(x), axis=-1, keepdims=True)
            return x * jax.lax.rsqrt(ms + EPS) * w
        B, T, D = x.shape
        residual = x
        x_norm = _rmsnorm(x, w_norm)
        proj = jnp.einsum('btd,de->bte', x_norm, W_in)
        gate_a, gate_r, v = jnp.split(proj, 3, axis=-1)
        a = jax.nn.sigmoid(gate_a)
        r = jax.nn.sigmoid(gate_r)
        v = jax.nn.gelu(v, approximate=False)
        lam = jax.nn.sigmoid(lambda_log)
        u = (1.0 - a) * (r * v) * lam
        a_t = jnp.swapaxes(a, 0, 1)
        u_t = jnp.swapaxes(u, 0, 1)

        def step(h, au):
            at, ut = au
            h = at * h + ut
            return (h, h)
        h0 = jnp.zeros((B, a.shape[-1]), dtype=x.dtype)
        _, ys = jax.lax.scan(step, h0, (a_t, u_t))
        y = jnp.swapaxes(ys, 0, 1)
        return residual + jnp.einsum('bte,ed->btd', y, W_out)

    def _L0_ffn_ref(x, weight, disha):
        import jax, jax.numpy as jnp
        import numpy as np
        R = 64
        result = jnp.einsum('bsd,od->bso', x, weight)
        r = disha.shape[0]
        pooled = x.reshape(*x.shape[:-1], x.shape[-1] // r, r).sum(axis=-2)
        return result + pooled @ disha

    def _L1_attn_ref(x, time_mix_k, time_mix_v, time_mix_r, time_decay, time_first, Wk, Wv, Wr, Wo, ln_w, ln_b):
        import jax, jax.numpy as jnp
        import numpy as np
        from jax import lax
        LN_EPS = 1e-05
        B, T, C = (4, 512, 128)

        def _layernorm(x, w, b):
            mu = jnp.mean(x, axis=-1, keepdims=True)
            var = jnp.mean((x - mu) ** 2, axis=-1, keepdims=True)
            return (x - mu) * lax.rsqrt(var + LN_EPS) * w + b
        xt = _layernorm(x, ln_w, ln_b)
        x_prev = jnp.pad(xt[:, :-1], ((0, 0), (1, 0), (0, 0)))
        decay = jax.nn.sigmoid(time_decay)
        first = jnp.exp(time_first)
        mk, mv, mr = (time_mix_k, time_mix_v, time_mix_r)
        K = jnp.einsum('btc,dc->btd', xt * mk + x_prev * (1.0 - mk), Wk)
        V = jnp.einsum('btc,dc->btd', xt * mv + x_prev * (1.0 - mv), Wv)
        R = jax.nn.sigmoid(jnp.einsum('btc,dc->btd', xt * mr + x_prev * (1.0 - mr), Wr))

        def step(state, k_t):
            state = state * decay + k_t
            return (state, state)
        _, S = lax.scan(step, jnp.zeros((x.shape[0], K.shape[-1]), x.dtype), jnp.swapaxes(K, 0, 1))
        S = jnp.swapaxes(S, 0, 1)
        rwkv = (S * first + K) * V
        y = jnp.einsum('btc,dc->btd', R * rwkv, Wo)
        return x + y

    def _L1_ffn_ref(x, ln1_w, ln1_b, ln2_w, ln2_b, conv_w, attn_w, proj_w, router_w, expert_wv, expert_proj):
        import jax, jax.numpy as jnp
        import numpy as np
        EPS = 1e-05

        def _layernorm(x, w, b):
            mu = jnp.mean(x, axis=-1, keepdims=True)
            var = jnp.mean((x - mu) ** 2, axis=-1, keepdims=True)
            return (x - mu) * jax.lax.rsqrt(var + EPS) * w + b

        def _rope_tables(T, D, base=10000.0):
            inv_freq = 1.0 / base ** (jnp.arange(0, D, 2, dtype=jnp.float32) / D)
            t = jnp.arange(T, dtype=jnp.float32)
            freqs = jnp.einsum('i,j->ij', t, inv_freq)
            emb = jnp.concatenate([freqs, freqs], axis=-1)
            return (jnp.cos(emb), jnp.sin(emb))

        def _rotate_half(x):
            x1, x2 = (x[..., :x.shape[-1] // 2], x[..., x.shape[-1] // 2:])
            return jnp.concatenate([-x2, x1], axis=-1)

        def _attn(x, ln_w, ln_b, conv_w, attn_w, proj_w, n_head):
            B, T, C = x.shape
            D = C // n_head
            h = _layernorm(x, ln_w, ln_b)
            hc = jnp.transpose(h, (0, 2, 1))
            hc = jnp.pad(hc, ((0, 0), (0, 0), (2, 0)))
            hc = jax.lax.conv_general_dilated(hc, conv_w, window_strides=(1,), padding='VALID', dimension_numbers=('NCH', 'OIH', 'NCH'), feature_group_count=C)
            h = jnp.transpose(hc, (0, 2, 1))
            qkv = h @ attn_w
            q, k, v = jnp.split(qkv, 3, axis=-1)
            q = q.reshape(B, T, n_head, D)
            k = k.reshape(B, T, n_head, D)
            v = v.reshape(B, T, n_head, D)
            cos, sin = _rope_tables(T, D)
            cos = cos[None, :, None, :]
            sin = sin[None, :, None, :]
            q = q * cos + _rotate_half(q) * sin
            k = k * cos + _rotate_half(k) * sin
            scores = jnp.einsum('bqhd,bkhd->bhqk', q, k) / jnp.sqrt(jnp.float32(D))
            causal = jnp.tril(jnp.ones((T, T), dtype=bool))
            scores = jnp.where(causal, scores, jnp.float32(-1e+30))
            p = jax.nn.softmax(scores, axis=-1)
            y = jnp.einsum('bhqk,bkhd->bqhd', p, v).reshape(B, T, C)
            return y @ proj_w

        def _moe(x, ln_w, ln_b, router_w, expert_wv, expert_proj):
            h = _layernorm(x, ln_w, ln_b)
            logits = h @ router_w
            expert_idx = jnp.argmax(logits, axis=-1)
            E = router_w.shape[-1]
            out = jnp.zeros_like(x)
            for e in range(E):
                gv = h @ expert_wv[e]
                gate_raw, value = jnp.split(gv, 2, axis=-1)
                y = gate_raw * jax.nn.sigmoid(gate_raw) * value @ expert_proj[e]
                out = out + jnp.where((expert_idx == e)[..., None], y, 0.0)
            return out
        n_head = 16
        x = x + _attn(x, ln1_w, ln1_b, conv_w, attn_w, proj_w, n_head)
        x = x + _moe(x, ln2_w, ln2_b, router_w, expert_wv, expert_proj)
        return x
    x = L0_attn_x
    x = x + _L0_attn_ref(_layernorm(x, axis=-1), L0_attn_w_norm, L0_attn_W_in, L0_attn_lambda_log, L0_attn_W_out)
    x = x + _L0_ffn_ref(_layernorm(x, axis=-1), L0_ffn_weight, L0_ffn_disha)
    x = x + _L1_attn_ref(_layernorm(x, axis=-1), L1_attn_time_mix_k, L1_attn_time_mix_v, L1_attn_time_mix_r, L1_attn_time_decay, L1_attn_time_first, L1_attn_Wk, L1_attn_Wv, L1_attn_Wr, L1_attn_Wo, L1_attn_ln_w, L1_attn_ln_b)
    x = x + _L1_ffn_ref(_layernorm(x, axis=-1), L1_ffn_ln1_w, L1_ffn_ln1_b, L1_ffn_ln2_w, L1_ffn_ln2_b, L1_ffn_conv_w, L1_ffn_attn_w, L1_ffn_proj_w, L1_ffn_router_w, L1_ffn_expert_wv, L1_ffn_expert_proj)
    return x

_drawn_inputs = setup_inputs


def setup_inputs(seed=0):
    import zlib

    import numpy as np

    out = dict(_drawn_inputs(seed))
    spreads = {'L0_attn_w_norm': (1.0, 0.6),
     'L0_attn_lambda_log': (-0.5, 0.6),
     'L1_attn_time_decay': (0.0, 0.8),
     'L1_attn_time_first': (0.0, 0.8),
     'L1_attn_ln_w': (1.0, 0.6),
     'L1_attn_ln_b': (0.0, 0.8),
     'L1_ffn_ln1_w': (1.0, 0.6),
     'L1_ffn_ln1_b': (0.0, 0.8),
     'L1_ffn_ln2_w': (1.0, 0.6),
     'L1_ffn_ln2_b': (0.0, 0.8)}
    factors = {'L1_attn_time_mix_k': 3.236,
     'L1_attn_time_mix_r': 8.0,
     'L1_attn_Wr': 5.252,
     'L1_ffn_conv_w': 8.0,
     'L1_ffn_attn_w': 8.0,
     'L1_ffn_proj_w': 8.0,
     'L1_ffn_router_w': 8.0,
     'L1_ffn_expert_wv': 8.0,
     'L1_ffn_expert_proj': 8.0}
    for name, (base, spread) in spreads.items():
        noise = np.random.default_rng([zlib.crc32(name.encode()), seed]).standard_normal(out[name].shape)
        drawn = base * np.exp(spread * noise) if base else spread * noise
        out[name] = jnp.asarray(drawn.astype(out[name].dtype))
    for name, factor in factors.items():
        out[name] = (out[name] * factor).astype(out[name].dtype)
    return out
```

```python
from contextlib import ExitStack

import concourse.bass as bass
from concourse import mybir

F32 = mybir.dt.float32
BF16 = mybir.dt.bfloat16
ALU = mybir.AluOpType
ACT = mybir.ActivationFunctionType
AX_X = mybir.AxisListType.X
ds = bass.ds

P = 128
B, T, C = 16, 256, 128
TOK = B * T
NT = TOK // P
CH = 512
NCH = TOK // CH
TPC = CH // P
SPC = CH // T
H, D = 16, 8
E, FF = 4, 512
FB = FF // P
LN_EPS, RMS_EPS = 1e-5, 1e-6
SCALE = float(D) ** -0.5
Q_PART = (0, 0, 0, 1, 1, 2)
K_PART = (0, 1, 2, 0, 1, 0)
MAX_ROW = 96
LANES = 4
PARAMS = ["w_norm", "lambda_log", "mix_k", "mix_v", "mix_r", "decay", "first", "ln_w", "ln_b",
          "ln1_w", "ln1_b", "ln2_w", "ln2_b", "conv0", "conv1", "conv2"]
GROUPS = ((0, 0, 4), (0, 4, 4), (1, 0, 8), (0, 8, 4), (0, 12, 4), (1, 8, 8))
NG = len(GROUPS)
NS = 12


class Signal:

    def __init__(self, sem, per=1):
        self.sem, self.per = sem, per

    def start(self, eng):
        eng.sem_inc(self.sem, 2 * self.per)

    def done(self, c, n=None):
        return (c + 2) * self.per + (self.per if n is None else n)

    def freed(self, c):
        return (c + 1) * self.per


class Lanes:

    def __init__(self, sems, per):
        self.sems, self.per = sems, per

    def start(self, eng):
        for s in self.sems:
            eng.sem_inc(s, self.per)

    def wait_done(self, eng, u, turn):
        eng.wait_ge(self.sems[u], (turn + 2) * self.per)

    def wait_freed(self, eng, u, turn):
        eng.wait_ge(self.sems[u], (turn + 1) * self.per)


def run_steps(eng, n, step, lag, period=2):
    lo = (lag + period - 1) // period * period
    hi = lo + (n - lo) // period * period

    def fixed(s):
        step(s, lambda l: (s - l, (s - l) % period, (s - l) // period), lambda l: 0 <= s - l < n)

    for s in range(lo):
        fixed(s)
    if hi > lo:
        with eng.Fori(0, (hi - lo) // period) as i:
            for w in range(lo, lo + period):
                step(i * period + w,
                     lambda l: (i * period + (w - l), (w - l) % period, i + (w - l) // period),
                     lambda l: True)
    for s in range(hi, n + lag):
        fixed(s)


def in_turn(eng, n, parts, period=2):
    def step(s, at, live):
        for lag, part in parts:
            if live(lag):
                part(*at(lag))
    run_steps(eng, n, step, max(lag for lag, _ in parts), period)


def model_kernel(nc, x_in, params_in, w_in, w_out, w_ffn, disha2, w_kvr, w_o, w_qk, w_v, w_proj,
                 w_router, w_up, w_down, ident_in, rope_in, mask_in, pick_in, out):
    x_tiles = x_in.rearrange("(n p) c -> p n c", p=P)
    out_tiles = out.rearrange("(n p) c -> p n c", p=P)
    qk_dram = nc.dram_tensor("qk_parts", [2, 3, P, TOK], BF16, kind="Internal").ap()

    with ExitStack() as ctx:
        def sb(name, shape, dt=F32):
            return ctx.enter_context(nc.sbuf_tensor(name, shape, dt))

        def sem(name):
            return ctx.enter_context(nc.semaphore(name))

        def signal(name, per=1):
            return Signal(sem(name), per)

        X = sb("X", [P, NT, C])
        XRES = sb("XRES", [P, NT, C])
        Y = sb("Y", [P, NT, C])
        V = sb("V", [P, NT, C])
        XA = V
        bn = sb("bn", [P, NT, 6])
        mean, var, half = (sb(k, [P, NT]) for k in ("mean", "var", "half"))
        tv, r1, r2, rs, rp1, mr, minus_half = (
            sb(k, [P, NT]) for k in ("tv", "r1", "r2", "rs", "rp1", "mr", "minus_half"))
        params = sb("params", [P, len(PARAMS)])
        W_in = sb("W_in", [P, 3 * C])
        W_out = sb("W_out", [P, C])
        W_ffn = sb("W_ffn", [P, C])
        DISHA = sb("DISHA", [P, C])
        W_kvr = sb("W_kvr", [P, 3 * C])
        W_o = sb("W_o", [P, C])
        W_qk = sb("W_qk", [P, 4 * C])
        W_v = sb("W_v", [P, C])
        W_proj = sb("W_proj", [P, C])
        W_router = sb("W_router", [P, E])
        ident = sb("ident", [P, P])
        ident_b = sb("ident_b", [P, P], BF16)
        rope = sb("rope", [P, 2, T])
        masks = sb("masks", [P, 2, P])
        masks_b = sb("masks_b", [P, 2, 4, P], BF16)
        pick = sb("pick", [P, E])
        lam = sb("lam", [P, 2])
        dec = sb("dec", [P, 2])
        first = sb("first", [P, 1])
        decay_row = sb("decay_row", [P, T])
        ones = sb("ones", [P, T])
        xs = sb("xs", [P, 2, TPC, C])
        xT = sb("xT", [P, 2, CH])
        ta, tr, gv, ga, rv, uu, y = (sb(k, [P, 2, CH]) for k in ("ta", "tr", "gv", "ga", "rv", "uu", "y"))
        hp = sb("hp", [P, 2, SPC, T + 2])
        dif, sk, rg = ta, tr, gv
        mix = sb("mix", [P, 2, 3, CH])
        hc = ga
        rot = mix
        full, rem = rv, uu
        kq = Y[:].rearrange("p n c -> p (n c)").bitcast(BF16)[:, 0:2 * 2 * 3 * CH].rearrange(
            "p (u n a t) -> p u n a t", u=2, n=2, a=3)
        stack_q = sb("stack_q", [P, LANES * H * T // 2])
        QS = stack_q[:].bitcast(BF16).rearrange("p (l h t) -> p l h t", l=LANES, h=H)
        W_up = stack_q[:, 0:E * 2 * FF].rearrange("p (e f) -> p e f", e=E)
        W_down = stack_q[:, E * 2 * FF:E * 3 * FF].rearrange("p (e f c) -> p e f c", e=E, f=FB)
        KS = sb("KS", [P, LANES, H, T], BF16)
        Vx = sb("Vx", [P, 2, 2, H, 32])
        Pt = mix[:].rearrange("p u n t -> p (u n t)")[:, 0:2048].rearrange("p (u n) -> p u n", u=2)
        M = sb("M", [P, 2, 2, H])
        mp = hp[:].rearrange("p u s t -> p (u s t)").bitcast(BF16)[0:H, 0:LANES * 2 * T].rearrange(
            "h (l r t) -> h l r t", l=LANES, r=2)
        yr = xs[:].rearrange("p u t c -> p u (t c)")
        rden = sb("rden", [P, 2, 2, 2, 4])
        lmax, smax = (sb(k, [P, TPC]) for k in ("lmax", "smax"))
        eq, pk, oh = (sb(k, [P, TPC, E]) for k in ("eq", "pk", "oh"))
        sg, glu = ta, tr
        ps = ctx.enter_context(nc.psum_tensor("ps", [P, 8, 512], F32))

        def par(name):
            k = PARAMS.index(name)
            return params[:, k:k + 1]

        ld_x = [sem(f"ld_x{c}") for c in range(NCH)]
        ld_w = sem("ld_w")
        N_W = 15
        ld_e = sem("ld_e")
        prep = sem("prep")
        prep_act = sem("prep_act")
        prep_pool = sem("prep_pool")
        N_POOL = 8
        stat_v = sem("stat_v")
        stat_p = sem("stat_p")
        s_xs = signal("s_xs")
        s_new = signal("s_new")
        s_res = signal("s_res")
        s_tr = signal("s_tr")
        s_xT = signal("s_xT")
        s_out = signal("s_out")
        s_mmA = signal("s_mmA", 3)
        s_actA = signal("s_actA", 4)
        s_uu = signal("s_uu", 2)
        s_y = signal("s_y")
        s_dif = signal("s_dif")
        s_mix = signal("s_mix", 3)
        s_mmC = signal("s_mmC", 3)
        s_sig = signal("s_sig")
        s_kvC = signal("s_kvC", 4)
        s_conv = signal("s_conv", 3)
        s_mmD = signal("s_mmD", 5)
        s_rot = signal("s_rot", 4)
        s_full = signal("s_full", 2)
        s_hi = signal("s_hi", 4)
        s_lo = signal("s_lo", 4)
        s_v = signal("s_v")
        s_st = Lanes([sem(f"s_st{u}") for u in range(2)], 32)
        s_ldst = Lanes([sem(f"s_ldst{u}") for u in range(LANES)], 16 * 12)
        s_mrow = Lanes([sem(f"s_mrow{u}") for u in range(LANES)], 32)
        s_use = signal("s_use")
        s_S = signal("s_S", NS)
        s_max = signal("s_max", NS)
        s_mT = signal("s_mT")
        s_mp = signal("s_mp", 2)
        s_ST = signal("s_ST", NG)
        s_exp = signal("s_exp", NG)
        s_pv = signal("s_pv", NG)
        s_yr = signal("s_yr", 2)
        s_yT = signal("s_yT", 2)
        s_rden = signal("s_rden", 2)
        s_yn = signal("s_yn", 2)
        s_vx = signal("s_vx")
        s_yc = signal("s_yc")
        s_sum = signal("s_sum")
        s_rt = signal("s_rt")
        s_oh = signal("s_oh", 5)
        s_up = signal("s_up", 2 * E * FB)
        s_silu = signal("s_silu", E * FB)
        s_glu = signal("s_glu", E * FB)
        s_dn = signal("s_dn", E * FB)
        s_acc = signal("s_acc", E)
        stored = sem("stored")

        XS0 = {k: NCH * n for n, k in enumerate("ABCDG")}
        TR0 = {k: NCH * n for n, k in enumerate("ABCDFG")}
        RES0 = {k: NCH * n for n, k in enumerate("ACF")}
        NEW0 = {k: NCH * n for n, k in enumerate("ABCF")}
        TWICE = "ACD"
        SV0, SP0, v, p = {}, {}, 0, 0
        for k in "ABCDG":
            SV0[k], SP0[k] = v, p
            v += 10 if k in TWICE else 6
            p += 2 if k in TWICE else 1
        SV0["end"], SP0["end"] = v, p
        source = {"A": X, "B": X, "C": X, "D": X, "G": XA}

        block = ctx.enter_context(nc.Block())

        @block.sync
        def _(sp):
            for s in (s_st, s_ldst, s_mrow):
                s.start(sp)
            for c in range(NCH):
                sp.dma_start(X[:, c * TPC:(c + 1) * TPC, :], x_tiles[:, c * TPC:(c + 1) * TPC, :])\
                  .then_inc(ld_x[c], 16)
            for dst, src in ((params[:], params_in), (ident[:], ident_in), (W_in[:], w_in),
                             (W_out[:], w_out), (W_ffn[:], w_ffn), (DISHA[:], disha2),
                             (W_kvr[:], w_kvr), (W_o[:], w_o), (W_qk[:], w_qk), (W_v[:], w_v),
                             (W_proj[:], w_proj), (W_router[:], w_router), (rope[:], rope_in), (masks[:], mask_in),
                             (pick[:], pick_in)):
                sp.dma_start(dst, src).then_inc(ld_w, 16)

            def store_parts(c, u, turn):
                for n in range(2):
                    sp.wait_ge(s_lo.sem, s_lo.done(c, 2 * n + 2))
                    sp.dma_start(qk_dram[n, :, :, ds(c * CH, CH)].rearrange("a p t -> p a t"),
                                 kq[:, u, n, :, :]).then_inc(s_st.sems[u], 16)

            in_turn(sp, NCH, [(0, store_parts)])

            def load_stack(b, u, turn):
                sp.wait_ge(s_ST.sem, s_ST.per * (b - LANES + 3) if not isinstance(b, int) else
                           max(s_ST.per * (b - LANES + 3), 1))
                for n, (dst, split) in enumerate(((QS, Q_PART), (KS, K_PART))):
                    for k, part in enumerate(split):
                        sp.dma_start(
                            dst[D * k:D * (k + 1), u, :, :],
                            qk_dram[n, part, :, ds(b * T, T)].rearrange("(h d) t -> d h t", d=D),
                        ).then_inc(s_ldst.sems[u], 16)

            def max_rows(b, u, turn):
                sp.wait_ge(s_mp.sem, s_mp.done(b))
                for r in range(2):
                    sp.dma_start(QS[MAX_ROW + r:MAX_ROW + r + 1, u, :, :], mp[:, u, r, :])\
                      .then_inc(s_mrow.sems[u], 16)

            for u in range(2):
                s_st.wait_done(sp, u, NCH // 2 - 1)
            sp.wait_ge(prep_pool, N_POOL)
            in_turn(sp, B, [(0, load_stack), (2, max_rows)], LANES)

            sp.wait_ge(s_ST.sem, s_ST.done(B - 1))
            sp.dma_start(W_up, w_up).then_inc(ld_e, 16)
            sp.dma_start(W_down, w_down).then_inc(ld_e, 16)

            def store_out(c, u, turn):
                sp.wait_ge(s_acc.sem, s_acc.done(c))
                sp.dma_start(out_tiles[:, ds(c * TPC, TPC), :], XRES[:, ds(c * TPC, TPC), :]).then_inc(stored, 16)

            in_turn(sp, NCH, [(0, store_out)])
            sp.wait_ge(stored, 16 * NCH)

        @block.gpsimd
        def _(pool):
            for s in (s_dif, s_vx, s_full, s_sum):
                s.start(pool)
            fills = ((minus_half[:], -0.5), (ones[:], 1.0), (hp[:], 0.0), (QS, 0.0), (KS[:], 0.0), (Vx[:], 0.0),
                     (KS[MAX_ROW:MAX_ROW + 2, :, :, :], 1.0), (Vx[:, :, :, :, D:D + 1], 1.0))
            for n, (to, value) in enumerate(fills):
                if n:
                    pool.wait_ge(prep_pool, n)
                pool.memset(to, value).then_inc(prep_pool, 1)
            pool.wait_ge(prep_pool, N_POOL)

            def powers(stage):
                pool.wait_ge(stat_v, SV0[stage] + 4)
                pool.tensor_tensor(r1[:], tv[:], minus_half[:], ALU.pow).then_inc(stat_p, 1)
                if stage in TWICE:
                    pool.wait_ge(stat_v, SV0[stage] + 7)
                    pool.tensor_tensor(r2[:], tv[:], minus_half[:], ALU.pow).then_inc(stat_p, 1)

            powers("A")

            powers("B")
            powers("C")

            def shift(c, u, turn):
                pool.wait_ge(s_xT.sem, s_xT.done(TR0["C"] + c))
                pool.wait_ge(s_mix.sem, s_mix.freed(c))
                pool.tensor_tensor(dif[:, u, :].rearrange("p (s t) -> p s t", s=SPC), hp[:, u, :, 2:T + 2],
                                   hp[:, u, :, 1:T + 1], ALU.subtract).then_inc(s_dif.sem, 1)

            in_turn(pool, NCH, [(0, shift)])
            powers("D")

            def rotate(c, u, turn):
                for n in range(2):
                    pool.wait_ge(s_rot.sem, s_rot.done(c, 2 * n + 2))
                    pool.wait_ge(s_lo.sem, s_lo.done(c, 2 * n - 2 + 1))
                    pool.tensor_tensor(full[:, n, :], rot[:, n, 0, :], rot[:, n, 1, :], ALU.add)\
                        .then_inc(s_full.sem, 1)

            in_turn(pool, NCH, [(0, rotate)])

            def spread_values(b, u, turn):
                pool.wait_ge(s_pv.sem, s_pv.freed(b))
                for kb in range(2):
                    ins = pool.tensor_copy(
                        Vx[:, u % 2, kb, :, 0:D],
                        V[:, ds(b * 2 + kb, 1), :].rearrange("p o (h d) -> p (o h) d", h=H))
                ins.then_inc(s_vx.sem, 1)

            pool.wait_ge(s_v.sem, s_v.done(NCH - 1))
            in_turn(pool, B, [(0, spread_values)])

            def add_streams(c, u, turn):
                pool.wait_ge(s_new.sem, s_new.done(NEW0["F"] + c))
                pool.tensor_tensor(XRES[:, ds(c * TPC, TPC), :], X[:, ds(c * TPC, TPC), :],
                                   XA[:, ds(c * TPC, TPC), :], ALU.add).then_inc(s_sum.sem, 1)

            in_turn(pool, NCH, [(0, add_streams)])
            powers("G")

        @block.scalar
        def _(act):
            for s in (s_xT, s_actA, s_sig, s_hi, s_v, s_exp, s_yr, s_yc, s_silu):
                s.start(act)
            act.wait_ge(ld_w, 16 * N_W)
            nc.scalar.activation(first[:], par("first"), ACT.Exp).then_inc(prep_act, 1)
            nc.scalar.activation(lam[:, 0:1], par("lambda_log"), ACT.Tanh, scale=0.5).then_inc(prep_act, 1)
            nc.scalar.activation(dec[:, 0:1], par("decay"), ACT.Tanh, scale=0.5).then_inc(prep_act, 1)

            def copy_turned(stage, users):
                def part(c, u, turn):
                    act.wait_ge(s_tr.sem, s_tr.done(TR0[stage] + c))
                    for sig, value in users:
                        act.wait_ge(sig.sem, value(c))
                    nc.scalar.copy(xT[:, u, :], ps[:, 0, :]).then_inc(s_xT.sem, 1)
                return part

            def scale_turned(stage, dst, w, b, users):
                def part(c, u, turn):
                    act.wait_ge(s_tr.sem, s_tr.done(TR0[stage] + c))
                    for sig, value in users:
                        act.wait_ge(sig.sem, value(c))
                    src, to = ps[:, 0, :], dst[:, u]
                    if dst is hp:
                        src, to = src.rearrange("p (s t) -> p s t", s=SPC), hp[:, u, :, 2:T + 2]
                    nc.scalar.activation(to, src, ACT.Identity, bias=par(b), scale=par(w)).then_inc(s_xT.sem, 1)
                return part

            def act_a(c, u, turn):
                act.wait_ge(s_y.sem, s_y.freed(c))
                for n, (dst, fn, scale) in enumerate(((ta, ACT.Tanh, 0.5), (tr, ACT.Tanh, 0.5), (gv, ACT.Gelu, 1.0))):
                    act.wait_ge(s_mmA.sem, s_mmA.done(c, n + 1))
                    nc.scalar.activation(dst[:, u, :], ps[:, 1 + 3 * u + n, :], fn, scale=scale).then_inc(s_actA.sem, 1)
                act.wait_ge(s_actA.sem, s_actA.done(c, 1))
                nc.scalar.activation(ga[:, u, :], ta[:, u, :], ACT.Copy, bias=0.5, scale=0.5).then_inc(s_actA.sem, 1)

            in_turn(act, NCH, [(0, copy_turned("A", [(s_mmA, s_mmA.freed)])), (1, act_a)])
            out_b = lambda c: s_out.freed(NEW0["B"] + c)
            in_turn(act, NCH, [(0, copy_turned("B", [(s_out, out_b)]))])

            def act_c(c, u, turn):
                act.wait_ge(s_mmC.sem, s_mmC.done(c, 3))
                act.wait_ge(s_kvC.sem, s_kvC.freed(c))
                nc.scalar.activation(rg[:, u, :], ps[:, 1 + 3 * u + 2, :], ACT.Sigmoid).then_inc(s_sig.sem, 1)

            act.wait_ge(prep_pool, N_POOL)
            in_turn(act, NCH, [(0, scale_turned("C", hp, "ln_w", "ln_b", [(s_mix, s_mix.freed)])), (1, act_c)])

            def split(c, u, turn):
                s_st.wait_freed(act, u, turn)
                for n in range(2):
                    act.wait_ge(s_full.sem, s_full.done(c, n + 1))
                    nc.scalar.copy(kq[:, u, n, 0, :], full[:, n, :]).then_inc(s_hi.sem, 1)
                    act.wait_ge(s_lo.sem, s_lo.done(c, 2 * n + 1))
                    nc.scalar.copy(kq[:, u, n, 1, :], rem[:, n, :]).then_inc(s_hi.sem, 1)

            def copy_values(c, u, turn):
                act.wait_ge(s_mmD.sem, s_mmD.done(c, 5))
                nc.scalar.copy(V[:, ds(c * TPC, TPC), :], ps[:, 5, :].rearrange("p (t c) -> p t c", t=TPC))\
                    .then_inc(s_v.sem, 1)

            in_turn(act, NCH, [(0, scale_turned("D", hp, "ln1_w", "ln1_b", [(s_conv, s_conv.freed)])),
                               (1, copy_values), (1, split)])

            def attend(s, at, live):
                if not live(1):
                    return
                b, u, turn = at(1)
                for g in range(NG):
                    act.wait_ge(s_ST.sem, s_ST.done(b, g + 1))
                    act.wait_ge(s_pv.sem, s_pv.done(b, g - 1))
                    nc.scalar.activation(Pt[:, g % 2, :].rearrange("p (k n) -> p k n", k=2),
                                         ps[:, 2 + 2 * (g % 2):4 + 2 * (g % 2), :], ACT.Exp,
                                         scale=SCALE).then_inc(s_exp.sem, 1)
                    if g in (3, 5):
                        half = 0 if g == 3 else 1
                        act.wait_ge(s_pv.sem, s_pv.done(b, 3 * half + 3))
                        act.wait_ge(s_yT.sem, s_yT.done(b, half - 1))
                        nc.scalar.copy(yr[:, half, :], ps[:, 6, :]).then_inc(s_yr.sem, 1)

            run_steps(act, B, attend, 1)
            out_f = lambda c: s_out.freed(NEW0["F"] + c)

            def take_outputs(c, u, turn):
                act.wait_ge(s_tr.sem, s_tr.freed(TR0["F"] + c))
                nc.scalar.copy(xs[:, u], Y[:, ds(c * TPC, TPC), :]).then_inc(s_yc.sem, 1)

            act.wait_ge(s_yn.sem, s_yn.done(B - 1))
            in_turn(act, NCH, [(0, take_outputs), (1, copy_turned("F", [(s_out, out_f)]))])

            def act_g(c, u, turn):
                for n in range(E * FB):
                    act.wait_ge(s_up.sem, s_up.done(c, 2 * n + 1))
                    act.wait_ge(s_glu.sem, s_glu.done(c, n - 1))
                    nc.scalar.activation(sg[:, n % 2, :], ps[:, 2 + n % 2, :], ACT.Silu).then_inc(s_silu.sem, 1)

            in_turn(act, NCH, [(0, scale_turned("G", xT, "ln2_w", "ln2_b", [(s_up, s_up.freed)])), (1, act_g)])

        @block.vector
        def _(dve):
            for s in (s_xs, s_new, s_res, s_uu, s_y, s_mix, s_kvC, s_conv, s_rot, s_lo, s_max,
                      s_mp, s_rden, s_yn, s_oh, s_glu, s_acc):
                s.start(dve)

            def tiles(c, j):
                return ds(c * TPC + j, 1)

            def take_stats(src, c):
                for j in range(TPC):
                    dve.bn_stats(bn[:, tiles(c, j), :].rearrange("p o s -> p (o s)"),
                                 src[:, tiles(c, j), :].rearrange("p o c -> p (o c)"))

            def factors(stage):
                at, ap = SV0[stage], SP0[stage]
                dve.drain()
                dve.tensor_tensor(mean[:], bn[:, :, 1], bn[:, :, 4], ALU.add)
                dve.tensor_tensor(half[:], bn[:, :, 1], bn[:, :, 4], ALU.subtract)
                dve.tensor_tensor(var[:], bn[:, :, 2], bn[:, :, 5], ALU.add).then_inc(stat_v, 1)
                dve.wait_ge(stat_v, at + 1)
                dve.tensor_scalar(mean[:], mean[:], 0.5, None, ALU.mult)
                dve.scalar_tensor_tensor(out=half[:], in0=half[:], scalar=0.25, in1=half[:], op0=ALU.mult,
                                         op1=ALU.mult).then_inc(stat_v, 1)
                dve.wait_ge(stat_v, at + 2)
                dve.scalar_tensor_tensor(out=var[:], in0=var[:], scalar=1.0 / C, in1=half[:], op0=ALU.mult,
                                         op1=ALU.add).then_inc(stat_v, 1)
                dve.wait_ge(stat_v, at + 3)
                at += 3
                dve.tensor_scalar(tv[:], var[:], LN_EPS, None, ALU.add).then_inc(stat_v, 1)
                dve.wait_ge(stat_p, ap + 1)
                if stage in TWICE:
                    dve.tensor_tensor(rs[:], var[:], r1[:], ALU.mult).then_inc(stat_v, 1)
                    dve.wait_ge(stat_v, at + 2)
                    dve.tensor_tensor(rs[:], rs[:], r1[:], ALU.mult).then_inc(stat_v, 1)
                    dve.wait_ge(stat_v, at + 3)
                    dve.tensor_scalar(tv[:], rs[:], RMS_EPS if stage == "A" else LN_EPS, None, ALU.add)\
                        .then_inc(stat_v, 1)
                    dve.wait_ge(stat_p, ap + 2)
                    dve.tensor_tensor(rs[:], r1[:], r2[:], ALU.mult).then_inc(stat_v, 1)
                dve.tensor_scalar(rp1[:], r1[:], 1.0, None, ALU.add).then_inc(stat_v, 1)
                dve.tensor_tensor(mr[:], mean[:], r1[:], ALU.mult).then_inc(stat_v, 1)
                dve.wait_ge(stat_v, at + (7 if stage in TWICE else 3))

            def scale_inputs(stage):
                f = rs if stage in TWICE else r1

                def part(c, u, turn):
                    dve.wait_ge(s_tr.sem, s_tr.freed(TR0[stage] + c))
                    for j in range(TPC):
                        x = source[stage][:, tiles(c, j), :].rearrange("p o c -> p (o c)")
                        ins = dve.tensor_scalar(xs[:, u, j, :], x, mean[:, tiles(c, j)],
                                                f[:, tiles(c, j)], ALU.subtract, ALU.mult)
                    ins.then_inc(s_xs.sem, 1)
                    if stage in "BG":
                        return
                    for j in range(TPC):
                        x = source[stage][:, tiles(c, j), :].rearrange("p o c -> p (o c)")
                        to = XRES[:, tiles(c, j), :].rearrange("p o c -> p (o c)")
                        if stage == "D":
                            ins = dve.tensor_scalar(to, x, mean[:, tiles(c, j)], r1[:, tiles(c, j)],
                                                    ALU.subtract, ALU.mult)
                        else:
                            ins = dve.tensor_scalar(to, x, rp1[:, tiles(c, j)], mr[:, tiles(c, j)],
                                                    ALU.mult, ALU.subtract)
                    ins.then_inc(s_res.sem, 1)
                return part

            def add_product(stage):
                k0 = NEW0[stage]
                to = XA if stage == "F" else X

                def part(c, u, turn):
                    dve.wait_ge(s_out.sem, s_out.done(k0 + c))
                    kept = X if stage == "B" else XRES
                    if stage != "B":
                        dve.wait_ge(s_res.sem, s_res.done(RES0[stage] + c))
                    dve.tensor_tensor(to[:, ds(c * TPC, TPC), :], ps[:, 7, :].rearrange("p (t c) -> p t c", t=TPC),
                                      kept[:, ds(c * TPC, TPC), :], ALU.add).then_inc(s_new.sem, 1)
                    dve.drain()
                    take_stats(to, c)
                return part

            for c in range(NCH):
                dve.wait_ge(ld_x[c], 16)
                take_stats(X, c)

            dve.wait_ge(ld_w, 16 * N_W)
            dve.wait_ge(prep_act, 3)
            dve.wait_ge(prep_pool, N_POOL)
            dve.tensor_scalar(W_in[:], W_in[:], par("w_norm"), None, ALU.mult).then_inc(prep, 1)
            dve.tensor_scalar(lam[:, 1:2], lam[:, 0:1], -0.125, -0.125, ALU.mult, ALU.add).then_inc(prep, 1)
            dve.tensor_scalar(dec[:, 1:2], dec[:, 0:1], 0.5, 0.5, ALU.mult, ALU.add).then_inc(prep, 1)
            dve.wait_ge(prep, 3)
            dve.tensor_scalar(W_out[:], W_out[:], lam[:, 1:2], None, ALU.mult).then_inc(prep, 1)
            dve.tensor_scalar(decay_row[:], ones[:], dec[:, 1:2], None, ALU.mult).then_inc(prep, 1)
            dve.tensor_tensor(W_ffn[:], W_ffn[:], DISHA[:], ALU.add).then_inc(prep, 1)
            dve.tensor_copy(ident_b[:], ident[:]).then_inc(prep, 1)
            for k in range(4):
                dve.tensor_copy(masks_b[:, :, k, :], masks[:]).then_inc(prep, 1)

            def recur(c, u, turn):
                dve.wait_ge(s_actA.sem, s_actA.done(c, 3))
                dve.wait_ge(s_y.sem, s_y.freed(c))
                dve.scalar_tensor_tensor(out=rv[:, u, :], in0=ta[:, u, :], scalar=-1.0, in1=gv[:, u, :],
                                         op0=ALU.add, op1=ALU.mult).then_inc(s_uu.sem, 1)
                dve.wait_ge(s_uu.sem, s_uu.done(c, 1))
                dve.scalar_tensor_tensor(out=uu[:, u, :], in0=tr[:, u, :], scalar=1.0, in1=rv[:, u, :],
                                         op0=ALU.add, op1=ALU.mult).then_inc(s_uu.sem, 1)
                dve.wait_ge(s_uu.sem, s_uu.done(c))
                dve.wait_ge(s_actA.sem, s_actA.done(c, 4))
                dve.wait_ge(s_out.sem, s_out.freed(NEW0["A"] + c))
                for s in range(SPC):
                    t = slice(s * T, (s + 1) * T)
                    ins = dve.tensor_tensor_scan(y[:, u, t], ga[:, u, t], uu[:, u, t], 0.0, ALU.mult, ALU.add)
                ins.then_inc(s_y.sem, 1)

            factors("A")
            in_turn(dve, NCH, [(0, scale_inputs("A")), (1, recur), (2, add_product("A"))])

            factors("B")
            in_turn(dve, NCH, [(0, scale_inputs("B")), (1, add_product("B"))])

            def mixes(c, u, turn):
                dve.wait_ge(s_dif.sem, s_dif.done(c))
                dve.wait_ge(s_mmC.sem, s_mmC.freed(c))
                for n, name in enumerate(("mix_k", "mix_v", "mix_r")):
                    dve.scalar_tensor_tensor(
                        out=mix[:, u, n, :].rearrange("p (s t) -> p s t", s=SPC),
                        in0=dif[:, u, :].rearrange("p (s t) -> p s t", s=SPC), scalar=par(name),
                        in1=hp[:, u, :, 1:T + 1], op0=ALU.mult, op1=ALU.add).then_inc(s_mix.sem, 1)

            def states(c, u, turn):
                K, Vb = ps[:, 1 + 3 * u, :], ps[:, 2 + 3 * u, :]
                dve.wait_ge(s_mmC.sem, s_mmC.done(c, 2))
                for s in range(SPC):
                    t = slice(s * T, (s + 1) * T)
                    ins = dve.tensor_tensor_scan(sk[:, u, t], decay_row[:], K[:, t], 0.0, ALU.mult, ALU.add)
                ins.then_inc(s_kvC.sem, 1)
                dve.wait_ge(s_kvC.sem, s_kvC.done(c, 1))
                dve.scalar_tensor_tensor(out=sk[:, u, :], in0=sk[:, u, :], scalar=first[:], in1=K,
                                         op0=ALU.mult, op1=ALU.add).then_inc(s_kvC.sem, 1)
                dve.wait_ge(s_kvC.sem, s_kvC.done(c, 2))
                dve.tensor_tensor(sk[:, u, :], sk[:, u, :], Vb, ALU.mult).then_inc(s_kvC.sem, 1)
                dve.wait_ge(s_kvC.sem, s_kvC.done(c, 3))
                dve.wait_ge(s_sig.sem, s_sig.done(c))
                dve.wait_ge(s_out.sem, s_out.freed(NEW0["C"] + c))
                dve.tensor_tensor(y[:, u, :], sk[:, u, :], rg[:, u, :], ALU.mult).then_inc(s_kvC.sem, 1)

            factors("C")
            in_turn(dve, NCH, [(0, scale_inputs("C")), (0, mixes), (1, states), (2, add_product("C"))])

            def convolve(c, u, turn):
                dve.wait_ge(s_xT.sem, s_xT.done(TR0["D"] + c))
                dve.wait_ge(s_mmD.sem, s_mmD.freed(c))
                o = hc[:, u, :].rearrange("p (s t) -> p s t", s=SPC)
                dve.tensor_scalar(o, hp[:, u, :, 2:T + 2], par("conv2"), None, ALU.mult).then_inc(s_conv.sem, 1)
                for k, name in ((1, "conv1"), (0, "conv0")):
                    dve.wait_ge(s_conv.sem, s_conv.done(c, 2 - k))
                    dve.scalar_tensor_tensor(out=o, in0=hp[:, u, :, k:k + T], scalar=par(name), in1=o,
                                             op0=ALU.mult, op1=ALU.add).then_inc(s_conv.sem, 1)

            def rotations(c, u, turn):
                for n in range(2):
                    for k in range(2):
                        dve.wait_ge(s_mmD.sem, s_mmD.done(c, 2 * n + k + 1))
                        dve.wait_ge(s_full.sem, s_full.done(c, n - 1))
                        dve.tensor_tensor(
                            rot[:, n, k, :].rearrange("p (s t) -> p s t", s=SPC),
                            ps[:, 1 + 2 * n + k, :].rearrange("p (s t) -> p s t", s=SPC),
                            rope[:, k:k + 1, :].to_broadcast([P, SPC, T]), ALU.mult).then_inc(s_rot.sem, 1)

            def low_parts(c, u, turn):
                s_st.wait_freed(dve, u, turn)
                for n in range(2):
                    dve.wait_ge(s_hi.sem, s_hi.done(c, 2 * n + 1))
                    dve.tensor_tensor(rem[:, n, :], full[:, n, :], kq[:, u, n, 0, :], ALU.subtract)\
                        .then_inc(s_lo.sem, 1)
                    dve.wait_ge(s_hi.sem, s_hi.done(c, 2 * n + 2))
                    dve.tensor_tensor(kq[:, u, n, 2, :], rem[:, n, :], kq[:, u, n, 1, :], ALU.subtract)\
                        .then_inc(s_lo.sem, 1)

            factors("D")
            in_turn(dve, NCH, [(0, scale_inputs("D")), (0, convolve), (1, rotations), (1, low_parts)])

            def maximum(b, u, n):
                dve.wait_ge(s_S.sem, s_S.done(b, n + 1))
                if n == 0:
                    dve.wait_ge(s_mT.sem, s_mT.freed(b))
                if n < 4:
                    to, src = M[:, u, 0, 4 * n:4 * n + 4], ps[:, n % 2, :].rearrange("p (h k) -> p h k", h=4)
                else:
                    h = 2 * (n - 4)
                    to, src = M[:, u, 1, h:h + 2], ps[:, n % 2, :].rearrange("p (h k) -> p h k", h=2)
                dve.tensor_reduce(to, src, AX_X, ALU.max).then_inc(s_max.sem, 1)

            def normalise(b, half):
                u = half
                dve.wait_ge(s_yT.sem, s_yT.done(b, half + 1))
                o = ps[:, 7, :].rearrange("p (g q j c) -> p g q j c", g=2, q=2, j=4)
                dve.reciprocal(rden[:, u], o[:, :, :, :, D]).then_inc(s_rden.sem, 1)
                dve.wait_ge(s_rden.sem, s_rden.done(b, half + 1))
                for q in range(2):
                    to = Y[:, ds(b * 2 + q, 1), half * 64:half * 64 + 64]
                    ins = dve.tensor_tensor(
                        to.rearrange("p o (g j d) -> p (o g) j d", g=2, j=4), o[:, :, q, :, 0:D],
                        rden[:, u, :, q, :].rearrange("p g (j d) -> p g j d", d=1).to_broadcast([P, 2, 4, D]),
                        ALU.mult)
                ins.then_inc(s_yn.sem, 1)

            def minus_max(b, u, turn):
                dve.wait_ge(s_mT.sem, s_mT.done(b))
                s_mrow.wait_freed(dve, u, turn)
                dve.tensor_scalar(mp[:, u, 0, :], ps[0:H, 7, 0:T], -1.0, None, ALU.mult).then_inc(s_mp.sem, 1)
                dve.wait_ge(s_mp.sem, s_mp.done(b, 1))
                dve.scalar_tensor_tensor(out=mp[:, u, 1, :], in0=ps[0:H, 7, 0:T], scalar=-1.0,
                                         in1=mp[:, u, 0, :], op0=ALU.mult, op1=ALU.subtract)\
                    .then_inc(s_mp.sem, 1)

            def attend(s, at, live):
                for n in range(NS):
                    if live(0):
                        b, u, _ = at(0)
                        maximum(b, u % 2, n)
                    if n == 2 and live(2):
                        normalise(at(2)[0], 1)
                if live(1):
                    normalise(at(1)[0], 0)
                if live(0):
                    minus_max(*at(0))

            run_steps(dve, B, attend, 2, LANES)

            in_turn(dve, NCH, [(0, add_product("F"))])

            def choose(c, u, turn):
                dve.wait_ge(s_rt.sem, s_rt.done(c))
                dve.wait_ge(s_acc.sem, s_acc.done(c - 1))
                lg = ps[:, 1, 0:TPC * E].rearrange("p (t e) -> p t e", t=TPC)
                dve.tensor_reduce(lmax[:], lg, AX_X, ALU.max).then_inc(s_oh.sem, 1)
                dve.wait_ge(s_oh.sem, s_oh.done(c, 1))
                wide = lambda a: a[:].rearrange("p (t e) -> p t e", e=1).to_broadcast([P, TPC, E])
                dve.tensor_tensor(eq[:], lg, wide(lmax), ALU.is_equal).then_inc(s_oh.sem, 1)
                dve.wait_ge(s_oh.sem, s_oh.done(c, 2))
                dve.tensor_tensor(pk[:], eq[:], pick[:].rearrange("p (t e) -> p t e", t=1).to_broadcast([P, TPC, E]),
                                  ALU.mult).then_inc(s_oh.sem, 1)
                dve.wait_ge(s_oh.sem, s_oh.done(c, 3))
                dve.tensor_reduce(smax[:], pk[:], AX_X, ALU.max).then_inc(s_oh.sem, 1)
                dve.wait_ge(s_oh.sem, s_oh.done(c, 4))
                dve.tensor_tensor(oh[:], pk[:], wide(smax), ALU.is_equal).then_inc(s_oh.sem, 1)
                dve.wait_ge(s_oh.sem, s_oh.done(c, 5))

            def gate(c, n):
                dve.wait_ge(s_silu.sem, s_silu.done(c, n + 1))
                dve.wait_ge(s_up.sem, s_up.done(c, 2 * n + 2))
                dve.wait_ge(s_dn.sem, s_dn.done(c, n - 1))
                dve.tensor_tensor(glu[:, n % 2, :], sg[:, n % 2, :], ps[:, 4 + n % 2, :], ALU.mult)\
                    .then_inc(s_glu.sem, 1)

            def accumulate(c, e):
                dve.wait_ge(s_dn.sem, s_dn.done(c, FB * (e + 1)))
                dve.wait_ge(s_acc.sem, s_acc.done(c, e))
                for j in range(TPC):
                    to = XRES[:, tiles(c, j), :].rearrange("p o c -> p (o c)")
                    ins = dve.scalar_tensor_tensor(out=to, in0=ps[:, 6 + e % 2, j * C:(j + 1) * C],
                                                   scalar=oh[:, j, e:e + 1], in1=to, op0=ALU.mult, op1=ALU.add)
                ins.then_inc(s_acc.sem, 1)

            def experts(c, u, turn):
                choose(c, u, turn)
                for n in range(E * FB):
                    gate(c, n)
                    if n % FB == 1 and n > FB:
                        accumulate(c, n // FB - 1)
                accumulate(c, E - 1)

            factors("G")
            dve.wait_ge(s_sum.sem, s_sum.done(NCH - 1))
            in_turn(dve, NCH, [(0, scale_inputs("G")), (1, experts)])

        @block.tensor
        def _(pe):
            for s in (s_tr, s_out, s_mmA, s_mmC, s_mmD, s_S, s_mT, s_ST, s_pv, s_yT, s_rt, s_up, s_dn):
                s.start(pe)

            def turn(stage):
                def part(c, u, turn_):
                    pe.wait_ge(s_xT.sem, s_xT.done(TR0[stage] + c - 1))
                    if stage == "F":
                        pe.wait_ge(s_yc.sem, s_yc.done(c))
                    else:
                        pe.wait_ge(s_xs.sem, s_xs.done(XS0[stage] + c))
                    for j in range(TPC):
                        ins = pe.transpose(ps[:, 0, j * P:(j + 1) * P], xs[:, u, j, :], ident[:])
                    ins.then_inc(s_tr.sem, 1)
                return part

            def product(stage, a, w, ready):
                k0 = NEW0[stage]

                def part(c, u, turn_):
                    ready(c)
                    pe.wait_ge(s_new.sem, s_new.done(k0 + c - 1))
                    for j in range(TPC):
                        ins = pe.matmul(ps[:, 7, j * C:(j + 1) * C], a[:, u, j * P:(j + 1) * P], w[:],
                                        start=(j == 0), stop=True, skip_group_check=True)
                    ins.then_inc(s_out.sem, 1)
                return part

            pe.wait_ge(ld_w, 16 * N_W)
            pe.wait_ge(prep, 11)

            def project_a(c, u, turn_):
                pe.wait_ge(s_xT.sem, s_xT.done(TR0["A"] + c))
                pe.wait_ge(s_actA.sem, s_actA.freed(c))
                for n in range(3):
                    pe.matmul(ps[:, 1 + 3 * u + n, :], W_in[:, n * C:(n + 1) * C], xT[:, u, :],
                              start=True, stop=True).then_inc(s_mmA.sem, 1)

            in_turn(pe, NCH, [(0, turn("A")), (1, project_a),
                              (2, product("A", y, W_out, lambda c: pe.wait_ge(s_y.sem, s_y.done(c))))])

            in_turn(pe, NCH, [(0, turn("B")), (1, product(
                "B", xT, W_ffn, lambda c: pe.wait_ge(s_xT.sem, s_xT.done(TR0["B"] + c))))])

            def project_c(c, u, turn_):
                pe.wait_ge(s_kvC.sem, s_kvC.freed(c))
                pe.wait_ge(s_sig.sem, s_sig.freed(c))
                for n in range(3):
                    pe.wait_ge(s_mix.sem, s_mix.done(c, n + 1))
                    pe.matmul(ps[:, 1 + 3 * u + n, :], W_kvr[:, n * C:(n + 1) * C], mix[:, u, n, :],
                              start=True, stop=True).then_inc(s_mmC.sem, 1)

            in_turn(pe, NCH, [(0, turn("C")), (1, project_c),
                              (2, product("C", y, W_o, lambda c: pe.wait_ge(s_kvC.sem, s_kvC.done(c))))])

            def project_d(c, u, turn_):
                pe.wait_ge(s_conv.sem, s_conv.done(c))
                for n in range(4):
                    pe.wait_ge(s_rot.sem, s_rot.done(c - 1, n + 1))
                    pe.matmul(ps[:, 1 + n, :], W_qk[:, n * C:(n + 1) * C], hc[:, u, :],
                              start=True, stop=True).then_inc(s_mmD.sem, 1)
                pe.wait_ge(s_v.sem, s_v.done(c - 1))
                for j in range(TPC):
                    ins = pe.matmul(ps[:, 5, j * C:(j + 1) * C], hc[:, u, j * P:(j + 1) * P], W_v[:],
                                    start=(j == 0), stop=True, skip_group_check=True)
                ins.then_inc(s_mmD.sem, 1)

            in_turn(pe, NCH, [(0, turn("D")), (1, project_d)])

            def scores(b, lane, n):
                pe.wait_ge(s_max.sem, s_max.done(b, n - 1))
                bank = ps[:, n % 2, :]
                if n < 4:
                    pe.matmul(bank, ident_b[:], masks_b[:, 0].rearrange("p k c -> p (k c)"), start=True, stop=False,
                              skip_group_check=True)
                    for k in range(4):
                        ins = pe.matmul(bank[:, k * P:(k + 1) * P], QS[0:MAX_ROW, lane, 4 * n + k, 0:P],
                                        KS[0:MAX_ROW, lane, 4 * n + k, 0:P], start=False, stop=True,
                                        skip_group_check=True)
                else:
                    h = 2 * (n - 4)
                    pe.matmul(bank.rearrange("p (h k c) -> p h k c", h=2, k=2)[:, :, 1, :], ident_b[:],
                              masks_b[:, 0, 0:2, :], start=True, stop=False, skip_group_check=True)
                    for k in range(2):
                        ins = pe.matmul(bank[:, k * T:(k + 1) * T], QS[0:MAX_ROW, lane, h + k, P:T],
                                        KS[0:MAX_ROW, lane, h + k, :], start=False, stop=True,
                                        skip_group_check=True)
                ins.then_inc(s_S.sem, 1)

            def turned_scores(b, lane, g):
                kb, h0, nh = GROUPS[g]
                pe.wait_ge(s_exp.sem, s_exp.done(b, g - 1))
                for half in range(2):
                    bank = ps[:, 2 + 2 * (g % 2) + half, :]
                    if kb == 0:
                        pe.matmul(bank.rearrange("p (h k c) -> p h k c", h=2, k=2)[:, :, 0, :], ident_b[:],
                                  masks_b[:, 1, 0:2, :], start=True, stop=False, skip_group_check=True)
                    else:
                        pe.matmul(bank, ident_b[:], masks_b[:, 1].rearrange("p k c -> p (k c)"), start=True,
                                  stop=False, skip_group_check=True)
                    w = T - kb * P
                    for k in range(nh // 2):
                        h = h0 + half * nh // 2 + k
                        ins = pe.matmul(bank[:, k * w:(k + 1) * w], KS[:, lane, h, kb * P:(kb + 1) * P],
                                        QS[:, lane, h, kb * P:T], start=False, stop=True, skip_group_check=True)
                ins.then_inc(s_ST.sem, 1)

            def weigh(b, u, g):
                kb, h0, nh = GROUPS[g]
                pe.wait_ge(s_exp.sem, s_exp.done(b, g + 1))
                if g in (0, 3):
                    pe.wait_ge(s_yr.sem, s_yr.done(b, g // 3))
                w = T - kb * P
                for k in range(nh):
                    h = h0 + k
                    j, q = h % 4, h // 4 % 2
                    ins = pe.matmul(ps[32 * j:32 * j + 32, 6, q * T + kb * P:(q + 1) * T], Vx[:, u, kb, h, :],
                                    Pt[:, g % 2, k * w:(k + 1) * w], start=(g % 3 == 0), stop=(kb == 1),
                                    skip_group_check=True)
                ins.then_inc(s_pv.sem, 1)

            def turn_outputs(b, half):
                pe.wait_ge(s_yn.sem, s_yn.done(b, half))
                pe.wait_ge(s_yr.sem, s_yr.done(b, half + 1))
                for k in range(4):
                    ins = pe.transpose(ps[:, 7, k * P:(k + 1) * P], yr[:, half, k * P:(k + 1) * P], ident[:])
                ins.then_inc(s_yT.sem, 1)

            def attend(s, at, live):
                if live(0):
                    s_ldst.wait_done(pe, at(0)[1], at(0)[2])
                if live(1):
                    b1, lane1, turn1 = at(1)
                    pe.wait_ge(s_vx.sem, s_vx.done(b1))
                for g in range(NG):
                    if live(0) and g < 4:
                        for n in range(3 * g, 3 * g + 3):
                            scores(at(0)[0], at(0)[1], n)
                    if g == 0 and live(2):
                        b2 = at(2)[0]
                        pe.wait_ge(s_mp.sem, s_mp.done(b2 + 1 if live(1) else b2))
                        turn_outputs(b2, 1)
                    if live(1):
                        if g == 0:
                            s_mrow.wait_done(pe, lane1, turn1)
                        turned_scores(b1, lane1, g)
                        if g > 0:
                            weigh(b1, lane1 % 2, g - 1)
                        if g == 4:
                            pe.wait_ge(s_mp.sem, s_mp.done(b1))
                            turn_outputs(b1, 0)
                    if g == 4 and live(0):
                        b0, lane0, _ = at(0)
                        pe.wait_ge(s_max.sem, s_max.done(b0))
                        if live(1):
                            pe.wait_ge(s_yn.sem, s_yn.done(b1, 1))
                        for q in range(2):
                            ins = pe.transpose(ps[0:H, 7, q * P:(q + 1) * P], M[:, lane0 % 2, q, :], ident[:])
                        ins.then_inc(s_mT.sem, 1)
                if live(1):
                    weigh(b1, lane1 % 2, NG - 1)

            run_steps(pe, B, attend, 2, LANES)

            in_turn(pe, NCH, [(0, turn("F")), (1, product(
                "F", xT, W_proj, lambda c: pe.wait_ge(s_xT.sem, s_xT.done(TR0["F"] + c))))])

            def route(c, u):
                pe.wait_ge(s_xT.sem, s_xT.done(TR0["G"] + c))
                pe.wait_ge(s_oh.sem, s_oh.done(c - 1))
                for j in range(TPC):
                    ins = pe.matmul(ps[:, 1, j * E:(j + 1) * E], xT[:, u, j * P:(j + 1) * P], W_router[:],
                                    start=(j == 0), stop=True, skip_group_check=True)
                ins.then_inc(s_rt.sem, 1)

            def up(c, u, n):
                e, f = n // FB, n % FB
                pe.wait_ge(s_glu.sem, s_glu.done(c, n - 1))
                for k in range(2):
                    pe.matmul(ps[:, 2 + 2 * k + n % 2, :], W_up[:, e, k * FF + f * P:k * FF + (f + 1) * P],
                              xT[:, u, :], start=True, stop=True).then_inc(s_up.sem, 1)

            def down(c, u, n):
                e, f = n // FB, n % FB
                pe.wait_ge(s_glu.sem, s_glu.done(c, n + 1))
                if f == 0:
                    pe.wait_ge(s_acc.sem, s_acc.done(c, e - 1))
                for j in range(TPC):
                    ins = pe.matmul(ps[:, 6 + e % 2, j * C:(j + 1) * C], glu[:, n % 2, j * P:(j + 1) * P],
                                    W_down[:, e, f, :], start=(f == 0 and j == 0), stop=(f == FB - 1),
                                    skip_group_check=True)
                ins.then_inc(s_dn.sem, 1)

            def experts(c, u, turn_):
                route(c, u)
                up(c, u, 0)
                for n in range(1, E * FB):
                    up(c, u, n)
                    down(c, u, n - 1)
                down(c, u, E * FB - 1)

            pe.wait_ge(ld_e, 32)
            in_turn(pe, NCH, [(0, turn("G")), (1, experts)])


_OUTS = [((B, T, C), "float32")]


def kernel(**inputs):
    import numpy as np
    import concourse.bacc as bacc
    from concourse.bass_utils import run_bass_kernel_spmd as run

    g = {k: np.asarray(v) for k, v in inputs.items()}
    L1 = "L1_attn_"
    F = "L1_ffn_"
    turned = np.arange(C).reshape(H, 2, D // 2)[:, ::-1].reshape(-1)
    wq, wk, wv = (g[F + "attn_w"][:, k * C:(k + 1) * C] for k in range(3))
    columns = [g["L0_attn_w_norm"], g["L0_attn_lambda_log"], g[L1 + "time_mix_k"], g[L1 + "time_mix_v"],
               g[L1 + "time_mix_r"], g[L1 + "time_decay"], g[L1 + "time_first"], g[L1 + "ln_w"], g[L1 + "ln_b"],
               g[F + "ln1_w"], g[F + "ln1_b"], g[F + "ln2_w"], g[F + "ln2_b"],
               g[F + "conv_w"][:, 0, 0], g[F + "conv_w"][:, 0, 1], g[F + "conv_w"][:, 0, 2]]
    freq = (1.0 / np.float32(10000.0) ** (np.arange(0, D, 2, dtype=np.float32) / np.float32(D))).astype(np.float32)
    angle = np.arange(T, dtype=np.float32)[:, None] * freq[None, :]
    angle = np.concatenate([angle, angle], 1).T
    sign = np.where(np.arange(D) < D // 2, -1.0, 1.0)[:, None]
    rope = np.stack([np.tile(np.cos(angle), (H, 1)), np.tile(np.sin(angle) * sign, (H, 1))], 1).astype(np.float32)
    q, k = np.arange(P)[:, None], np.arange(P)[None, :]
    mask = np.stack([np.where(k > q, -1e30, 0.0), np.where(q > k, -1e30, 0.0)], 1).astype(np.float32)
    arrays = {
        "x": g["L0_attn_x"].reshape(TOK, C),
        "params": np.stack(columns, 1),
        "w_in": g["L0_attn_W_in"], "w_out": g["L0_attn_W_out"], "w_ffn": g["L0_ffn_weight"].T,
        "disha2": np.concatenate([g["L0_ffn_disha"], g["L0_ffn_disha"]], 0),
        "w_kvr": np.concatenate([g[L1 + "Wk"].T, g[L1 + "Wv"].T, g[L1 + "Wr"].T], 1), "w_o": g[L1 + "Wo"].T,
        "w_qk": np.concatenate([wq, wq[:, turned], wk, wk[:, turned]], 1), "w_v": wv, "w_proj": g[F + "proj_w"],
        "w_router": g[F + "router_w"], "w_up": g[F + "expert_wv"].transpose(1, 0, 2),
        "w_down": g[F + "expert_proj"].reshape(E, FB, P, C).transpose(2, 0, 1, 3),
        "ident": np.eye(P, dtype=np.float32), "rope": rope, "mask": mask,
        "pick": np.tile(np.arange(E, 0, -1, dtype=np.float32), (P, 1)),
    }
    nc = bacc.Bacc("TRN2", target_bir_lowering=False, num_devices=1)
    data, args = {}, []
    for name, a in arrays.items():
        a = np.ascontiguousarray(a)
        data[f"in_{name}"] = a
        args.append(nc.dram_tensor(f"in_{name}", a.shape, mybir.dt.from_np(a.dtype), kind="ExternalInput").ap())
    o = nc.dram_tensor("out_0", [TOK, C], F32, kind="ExternalOutput").ap()
    model_kernel(nc, *args, o)
    r = run(nc, [data], core_ids=[0])
    return r.results[0]["out_0"].reshape(B, T, C)
```

```python
from contextlib import ExitStack

import concourse.bass as bass
from concourse import mybir

F32 = mybir.dt.float32
BF16 = mybir.dt.bfloat16
I32 = mybir.dt.int32
U32 = mybir.dt.uint32
ALU = mybir.AluOpType
ACT = mybir.ActivationFunctionType
AX_X = mybir.AxisListType.X
ds = bass.ds

P = 128
B, T, C = 16, 256, 128
TOK = B * T
NT = TOK // P
CH = 512
NCH = TOK // CH
TPC = CH // P
SPC = CH // T
H, D = 16, 8
E, FF = 4, 512
FB = FF // P
GROUPS_G = 2
GT = NT // GROUPS_G
GB = GT + E - 1
NB = GROUPS_G * GB
LN_EPS, RMS_EPS = 1e-5, 1e-6
SCALE = float(D) ** -0.5
Q_PART = (0, 0, 0, 1, 1, 2)
K_PART = (0, 1, 2, 0, 1, 0)
MAX_ROW = 96
LANES = 4
PARAMS = ["w_norm", "lambda_log", "mix_k", "mix_v", "mix_r", "decay", "first", "ln_w", "ln_b",
          "ln1_w", "ln1_b", "ln2_w", "ln2_b", "conv0", "conv1", "conv2"]
GROUPS = ((0, 0, 4), (0, 4, 4), (1, 0, 8), (0, 8, 4), (0, 12, 4), (1, 8, 8))
NG = len(GROUPS)
NS = 12


class Signal:

    def __init__(self, sem, per=1):
        self.sem, self.per = sem, per

    def start(self, eng):
        eng.sem_inc(self.sem, 2 * self.per)

    def done(self, c, n=None):
        return (c + 2) * self.per + (self.per if n is None else n)

    def freed(self, c):
        return (c + 1) * self.per


class Fixed:

    def __init__(self, sem):
        self.sem = sem


class Lanes:

    def __init__(self, sems, per):
        self.sems, self.per = sems, per

    def start(self, eng):
        for s in self.sems:
            eng.sem_inc(s, self.per)

    def wait_done(self, eng, u, turn):
        eng.wait_ge(self.sems[u], (turn + 2) * self.per)

    def wait_freed(self, eng, u, turn):
        eng.wait_ge(self.sems[u], (turn + 1) * self.per)


def run_steps(eng, n, step, lag, period=2):
    lo = (lag + period - 1) // period * period
    hi = lo + (n - lo) // period * period

    def fixed(s):
        step(s, lambda l: (s - l, (s - l) % period, (s - l) // period), lambda l: 0 <= s - l < n)

    for s in range(lo):
        fixed(s)
    if hi > lo:
        with eng.Fori(0, (hi - lo) // period) as i:
            for w in range(lo, lo + period):
                step(i * period + w,
                     lambda l: (i * period + (w - l), (w - l) % period, i + (w - l) // period),
                     lambda l: True)
    for s in range(hi, n + lag):
        fixed(s)


START = {"A": 0, "B": NCH + 1, "C": 2 * NCH + 1, "D": 3 * NCH + 1, "F": 0, "G": NCH // GROUPS_G + 2}


def dense(parts):
    for s in range(START["D"] + NCH + 4):
        for stage, lag, part in parts:
            c = s - START[stage] - lag
            if 0 <= c < NCH:
                part(c, c % 2, c // 2)


def in_turn(eng, n, parts, period=2):
    def step(s, at, live):
        for lag, part in parts:
            if live(lag):
                part(*at(lag))
    run_steps(eng, n, step, max(lag for lag, _ in parts), period)


def model_kernel(nc, x_in, params_in, w_in, w_out, w_ffn, disha2, w_kvr, w_o, w_qk, w_v, w_proj,
                 w_router, w_up, w_down, ident_in, rope_in, mask_in, pick_in, before_in, block_in, out):
    x_tiles = x_in.rearrange("(n p) c -> p n c", p=P)
    out_tiles = out.rearrange("(n p) c -> p n c", p=P)
    qk_dram = nc.dram_tensor("qk_parts", [2, 3, P, TOK], BF16, kind="Internal").ap()

    sorted_in, sorted_out = ([nc.dram_tensor(f"{name}{g}", [GB * P, C], F32, kind="Internal").ap()
                              for g in range(GROUPS_G)] for name in ("sorted_in", "sorted_out"))

    with ExitStack() as ctx:
        def sb(name, shape, dt=F32):
            return ctx.enter_context(nc.sbuf_tensor(name, shape, dt))

        def sem(name):
            return ctx.enter_context(nc.semaphore(name))

        def signal(name, per=1):
            return Signal(sem(name), per)

        X = sb("X", [P, NT, C])
        XRES = sb("XRES", [P, NT, C])
        Y = sb("Y", [P, NT, C])
        V = sb("V", [P, NT, C])
        XA = V
        bn = sb("bn", [P, NT, 6])
        mean, var, half = (sb(k, [P, NT]) for k in ("mean", "var", "half"))
        tv, rsq, nt = (sb(k, [P, 2, NT]) for k in ("tv", "rsq", "nt"))
        r1, rs = rsq[:, 0, :], rsq[:, 1, :]
        rp1, mr = (sb(k, [P, NT]) for k in ("rp1", "mr"))
        params = sb("params", [P, len(PARAMS)])
        W_in = sb("W_in", [P, 3 * C])
        W_out = sb("W_out", [P, C])
        W_ffn = sb("W_ffn", [P, C])
        DISHA = sb("DISHA", [P, C])
        W_kvr = sb("W_kvr", [P, 3 * C])
        W_o = sb("W_o", [P, C])
        W_qk = sb("W_qk", [P, 4 * C])
        W_v = sb("W_v", [P, C])
        W_proj = sb("W_proj", [P, C])
        W_router = sb("W_router", [P, E])
        ident = sb("ident", [P, P])
        ident_b = sb("ident_b", [P, P], BF16)
        rope = sb("rope", [P, 2, T])
        masks = sb("masks", [P, 2, P])
        masks_b = sb("masks_b", [P, 2, 4, P], BF16)
        pick = sb("pick", [P, E])
        lam = sb("lam", [P, 2])
        dec = sb("dec", [P, 2])
        first = sb("first", [P, 1])
        decay_row = sb("decay_row", [P, T])
        ones = sb("ones", [P, T])
        xs = sb("xs", [P, 2, TPC, C])
        xT = sb("xT", [P, 2, CH])
        ta, tr, gv, ga, rv, uu, y = (sb(k, [P, 2, CH]) for k in ("ta", "tr", "gv", "ga", "rv", "uu", "y"))
        hp = sb("hp", [P, 2, SPC, T + 2])
        dif, sk, rg = ta, tr, gv
        mix = sb("mix", [P, 2, 3, CH])
        hc = ga
        rot = mix
        full, rem = rv, uu
        kq = Y[:].rearrange("p n c -> p (n c)").bitcast(BF16)[:, 0:2 * 2 * 3 * CH].rearrange(
            "p (u n a t) -> p u n a t", u=2, n=2, a=3)
        stack_q = sb("stack_q", [P, LANES * H * T // 2])
        QS = stack_q[:].bitcast(BF16).rearrange("p (l h t) -> p l h t", l=LANES, h=H)
        W_up = stack_q[:, 0:E * 2 * FF]
        W_down = stack_q[:, E * 2 * FF:E * 3 * FF]
        stack_k = sb("stack_k", [P, LANES * H * T // 2])
        KS = stack_k[:].bitcast(BF16).rearrange("p (l h t) -> p l h t", l=LANES, h=H)
        Vx = sb("Vx", [P, 2, 2, H, 32])
        Pt = mix[:].rearrange("p u n t -> p (u n t)")[:, 0:2048].rearrange("p (u n) -> p u n", u=2)
        M = sb("M", [P, 2, 2, H])
        mp = hp[:].rearrange("p u s t -> p (u s t)").bitcast(BF16)[0:H, 0:LANES * 2 * T].rearrange(
            "h (l r t) -> h l r t", l=LANES, r=2)
        yr = xs[:].rearrange("p u t c -> p u (t c)")
        rden = sb("rden", [P, 2, 2, 2, 4])
        HN = Y
        used = [0]

        def late(*shape):
            n = 1
            for k in shape:
                n *= k
            a = stack_k[:, used[0]:used[0] + n]
            used[0] += n
            if len(shape) == 1:
                return a
            names = "abc"[:len(shape)]
            return a.rearrange(f"p ({' '.join(names)}) -> p {' '.join(names)}",
                               **{k: v for k, v in zip(names, shape)})

        hs = late(LANES, C)
        hT, yo = late(2, C), late(2, C)
        xTg, sg, glu, gT = ta, tr, gv, ga
        before = sb("before", [P, P])
        before_b, ones_b = (sb(k, [P, P], BF16) for k in ("before_b", "ones_b"))
        block_at = sb("block_at", [P, GB])
        logits, pk, oh, at4 = (late(NT, E) for _ in range(4))
        oh_b = late(NT * E // 2).bitcast(BF16).rearrange("p (t e) -> p t e", e=E)
        lmax, smax, posf = (late(NT) for _ in range(3))
        pos = late(NT).bitcast(U32)
        cum = late(E, GT)
        padded_i = late(E).bitcast(I32)
        padded, ends, starts = (late(E) for _ in range(3))
        expf = late(NB)
        exp_i = late(NB).bitcast(I32)
        ps = ctx.enter_context(nc.psum_tensor("ps", [P, 8, 512], F32))

        def par(name):
            k = PARAMS.index(name)
            return params[:, k:k + 1]

        ld_x = [sem(f"ld_x{c}") for c in range(NCH)]
        ld_w = sem("ld_w")
        N_W, N_W2 = 6, 11
        ld_w2 = sem("ld_w2")
        ld_e = sem("ld_e")
        prep = sem("prep")
        prep_act = sem("prep_act")
        prep_pool = sem("prep_pool")
        N_POOL = 7
        stat_v = sem("stat_v")
        s_xs = signal("s_xs")
        s_new = signal("s_new")
        s_res = signal("s_res")
        s_tr = signal("s_tr")
        s_xT = signal("s_xT")
        s_out = signal("s_out")
        s_mmA = signal("s_mmA", 3)
        s_actA = signal("s_actA", 5)
        s_rv = signal("s_rv")
        s_uu = signal("s_uu")
        s_y = signal("s_y")
        s_dif = signal("s_dif")
        s_mix = signal("s_mix", 3)
        s_mmC = signal("s_mmC", 3)
        s_sig = signal("s_sig")
        s_kvC = signal("s_kvC", 4)
        s_conv = signal("s_conv", 3)
        s_mmD = signal("s_mmD", 5)
        s_rot = signal("s_rot", 4)
        s_full = signal("s_full", 2)
        s_hi = signal("s_hi", 4)
        s_lo = signal("s_lo", 4)
        s_v = signal("s_v")
        s_st = Lanes([sem(f"s_st{u}") for u in range(2)], 32)
        s_ldst = Lanes([sem(f"s_ldst{u}") for u in range(LANES)], 16 * 12)
        s_mrow = Lanes([sem(f"s_mrow{u}") for u in range(LANES)], 32)
        s_use = signal("s_use")
        s_S = signal("s_S", NS)
        s_max = signal("s_max", NS)
        s_mT = signal("s_mT")
        s_mp = signal("s_mp", 2)
        s_ST = signal("s_ST", NG)
        s_exp = signal("s_exp", NG)
        s_pv = signal("s_pv", NG)
        s_yr = signal("s_yr", 2)
        s_yT = signal("s_yT", 2)
        s_rden = signal("s_rden", 2)
        s_yn = signal("s_yn", 2)
        s_vx = signal("s_vx")
        s_sum = signal("s_sum")
        zeroed = sem("zeroed")
        s_turnG, s_xTG, s_rt, s_lg = (signal(k) for k in ("s_turnG", "s_xTG", "s_rt", "s_lg"))
        s_cnt = sem("s_cnt")
        route_v = sem("route_v")
        scattered = [sem(f"scattered{g}") for g in range(GROUPS_G)]
        gathered = [sem(f"gathered{c}") for c in range(NCH)]
        s_hs = Lanes([sem(f"s_hs{u}") for u in range(LANES)], 16)
        s_yo = Lanes([sem(f"s_yo{u}") for u in range(2)], 16)
        s_bT, s_hT, s_up, s_silu, s_glu, s_gT, s_gTc, s_dn, s_yc = (
            signal(k) for k in ("s_bT", "s_hT", "s_up", "s_silu", "s_glu", "s_gT", "s_gTc", "s_dn", "s_yc"))
        s_fin = sem("s_fin")
        stored = sem("stored")

        XS0 = {k: NCH * n for n, k in enumerate("ABCDG")}
        TR0 = {k: NCH * n for n, k in enumerate("ABCDF")}
        RES0 = {k: NCH * n for n, k in enumerate("ACF")}
        NEW0 = {k: NCH * n for n, k in enumerate("ABCF")}
        TWICE = "ACD"
        source = {"A": X, "B": X, "C": X, "D": X, "G": XA}

        def out_bank(stage, u):
            return 7 - u if stage in "BF" else 7

        ONE_HOT = [6 + g * (17 + E) for g in range(GROUPS_G)]
        ROUTED = [17 + g * (17 + E) for g in range(GROUPS_G)]

        block = ctx.enter_context(nc.Block())

        @block.sync
        def _(sp):
            for s in (s_st, s_ldst, s_mrow, s_hs, s_yo):
                s.start(sp)
            for c in range(NCH):
                sp.dma_start(X[:, c * TPC:(c + 1) * TPC, :], x_tiles[:, c * TPC:(c + 1) * TPC, :])\
                  .then_inc(ld_x[c], 16)

            def store_parts(c, u, turn):
                for n in range(2):
                    sp.wait_ge(s_lo.sem, s_lo.done(c, n + 3))
                    sp.dma_start(qk_dram[n, :, :, ds(c * CH, CH)].rearrange("a p t -> p a t"),
                                 kq[:, u, n, :, :]).then_inc(s_st.sems[u], 16)

            sp.wait_ge(prep_pool, 4)
            for g in range(GROUPS_G):
                sp.dma_start(sorted_in[g].rearrange("(p n) c -> p (n c)", p=P), stack_q[:, 0:GB * C])\
                  .then_inc(zeroed, 16)
            dense([("D", 2, store_parts)])

            def load_stack(b, u, turn):
                sp.wait_ge(s_ST.sem, s_ST.per * (b - LANES + 3) if not isinstance(b, int) else
                           max(s_ST.per * (b - LANES + 3), 1))
                for n, (dst, split) in enumerate(((QS, Q_PART), (KS, K_PART))):
                    for k, part in enumerate(split):
                        sp.dma_start(
                            dst[D * k:D * (k + 1), u, :, :],
                            qk_dram[n, part, :, ds(b * T, T)].rearrange("(h d) t -> d h t", d=D),
                        ).then_inc(s_ldst.sems[u], 16)

            def max_rows(b, u, turn):
                sp.wait_ge(s_mp.sem, s_mp.done(b))
                for r in range(2):
                    sp.dma_start(QS[MAX_ROW + r:MAX_ROW + r + 1, u, :, :], mp[:, u, r, :])\
                      .then_inc(s_mrow.sems[u], 16)

            for u in range(2):
                s_st.wait_done(sp, u, NCH // 2 - 1)
            sp.wait_ge(prep_pool, N_POOL)
            sp.wait_ge(zeroed, 16 * GROUPS_G)
            in_turn(sp, B, [(0, load_stack), (2, max_rows)], LANES)

            sp.wait_ge(s_ST.sem, s_ST.done(B - 1))
            sp.dma_start(W_up, w_up).then_inc(ld_e, 16)
            sp.dma_start(W_down, w_down).then_inc(ld_e, 16)

            def block_rows(tensors, k):
                return tensors[k // GB][k % GB * P:(k % GB + 1) * P, :]

            for s in range(NB + 4):
                if s < NB:
                    u = s % LANES
                    if s % GB == 0:
                        sp.wait_ge(scattered[s // GB], 16 * GT)
                    sp.wait_ge(s_bT.sem, s_bT.done(s - LANES) if s >= LANES else 2)
                    sp.dma_start(hs[:, u, :], block_rows(sorted_in, s)).then_inc(s_hs.sems[u], 16)
                if s >= 4:
                    k = s - 4
                    sp.wait_ge(s_yc.sem, s_yc.done(k))
                    sp.dma_start(block_rows(sorted_out, k), yo[:, k % 2, :]).then_inc(s_yo.sems[k % 2], 16)
            for c in range(NCH):
                sp.wait_ge(s_fin, c + 1)
                sp.dma_start(out_tiles[:, c * TPC:(c + 1) * TPC, :], XRES[:, c * TPC:(c + 1) * TPC, :])\
                  .then_inc(stored, 16)
            sp.wait_ge(stored, 16 * NCH)

        @block.gpsimd
        def _(pool):
            for s in (s_rv, s_dif, s_vx, s_full, s_sum, s_res):
                s.start(pool)
            fills = ((ones[:], 1.0), (hp[:], 0.0), (stack_q[:], 0.0), (stack_k[:], 0.0), (Vx[:], 0.0),
                     (KS[MAX_ROW:MAX_ROW + 2, :, :, :], 1.0), (Vx[:, :, :, :, D:D + 1], 1.0))
            for n, (to, value) in enumerate(fills):
                if n:
                    pool.wait_ge(prep_pool, n)
                pool.memset(to, value).then_inc(prep_pool, 1)
            def gates(c, u, turn):
                pool.wait_ge(s_actA.sem, s_actA.done(c, 5))
                pool.wait_ge(s_uu.sem, s_uu.freed(c))
                pool.tensor_tensor(rv[:, u, :], tr[:, u, :], gv[:, u, :], ALU.mult).then_inc(s_rv.sem, 1)

            def shift(c, u, turn):
                pool.wait_ge(s_xT.sem, s_xT.done(TR0["C"] + c))
                pool.wait_ge(s_mix.sem, s_mix.freed(c))
                pool.tensor_tensor(dif[:, u, :].rearrange("p (s t) -> p s t", s=SPC), hp[:, u, :, 2:T + 2],
                                   hp[:, u, :, 1:T + 1], ALU.subtract).then_inc(s_dif.sem, 1)

            def rotate(c, u, turn):
                for n in range(2):
                    pool.wait_ge(s_rot.sem, s_rot.done(c, 2 * n + 2))
                    pool.wait_ge(s_lo.sem, s_lo.done(c - 1, n + 1))
                    pool.tensor_tensor(full[:, n, :], rot[:, n, 0, :], rot[:, n, 1, :], ALU.add)\
                        .then_inc(s_full.sem, 1)

            def keep(stage):
                def part(c, u, turn):
                    pool.wait_ge(s_xs.sem, s_xs.done(XS0[stage] + c))
                    for n in range(c * TPC, (c + 1) * TPC):
                        if stage == "D":
                            ins = pool.tensor_scalar(XRES[:, n, :], X[:, n, :], mean[:, n:n + 1], r1[:, n:n + 1],
                                                     ALU.subtract, ALU.mult)
                        else:
                            ins = pool.tensor_scalar(XRES[:, n, :], X[:, n, :], rp1[:, n:n + 1], mr[:, n:n + 1],
                                                     ALU.mult, ALU.subtract)
                    ins.then_inc(s_res.sem, 1)
                return part

            dense([("A", 1, gates), ("A", 0, keep("A")), ("C", 0, keep("C")), ("C", 0, shift),
                   ("D", 2, rotate), ("D", 0, keep("D"))])

            def spread_values(b, u, turn):
                pool.wait_ge(s_pv.sem, s_pv.freed(b))
                for kb in range(2):
                    ins = pool.tensor_copy(
                        Vx[:, u % 2, kb, :, 0:D],
                        V[:, ds(b * 2 + kb, 1), :].rearrange("p o (h d) -> p (o h) d", h=H))
                ins.then_inc(s_vx.sem, 1)

            pool.wait_ge(s_v.sem, s_v.done(NCH - 1))
            in_turn(pool, B, [(0, spread_values)])

            def add_streams(c, u, turn):
                pool.wait_ge(s_new.sem, s_new.done(NEW0["F"] + c))
                pool.tensor_tensor(XRES[:, ds(c * TPC, TPC), :], X[:, ds(c * TPC, TPC), :],
                                   XA[:, ds(c * TPC, TPC), :], ALU.add).then_inc(s_sum.sem, 1)

            dense([("F", 2, add_streams)])

            for g in range(GROUPS_G):
                if g == 0:
                    pool.wait_ge(zeroed, 16 * GROUPS_G)
                pool.wait_ge(route_v, ROUTED[g])
                for t in range(g * GT, (g + 1) * GT):
                    pool.indirect_dma_start(
                        out=sorted_in[g], out_offset=bass.IndirectOffsetOnAxis(ap=pos[:, t:t + 1], axis=0),
                        in_=HN[:, t, :], in_offset=None).then_inc(scattered[g], 16)
            pool.wait_ge(s_sum.sem, s_sum.done(NCH - 1))
            for g in range(GROUPS_G):
                for u in range(2):
                    k = (g + 1) * GB
                    pool.wait_ge(s_yo.sems[u], 16 * (1 + (k + 1 - u) // 2))
                for t in range(g * GT, (g + 1) * GT):
                    pool.indirect_dma_start(
                        out=X[:, t, :], out_offset=None, in_=sorted_out[g],
                        in_offset=bass.IndirectOffsetOnAxis(ap=pos[:, t:t + 1], axis=0))\
                        .then_inc(gathered[t // TPC], 16)

        @block.scalar
        def _(act):
            for s in (s_xT, s_actA, s_sig, s_hi, s_v, s_exp, s_yr, s_xTG, s_lg, s_hT, s_silu, s_gTc):
                s.start(act)
            for n, (dst, src) in enumerate((
                    (params[:], params_in), (W_in[:], w_in), (ident[:], ident_in), (W_out[:], w_out),
                    (W_ffn[:], w_ffn), (DISHA[:], disha2), (W_kvr[:], w_kvr), (W_o[:], w_o),
                    (W_qk[:], w_qk), (W_v[:], w_v), (W_proj[:], w_proj), (W_router[:], w_router),
                    (rope[:], rope_in), (masks[:], mask_in), (pick[:], pick_in),
                    (before[:], before_in), (block_at[:], block_in))):
                act.dma_start(dst, src).then_inc(ld_w if n < N_W else ld_w2, 16)
            act.wait_ge(ld_w, 16 * N_W)
            nc.scalar.activation(first[:], par("first"), ACT.Exp).then_inc(prep_act, 1)
            nc.scalar.activation(lam[:, 0:1], par("lambda_log"), ACT.Tanh, scale=0.5).then_inc(prep_act, 1)
            nc.scalar.activation(dec[:, 0:1], par("decay"), ACT.Tanh, scale=0.5).then_inc(prep_act, 1)

            def copy_turned(stage, users):
                def part(c, u, turn):
                    act.wait_ge(s_tr.sem, s_tr.done(TR0[stage] + c))
                    for sig, value in users:
                        act.wait_ge(sig.sem, value(c))
                    nc.scalar.copy(xT[:, u, :], ps[:, 0, :]).then_inc(s_xT.sem, 1)
                return part

            def scale_turned(stage, dst, w, b, users):
                def part(c, u, turn):
                    act.wait_ge(s_tr.sem, s_tr.done(TR0[stage] + c))
                    for sig, value in users:
                        act.wait_ge(sig.sem, value(c))
                    src, to = ps[:, 0, :], dst[:, u]
                    if dst is hp:
                        src, to = src.rearrange("p (s t) -> p s t", s=SPC), hp[:, u, :, 2:T + 2]
                    nc.scalar.activation(to, src, ACT.Identity, bias=par(b), scale=par(w)).then_inc(s_xT.sem, 1)
                return part

            def act_a(c, u, turn):
                act.wait_ge(s_y.sem, s_y.freed(c))
                for n, (dst, fn, scale) in enumerate(((ta, ACT.Tanh, 0.5), (tr, ACT.Tanh, 0.5), (gv, ACT.Gelu, 1.0))):
                    act.wait_ge(s_mmA.sem, s_mmA.done(c, n + 1))
                    nc.scalar.activation(dst[:, u, :], ps[:, 1 + 3 * u + n, :], fn, scale=scale).then_inc(s_actA.sem, 1)
                for dst, src in ((ga, ta), (tr, tr)):
                    act.wait_ge(s_actA.sem, s_actA.done(c, 2))
                    nc.scalar.activation(dst[:, u, :], src[:, u, :], ACT.Copy, bias=0.5, scale=0.5)\
                        .then_inc(s_actA.sem, 1)

            out_b = lambda c: s_out.freed(NEW0["B"] + c)

            def act_c(c, u, turn):
                act.wait_ge(s_mmC.sem, s_mmC.done(c, 3))
                act.wait_ge(s_kvC.sem, s_kvC.freed(c))
                nc.scalar.activation(rg[:, u, :], ps[:, 1 + 3 * u + 2, :], ACT.Sigmoid).then_inc(s_sig.sem, 1)

            pads = [(Fixed(prep_pool), lambda c: 2)]

            def split(c, u, turn):
                s_st.wait_freed(act, u, turn)
                for n in range(2):
                    act.wait_ge(s_full.sem, s_full.done(c, n + 1))
                    nc.scalar.copy(kq[:, u, n, 0, :], full[:, n, :]).then_inc(s_hi.sem, 1)
                for n in range(2):
                    act.wait_ge(s_lo.sem, s_lo.done(c, n + 1))
                    nc.scalar.copy(kq[:, u, n, 1, :], rem[:, n, :]).then_inc(s_hi.sem, 1)

            def copy_values(c, u, turn):
                act.wait_ge(s_mmD.sem, s_mmD.done(c, 5))
                nc.scalar.copy(V[:, ds(c * TPC, TPC), :], ps[:, 5, :].rearrange("p (t c) -> p t c", t=TPC))\
                    .then_inc(s_v.sem, 1)

            dense([("A", 1, act_a), ("A", 0, copy_turned("A", [(s_mmA, s_mmA.freed)])),
                   ("B", 0, copy_turned("B", [(s_out, out_b)])),
                   ("C", 1, act_c),
                   ("C", 0, scale_turned("C", hp, "ln_w", "ln_b", pads + [(s_mix, s_mix.freed)])),
                   ("D", 2, split), ("D", 1, copy_values),
                   ("D", 0, scale_turned("D", hp, "ln1_w", "ln1_b",
                                         [(s_conv, s_conv.freed), (Fixed(s_mix.sem), lambda c: s_mix.done(NCH - 1))]))])

            def attend(s, at, live):
                if not live(1):
                    return
                b, u, turn = at(1)
                for g in range(NG):
                    act.wait_ge(s_ST.sem, s_ST.done(b, g + 1))
                    act.wait_ge(s_pv.sem, s_pv.done(b, g - 1))
                    nc.scalar.activation(Pt[:, g % 2, :].rearrange("p (k n) -> p k n", k=2),
                                         ps[:, 2 + 2 * (g % 2):4 + 2 * (g % 2), :], ACT.Exp,
                                         scale=SCALE).then_inc(s_exp.sem, 1)
                    if g in (3, 5):
                        half = 0 if g == 3 else 1
                        act.wait_ge(s_pv.sem, s_pv.done(b, 3 * half + 3))
                        act.wait_ge(s_yT.sem, s_yT.done(b, half - 1))
                        nc.scalar.copy(yr[:, half, :], ps[:, 6, :]).then_inc(s_yr.sem, 1)

            run_steps(act, B, attend, 1)
            out_f = lambda c: s_out.freed(NEW0["F"] + c)

            def scale_g(c, u, turn):
                act.wait_ge(s_turnG.sem, s_turnG.done(c))
                act.wait_ge(s_rt.sem, s_rt.freed(c))
                nc.scalar.activation(xTg[:, u, :], ps[:, 1, :], ACT.Identity, bias=par("ln2_b"),
                                     scale=par("ln2_w")).then_inc(s_xTG.sem, 1)

            def take_logits(c, u, turn):
                act.wait_ge(s_rt.sem, s_rt.done(c))
                nc.scalar.copy(logits[:, c * TPC:(c + 1) * TPC, :],
                               ps[:, 2 + u, 0:TPC * E].rearrange("p (t e) -> p t e", t=TPC)).then_inc(s_lg.sem, 1)

            dense([("F", 0, copy_turned("F", [(s_out, out_f)])), ("G", 0, scale_g), ("G", 1, take_logits)])

            def block_in_(k, u, turn):
                act.wait_ge(s_bT.sem, s_bT.done(k))
                act.wait_ge(s_up.sem, s_up.freed(k))
                nc.scalar.activation(hT[:, u, :], ps[:, 0, 0:P], ACT.Identity, bias=par("ln2_b"),
                                     scale=par("ln2_w")).then_inc(s_hT.sem, 1)

            def block_silu(k, u, turn):
                act.wait_ge(s_up.sem, s_up.done(k))
                act.wait_ge(s_glu.sem, s_glu.freed(k))
                nc.scalar.activation(sg[:, u, :], ps[:, 1 + u, :], ACT.Silu).then_inc(s_silu.sem, 1)

            def block_turned(k, u, turn):
                act.wait_ge(s_gT.sem, s_gT.done(k))
                act.wait_ge(s_dn.sem, s_dn.freed(k))
                nc.scalar.copy(gT[:, u, :], ps[:, 5, :]).then_inc(s_gTc.sem, 1)

            in_turn(act, NB, [(3, block_turned), (1, block_silu), (0, block_in_)])

        @block.vector
        def _(dve):
            for s in (s_xs, s_new, s_uu, s_y, s_mix, s_kvC, s_conv, s_rot, s_lo, s_max,
                      s_mp, s_rden, s_yn, s_glu, s_yc):
                s.start(dve)

            def tiles(c, j):
                return ds(c * TPC + j, 1)

            def take_stats(src, c):
                for j in range(TPC):
                    dve.bn_stats(bn[:, tiles(c, j), :].rearrange("p o s -> p (o s)"),
                                 src[:, tiles(c, j), :].rearrange("p o c -> p (o c)"))

            links = [0]

            def link(*made):
                links[0] += 1
                made[-1].then_inc(stat_v, 1)
                dve.wait_ge(stat_v, links[0])

            def factors(stage, part):
                t = slice(part * NT // 2, (part + 1) * NT // 2)
                n = 2 if stage in TWICE else 1
                eps2 = RMS_EPS if stage == "A" else LN_EPS
                v, r, w = tv[:, 0:n, t], rsq[:, 0:n, t], nt[:, 0:n, t]
                dve.drain()
                link(dve.tensor_tensor(mean[:, t], bn[:, t, 1], bn[:, t, 4], ALU.add),
                     dve.tensor_tensor(half[:, t], bn[:, t, 1], bn[:, t, 4], ALU.subtract),
                     dve.tensor_tensor(var[:, t], bn[:, t, 2], bn[:, t, 5], ALU.add))
                link(dve.tensor_scalar(mean[:, t], mean[:, t], 0.5, None, ALU.mult),
                     dve.scalar_tensor_tensor(out=half[:, t], in0=half[:, t], scalar=0.25, in1=half[:, t],
                                              op0=ALU.mult, op1=ALU.mult))
                link(dve.scalar_tensor_tensor(out=var[:, t], in0=var[:, t], scalar=1.0 / C, in1=half[:, t],
                                              op0=ALU.mult, op1=ALU.add))
                made = [dve.tensor_scalar(tv[:, 0, t], var[:, t], LN_EPS, None, ALU.add)]
                if n == 2:
                    made.append(dve.tensor_scalar(tv[:, 1, t], var[:, t], 1.0 + eps2, LN_EPS * eps2,
                                                  ALU.mult, ALU.add))
                link(*made)
                link(dve.tensor_scalar(r.bitcast(I32), v.bitcast(I32), -0.5, float(0x5F3759DF), ALU.mult, ALU.add))
                for _ in range(3):
                    link(dve.scalar_tensor_tensor(out=w, in0=r, scalar=-0.5, in1=v, op0=ALU.mult, op1=ALU.mult))
                    link(dve.tensor_tensor(w, w, r, ALU.mult))
                    link(dve.scalar_tensor_tensor(out=r, in0=w, scalar=1.5, in1=r, op0=ALU.add, op1=ALU.mult))
                if stage in "AC":
                    link(dve.tensor_scalar(rp1[:, t], r1[:, t], 1.0, None, ALU.add),
                         dve.tensor_tensor(mr[:, t], mean[:, t], r1[:, t], ALU.mult))

            def scale_inputs(stage):
                f = rs if stage in TWICE else r1

                def part(c, u, turn):
                    if stage != "G":
                        dve.wait_ge(s_tr.sem, s_tr.freed(TR0[stage] + c))
                    for j in range(TPC):
                        x = source[stage][:, tiles(c, j), :].rearrange("p o c -> p (o c)")
                        to = HN[:, c * TPC + j, :] if stage == "G" else xs[:, u, j, :]
                        ins = dve.tensor_scalar(to, x, mean[:, tiles(c, j)],
                                                f[:, tiles(c, j)], ALU.subtract, ALU.mult)
                    ins.then_inc(s_xs.sem, 1)
                return part

            def add_product(stage):
                k0 = NEW0[stage]
                to = XA if stage == "F" else X

                def part(c, u, turn):
                    dve.wait_ge(s_out.sem, s_out.done(k0 + c))
                    kept = X if stage == "B" else XRES
                    if stage != "B":
                        dve.wait_ge(s_res.sem, s_res.done(RES0[stage] + c))
                    dve.tensor_tensor(to[:, ds(c * TPC, TPC), :], ps[:, out_bank(stage, u), :].rearrange("p (t c) -> p t c", t=TPC),
                                      kept[:, ds(c * TPC, TPC), :], ALU.add).then_inc(s_new.sem, 1)
                    dve.drain()
                    take_stats(to, c)
                    if (c + 1) % (NCH // 2) == 0:
                        factors({"A": "B", "B": "C", "C": "D", "F": "G"}[stage], c // (NCH // 2))
                return part

            for c in range(NCH):
                dve.wait_ge(ld_x[c], 16)
                take_stats(X, c)
                if (c + 1) % (NCH // 2) == 0:
                    factors("A", c // (NCH // 2))

            dve.wait_ge(ld_w, 16 * N_W)
            dve.wait_ge(prep_act, 3)
            dve.wait_ge(prep_pool, 1)
            dve.tensor_scalar(W_in[:], W_in[:], par("w_norm"), None, ALU.mult).then_inc(prep, 1)
            dve.tensor_scalar(lam[:, 1:2], lam[:, 0:1], -0.5, -0.5, ALU.mult, ALU.add).then_inc(prep, 1)
            dve.tensor_scalar(dec[:, 1:2], dec[:, 0:1], 0.5, 0.5, ALU.mult, ALU.add).then_inc(prep, 1)
            dve.wait_ge(prep, 3)
            dve.tensor_scalar(W_out[:], W_out[:], lam[:, 1:2], None, ALU.mult).then_inc(prep, 1)
            dve.tensor_scalar(decay_row[:], ones[:], dec[:, 1:2], None, ALU.mult).then_inc(prep, 1)
            dve.tensor_tensor(W_ffn[:], W_ffn[:], DISHA[:], ALU.add).then_inc(prep, 1)
            dve.tensor_copy(ident_b[:], ident[:]).then_inc(prep, 1)

            def recur(c, u, turn):
                dve.wait_ge(s_rv.sem, s_rv.done(c))
                dve.wait_ge(s_y.sem, s_y.freed(c))
                dve.scalar_tensor_tensor(out=uu[:, u, :], in0=ga[:, u, :], scalar=-1.0, in1=rv[:, u, :],
                                         op0=ALU.add, op1=ALU.mult).then_inc(s_uu.sem, 1)
                dve.wait_ge(s_uu.sem, s_uu.done(c))
                dve.wait_ge(s_out.sem, s_out.freed(NEW0["A"] + c))
                for s in range(SPC):
                    t = slice(s * T, (s + 1) * T)
                    ins = dve.tensor_tensor_scan(y[:, u, t], ga[:, u, t], uu[:, u, t], 0.0, ALU.mult, ALU.add)
                ins.then_inc(s_y.sem, 1)


            def mixes(c, u, turn):
                dve.wait_ge(s_dif.sem, s_dif.done(c))
                dve.wait_ge(s_mmC.sem, s_mmC.freed(c))
                for n, name in enumerate(("mix_k", "mix_v", "mix_r")):
                    dve.scalar_tensor_tensor(
                        out=mix[:, u, n, :].rearrange("p (s t) -> p s t", s=SPC),
                        in0=dif[:, u, :].rearrange("p (s t) -> p s t", s=SPC), scalar=par(name),
                        in1=hp[:, u, :, 1:T + 1], op0=ALU.mult, op1=ALU.add).then_inc(s_mix.sem, 1)

            def states(c, u, turn):
                K, Vb = ps[:, 1 + 3 * u, :], ps[:, 2 + 3 * u, :]
                dve.wait_ge(s_mmC.sem, s_mmC.done(c, 2))
                for s in range(SPC):
                    t = slice(s * T, (s + 1) * T)
                    ins = dve.tensor_tensor_scan(sk[:, u, t], decay_row[:], K[:, t], 0.0, ALU.mult, ALU.add)
                ins.then_inc(s_kvC.sem, 1)
                dve.wait_ge(s_kvC.sem, s_kvC.done(c, 1))
                dve.scalar_tensor_tensor(out=sk[:, u, :], in0=sk[:, u, :], scalar=first[:], in1=K,
                                         op0=ALU.mult, op1=ALU.add).then_inc(s_kvC.sem, 1)
                dve.wait_ge(s_kvC.sem, s_kvC.done(c, 2))
                dve.tensor_tensor(sk[:, u, :], sk[:, u, :], Vb, ALU.mult).then_inc(s_kvC.sem, 1)
                dve.wait_ge(s_kvC.sem, s_kvC.done(c, 3))
                dve.wait_ge(s_sig.sem, s_sig.done(c))
                dve.wait_ge(s_out.sem, s_out.freed(NEW0["C"] + c))
                dve.tensor_tensor(y[:, u, :], sk[:, u, :], rg[:, u, :], ALU.mult).then_inc(s_kvC.sem, 1)


            def convolve(c, u, turn):
                dve.wait_ge(s_xT.sem, s_xT.done(TR0["D"] + c))
                dve.wait_ge(s_mmD.sem, s_mmD.freed(c))
                o = hc[:, u, :].rearrange("p (s t) -> p s t", s=SPC)
                dve.tensor_scalar(o, hp[:, u, :, 2:T + 2], par("conv2"), None, ALU.mult).then_inc(s_conv.sem, 1)
                for k, name in ((1, "conv1"), (0, "conv0")):
                    dve.wait_ge(s_conv.sem, s_conv.done(c, 2 - k))
                    dve.scalar_tensor_tensor(out=o, in0=hp[:, u, :, k:k + T], scalar=par(name), in1=o,
                                             op0=ALU.mult, op1=ALU.add).then_inc(s_conv.sem, 1)

            def rotations(c, u, turn):
                for n in range(2):
                    for k in range(2):
                        dve.wait_ge(s_mmD.sem, s_mmD.done(c, 2 * n + k + 1))
                        dve.wait_ge(s_full.sem, s_full.done(c, n - 1))
                        dve.tensor_tensor(
                            rot[:, n, k, :].rearrange("p (s t) -> p s t", s=SPC),
                            ps[:, 1 + 2 * n + k, :].rearrange("p (s t) -> p s t", s=SPC),
                            rope[:, k:k + 1, :].to_broadcast([P, SPC, T]), ALU.mult).then_inc(s_rot.sem, 1)

            def remainder(n):
                def part(c, u, turn):
                    dve.wait_ge(s_hi.sem, s_hi.done(c, n + 1))
                    dve.tensor_tensor(rem[:, n, :], full[:, n, :], kq[:, u, n, 0, :], ALU.subtract)\
                        .then_inc(s_lo.sem, 1)
                return part

            def low_parts(c, u, turn):
                s_st.wait_freed(dve, u, turn)
                for n in range(2):
                    dve.wait_ge(s_hi.sem, s_hi.done(c, n + 3))
                    dve.tensor_tensor(kq[:, u, n, 2, :], rem[:, n, :], kq[:, u, n, 1, :], ALU.subtract)\
                        .then_inc(s_lo.sem, 1)

            dense([("A", 3, add_product("A")), ("A", 2, recur), ("A", 0, scale_inputs("A")),
                   ("B", 2, add_product("B")), ("B", 0, scale_inputs("B")),
                   ("C", 3, add_product("C")), ("C", 2, states), ("C", 1, mixes), ("C", 0, scale_inputs("C")),
                   ("D", 2, rotations), ("D", 1, convolve), ("D", 2, remainder(0)), ("D", 0, scale_inputs("D")),
                   ("D", 2, remainder(1)), ("D", 2, low_parts)])
            dve.wait_ge(ld_w2, 16 * N_W2)
            for k in range(4):
                dve.tensor_copy(masks_b[:, :, k, :], masks[:]).then_inc(prep, 1)
            dve.tensor_copy(before_b[:], before[:]).then_inc(prep, 1)
            dve.tensor_copy(ones_b[:], ones[:, 0:P]).then_inc(prep, 1)

            def maximum(b, u, n):
                dve.wait_ge(s_S.sem, s_S.done(b, n + 1))
                if n == 0:
                    dve.wait_ge(s_mT.sem, s_mT.freed(b))
                if n < 4:
                    to, src = M[:, u, 0, 4 * n:4 * n + 4], ps[:, n % 2, :].rearrange("p (h k) -> p h k", h=4)
                else:
                    h = 2 * (n - 4)
                    to, src = M[:, u, 1, h:h + 2], ps[:, n % 2, :].rearrange("p (h k) -> p h k", h=2)
                dve.tensor_reduce(to, src, AX_X, ALU.max).then_inc(s_max.sem, 1)

            def normalise(b, half):
                u = half
                dve.wait_ge(s_yT.sem, s_yT.done(b, half + 1))
                o = ps[:, 7, :].rearrange("p (g q j c) -> p g q j c", g=2, q=2, j=4)
                dve.reciprocal(rden[:, u], o[:, :, :, :, D]).then_inc(s_rden.sem, 1)
                dve.wait_ge(s_rden.sem, s_rden.done(b, half + 1))
                for q in range(2):
                    to = Y[:, ds(b * 2 + q, 1), half * 64:half * 64 + 64]
                    ins = dve.tensor_tensor(
                        to.rearrange("p o (g j d) -> p (o g) j d", g=2, j=4), o[:, :, q, :, 0:D],
                        rden[:, u, :, q, :].rearrange("p g (j d) -> p g j d", d=1).to_broadcast([P, 2, 4, D]),
                        ALU.mult)
                ins.then_inc(s_yn.sem, 1)

            def minus_max(b, u, turn):
                dve.wait_ge(s_mT.sem, s_mT.done(b))
                s_mrow.wait_freed(dve, u, turn)
                dve.tensor_scalar(mp[:, u, 0, :], ps[0:H, 7, 0:T], -1.0, None, ALU.mult).then_inc(s_mp.sem, 1)
                dve.wait_ge(s_mp.sem, s_mp.done(b, 1))
                dve.scalar_tensor_tensor(out=mp[:, u, 1, :], in0=ps[0:H, 7, 0:T], scalar=-1.0,
                                         in1=mp[:, u, 0, :], op0=ALU.mult, op1=ALU.subtract)\
                    .then_inc(s_mp.sem, 1)

            def attend(s, at, live):
                for n in range(NS):
                    if live(0):
                        b, u, _ = at(0)
                        maximum(b, u % 2, n)
                    if n == 2 and live(2):
                        normalise(at(2)[0], 1)
                if live(1):
                    normalise(at(1)[0], 0)
                if live(0):
                    minus_max(*at(0))

            run_steps(dve, B, attend, 2, LANES)

            def route(c, u, turn):
                if (c + 1) % (NCH // GROUPS_G):
                    return
                g = c // (NCH // GROUPS_G)
                t = slice(g * GT, (g + 1) * GT)
                k = slice(g * GB, (g + 1) * GB)
                wide = lambda a: a.rearrange("p (t e) -> p t e", e=1).to_broadcast([P, GT, E])
                over = lambda a: a.rearrange("p (t e) -> p t e", t=1).to_broadcast([P, GT, E])

                def link(*made):
                    routes[0] += 1
                    made[-1].then_inc(route_v, 1)
                    dve.wait_ge(route_v, routes[0])

                dve.wait_ge(s_lg.sem, s_lg.done(c))
                link(dve.tensor_reduce(lmax[:, t], logits[:, t, :], AX_X, ALU.max))
                link(dve.tensor_tensor(pk[:, t, :], logits[:, t, :], wide(lmax[:, t]), ALU.is_equal))
                link(dve.tensor_tensor(pk[:, t, :], pk[:, t, :], over(pick[:]), ALU.mult))
                link(dve.tensor_reduce(smax[:, t], pk[:, t, :], AX_X, ALU.max))
                link(dve.tensor_tensor(oh[:, t, :], pk[:, t, :], wide(smax[:, t]), ALU.is_equal))
                link(dve.tensor_copy(oh_b[:, t, :], oh[:, t, :]))
                assert routes[0] == ONE_HOT[g]
                dve.wait_ge(s_cnt, g + 1)
                tile_n = ps[:, 5, 0:GT * E].rearrange("p (t e) -> p t e", t=GT)
                link(*(dve.tensor_tensor_scan(cum[:, e, :], ones[:, 0:GT], tile_n[:, :, e], 0.0, ALU.mult, ALU.add)
                       for e in range(E)))
                link(dve.tensor_scalar(padded_i, cum[:, :, GT - 1], float(P - 1), None, ALU.add))
                shift = P.bit_length() - 1
                link(dve.tensor_scalar(padded_i, padded_i, shift, shift, ALU.logical_shift_right,
                                       ALU.logical_shift_left))
                link(dve.tensor_copy(padded, padded_i))
                link(dve.tensor_tensor_scan(ends, ones[:, 0:E], padded, 0.0, ALU.mult, ALU.add))
                link(dve.tensor_tensor(starts, ends, padded, ALU.subtract),
                     dve.tensor_tensor(at4[:, t, :], cum[:].rearrange("p e t -> p t e"), tile_n, ALU.subtract))
                link(dve.tensor_tensor(at4[:, t, :], at4[:, t, :],
                                       ps[:, 4, 0:GT * E].rearrange("p (t e) -> p t e", t=GT), ALU.add))
                link(dve.tensor_tensor(at4[:, t, :], at4[:, t, :], over(starts), ALU.add))
                link(dve.tensor_tensor(at4[:, t, :], at4[:, t, :], oh[:, t, :], ALU.mult))
                link(dve.tensor_reduce(posf[:, t], at4[:, t, :], AX_X, ALU.add))
                link(dve.tensor_copy(pos[:, t], posf[:, t]))
                assert routes[0] == ROUTED[g]
                link(dve.tensor_scalar(expf[:, k], block_at[:], starts[:, 1:2], None, ALU.is_ge))
                for e in range(2, E):
                    link(dve.scalar_tensor_tensor(out=expf[:, k], in0=block_at[:], scalar=starts[:, e:e + 1],
                                                  in1=expf[:, k], op0=ALU.is_ge, op1=ALU.add))
                link(dve.tensor_scalar(exp_i[:, k], expf[:, k], float(FF), None, ALU.mult))

            routes = [0]
            dense([("F", 2, add_product("F")), ("G", 0, scale_inputs("G")), ("G", 2, route)])

            def block_glu(k, u, turn):
                dve.wait_ge(s_silu.sem, s_silu.done(k))
                dve.wait_ge(s_gT.sem, s_gT.freed(k))
                dve.tensor_tensor(glu[:, u, :], sg[:, u, :], ps[:, 3 + u, :], ALU.mult).then_inc(s_glu.sem, 1)

            def block_out(k, u, turn):
                dve.wait_ge(s_dn.sem, s_dn.done(k))
                s_yo.wait_freed(dve, u, turn)
                dve.tensor_copy(yo[:, u, :], ps[:, 6 + u, 0:C]).then_inc(s_yc.sem, 1)

            in_turn(dve, NB, [(1, block_glu), (3, block_out)])
            for c in range(NCH):
                dve.wait_ge(gathered[c], 16 * TPC)
                t = slice(c * TPC, (c + 1) * TPC)
                if c == 0:
                    dve.wait_ge(s_sum.sem, s_sum.done(NCH - 1))
                dve.tensor_tensor(XRES[:, t, :], XRES[:, t, :], X[:, t, :], ALU.add).then_inc(s_fin, 1)

        @block.tensor
        def _(pe):
            for s in (s_tr, s_out, s_mmA, s_mmC, s_mmD, s_S, s_mT, s_ST, s_pv, s_yT, s_turnG, s_rt, s_bT, s_up,
                      s_gT, s_dn):
                s.start(pe)

            def turn(stage):
                def part(c, u, turn_):
                    pe.wait_ge(s_xT.sem, s_xT.done(TR0[stage] + c - 1))
                    if stage == "F":
                        pe.wait_ge(s_yn.sem, s_yn.done(B - 1))
                    else:
                        pe.wait_ge(s_xs.sem, s_xs.done(XS0[stage] + c))
                    for j in range(TPC):
                        src = Y[:, c * TPC + j, :] if stage == "F" else xs[:, u, j, :]
                        ins = pe.transpose(ps[:, 0, j * P:(j + 1) * P], src, ident[:])
                    ins.then_inc(s_tr.sem, 1)
                return part

            def product(stage, a, w, ready):
                k0 = NEW0[stage]

                def part(c, u, turn_):
                    ready(c)
                    pe.wait_ge(s_new.sem, s_new.freed(k0 + c) if stage in "BF" and c > 0 else s_new.done(k0 + c - 1))
                    for j in range(TPC):
                        ins = pe.matmul(ps[:, out_bank(stage, u), j * C:(j + 1) * C], a[:, u, j * P:(j + 1) * P], w[:],
                                        start=(j == 0), stop=True, skip_group_check=True)
                    ins.then_inc(s_out.sem, 1)
                return part

            pe.wait_ge(ld_w, 16 * N_W)
            pe.wait_ge(prep, 7)

            def project_a(c, u, turn_):
                pe.wait_ge(s_xT.sem, s_xT.done(TR0["A"] + c))
                pe.wait_ge(s_actA.sem, s_actA.freed(c))
                for n in range(3):
                    pe.matmul(ps[:, 1 + 3 * u + n, :], W_in[:, n * C:(n + 1) * C], xT[:, u, :],
                              start=True, stop=True).then_inc(s_mmA.sem, 1)


            def project_c(c, u, turn_):
                pe.wait_ge(s_kvC.sem, s_kvC.freed(c))
                pe.wait_ge(s_sig.sem, s_sig.freed(c))
                if c == 1:
                    pe.wait_ge(s_new.sem, s_new.done(NEW0["B"] + NCH - 1))
                for n in range(3):
                    pe.wait_ge(s_mix.sem, s_mix.done(c, n + 1))
                    pe.matmul(ps[:, 1 + 3 * u + n, :], W_kvr[:, n * C:(n + 1) * C], mix[:, u, n, :],
                              start=True, stop=True).then_inc(s_mmC.sem, 1)


            def project_d(c, u, turn_):
                pe.wait_ge(s_conv.sem, s_conv.done(c))
                if c == 0:
                    pe.wait_ge(s_kvC.sem, s_kvC.done(NCH - 1))
                for n in range(4):
                    pe.wait_ge(s_rot.sem, s_rot.done(c - 1, n + 1))
                    pe.matmul(ps[:, 1 + n, :], W_qk[:, n * C:(n + 1) * C], hc[:, u, :],
                              start=True, stop=True).then_inc(s_mmD.sem, 1)
                pe.wait_ge(s_v.sem, s_v.done(c - 1))
                for j in range(TPC):
                    ins = pe.matmul(ps[:, 5, j * C:(j + 1) * C], hc[:, u, j * P:(j + 1) * P], W_v[:],
                                    start=(j == 0), stop=True, skip_group_check=True)
                ins.then_inc(s_mmD.sem, 1)

            def weights_there(c, u, turn_):
                if c == 0:
                    pe.wait_ge(ld_w2, 16 * N_W2)

            dense([("A", 3, product("A", y, W_out, lambda c: pe.wait_ge(s_y.sem, s_y.done(c)))),
                   ("A", 1, project_a), ("A", 0, turn("A")),
                   ("B", 1, product("B", xT, W_ffn, lambda c: pe.wait_ge(s_xT.sem, s_xT.done(TR0["B"] + c)))),
                   ("B", 0, turn("B")), ("C", 0, weights_there),
                   ("C", 3, product("C", y, W_o, lambda c: pe.wait_ge(s_kvC.sem, s_kvC.done(c)))),
                   ("C", 1, project_c), ("C", 0, turn("C")), ("D", 1, project_d), ("D", 0, turn("D"))])
            pe.wait_ge(prep, 13)

            def scores(b, lane, n):
                pe.wait_ge(s_max.sem, s_max.done(b, n - 1))
                bank = ps[:, n % 2, :]
                if n < 4:
                    pe.matmul(bank, ident_b[:], masks_b[:, 0].rearrange("p k c -> p (k c)"), start=True, stop=False,
                              skip_group_check=True)
                    for k in range(4):
                        ins = pe.matmul(bank[:, k * P:(k + 1) * P], QS[0:MAX_ROW, lane, 4 * n + k, 0:P],
                                        KS[0:MAX_ROW, lane, 4 * n + k, 0:P], start=False, stop=True,
                                        skip_group_check=True)
                else:
                    h = 2 * (n - 4)
                    pe.matmul(bank.rearrange("p (h k c) -> p h k c", h=2, k=2)[:, :, 1, :], ident_b[:],
                              masks_b[:, 0, 0:2, :], start=True, stop=False, skip_group_check=True)
                    for k in range(2):
                        ins = pe.matmul(bank[:, k * T:(k + 1) * T], QS[0:MAX_ROW, lane, h + k, P:T],
                                        KS[0:MAX_ROW, lane, h + k, :], start=False, stop=True,
                                        skip_group_check=True)
                ins.then_inc(s_S.sem, 1)

            def turned_scores(b, lane, g):
                kb, h0, nh = GROUPS[g]
                pe.wait_ge(s_exp.sem, s_exp.done(b, g - 1))
                for half in range(2):
                    bank = ps[:, 2 + 2 * (g % 2) + half, :]
                    if kb == 0:
                        pe.matmul(bank.rearrange("p (h k c) -> p h k c", h=2, k=2)[:, :, 0, :], ident_b[:],
                                  masks_b[:, 1, 0:2, :], start=True, stop=False, skip_group_check=True)
                    else:
                        pe.matmul(bank, ident_b[:], masks_b[:, 1].rearrange("p k c -> p (k c)"), start=True,
                                  stop=False, skip_group_check=True)
                    w = T - kb * P
                    for k in range(nh // 2):
                        h = h0 + half * nh // 2 + k
                        ins = pe.matmul(bank[:, k * w:(k + 1) * w], KS[:, lane, h, kb * P:(kb + 1) * P],
                                        QS[:, lane, h, kb * P:T], start=False, stop=True, skip_group_check=True)
                ins.then_inc(s_ST.sem, 1)

            def weigh(b, u, g):
                kb, h0, nh = GROUPS[g]
                pe.wait_ge(s_exp.sem, s_exp.done(b, g + 1))
                if g in (0, 3):
                    pe.wait_ge(s_yr.sem, s_yr.done(b, g // 3))
                w = T - kb * P
                for k in range(nh):
                    h = h0 + k
                    j, q = h % 4, h // 4 % 2
                    ins = pe.matmul(ps[32 * j:32 * j + 32, 6, q * T + kb * P:(q + 1) * T], Vx[:, u, kb, h, :],
                                    Pt[:, g % 2, k * w:(k + 1) * w], start=(g % 3 == 0), stop=(kb == 1),
                                    skip_group_check=True)
                ins.then_inc(s_pv.sem, 1)

            def turn_outputs(b, half):
                pe.wait_ge(s_yn.sem, s_yn.done(b, half))
                pe.wait_ge(s_yr.sem, s_yr.done(b, half + 1))
                for k in range(4):
                    ins = pe.transpose(ps[:, 7, k * P:(k + 1) * P], yr[:, half, k * P:(k + 1) * P], ident[:])
                ins.then_inc(s_yT.sem, 1)

            def attend(s, at, live):
                if live(0):
                    s_ldst.wait_done(pe, at(0)[1], at(0)[2])
                if live(1):
                    b1, lane1, turn1 = at(1)
                    pe.wait_ge(s_vx.sem, s_vx.done(b1))
                for g in range(NG):
                    if live(0) and g < 4:
                        for n in range(3 * g, 3 * g + 3):
                            scores(at(0)[0], at(0)[1], n)
                    if g == 0 and live(2):
                        b2 = at(2)[0]
                        pe.wait_ge(s_mp.sem, s_mp.done(b2 + 1 if live(1) else b2))
                        turn_outputs(b2, 1)
                    if live(1):
                        if g == 0:
                            s_mrow.wait_done(pe, lane1, turn1)
                        turned_scores(b1, lane1, g)
                        if g > 0:
                            weigh(b1, lane1 % 2, g - 1)
                        if g == 4:
                            pe.wait_ge(s_mp.sem, s_mp.done(b1))
                            turn_outputs(b1, 0)
                    if g == 4 and live(0):
                        b0, lane0, _ = at(0)
                        pe.wait_ge(s_max.sem, s_max.done(b0))
                        if live(1):
                            pe.wait_ge(s_yn.sem, s_yn.done(b1, 1))
                        for q in range(2):
                            ins = pe.transpose(ps[0:H, 7, q * P:(q + 1) * P], M[:, lane0 % 2, q, :], ident[:])
                        ins.then_inc(s_mT.sem, 1)
                if live(1):
                    weigh(b1, lane1 % 2, NG - 1)

            run_steps(pe, B, attend, 2, LANES)

            def turn_g(c, u, turn_):
                pe.wait_ge(s_xTG.sem, s_xTG.done(c - 1))
                pe.wait_ge(s_xs.sem, s_xs.done(XS0["G"] + c))
                for j in range(TPC):
                    ins = pe.transpose(ps[:, 1, j * P:(j + 1) * P], HN[:, c * TPC + j, :], ident[:])
                ins.then_inc(s_turnG.sem, 1)

            def logits_g(c, u, turn_):
                pe.wait_ge(s_xTG.sem, s_xTG.done(c))
                pe.wait_ge(s_lg.sem, s_lg.freed(c))
                for j in range(TPC):
                    ins = pe.matmul(ps[:, 2 + u, j * E:(j + 1) * E], xTg[:, u, j * P:(j + 1) * P], W_router[:],
                                    start=(j == 0), stop=True, skip_group_check=True)
                ins.then_inc(s_rt.sem, 1)

            def count_g(c, u, turn_):
                if (c + 1) % (NCH // GROUPS_G):
                    return
                g = c // (NCH // GROUPS_G)
                pe.wait_ge(route_v, ONE_HOT[g])
                o = oh_b[:, g * GT:(g + 1) * GT, :].rearrange("p t e -> p (t e)")
                pe.matmul(ps[:, 4, 0:GT * E], before_b[:], o, start=True, stop=True)
                pe.matmul(ps[:, 5, 0:GT * E], ones_b[:], o, start=True, stop=True).then_inc(s_cnt, 1)

            dense([("F", 1, product("F", xT, W_proj, lambda c: pe.wait_ge(s_xT.sem, s_xT.done(TR0["F"] + c)))),
                   ("F", 0, turn("F")), ("G", 2, count_g), ("G", 1, logits_g), ("G", 0, turn_g)])

            pe.wait_ge(ld_e, 32)
            pe.wait_ge(route_v, ROUTED[-1] + E)

            def block_turn(k, u, turn_):
                s_hs.wait_done(pe, u, turn_)
                pe.wait_ge(s_hT.sem, s_hT.done(k - 1))
                pe.transpose(ps[:, 0, 0:P], hs[:, u, :], ident[:]).then_inc(s_bT.sem, 1)

            def block_up(k, u, turn_, e):
                pe.wait_ge(s_hT.sem, s_hT.done(k))
                pe.wait_ge(s_glu.sem, s_glu.freed(k))
                for n in range(2):
                    ins = pe.matmul(ps[:, 1 + 2 * n + u % 2, :], hT[:, u % 2, :], W_up[:, ds(e * 2 + n * FF, FF)],
                                    start=True, stop=True)
                ins.then_inc(s_up.sem, 1)

            def block_back(k, u, turn_):
                pe.wait_ge(s_glu.sem, s_glu.done(k))
                pe.wait_ge(s_gTc.sem, s_gTc.done(k - 1))
                for f in range(FB):
                    ins = pe.transpose(ps[:, 5, f * P:(f + 1) * P], glu[:, u % 2, f * P:(f + 1) * P], ident[:])
                ins.then_inc(s_gT.sem, 1)

            def block_down(k, u, turn_, e):
                pe.wait_ge(s_gTc.sem, s_gTc.done(k))
                pe.wait_ge(s_yc.sem, s_yc.freed(k))
                for f in range(FB):
                    ins = pe.matmul(ps[:, 6 + u % 2, 0:C], gT[:, u % 2, f * P:(f + 1) * P],
                                    W_down[:, ds(e + f * C, C)], start=(f == 0), stop=(f == FB - 1))
                ins.then_inc(s_dn.sem, 1)

            def blocks(s, at, live):
                def expert(l):
                    return pe.value_load(exp_i[0:1, ds(at(l)[0], 1)], min_val=0, max_val=(E - 1) * FF)

                if live(3):
                    block_back(*at(3))
                if live(1):
                    block_up(*at(1), expert(1))
                if live(3):
                    block_down(*at(3), expert(3))
                if live(0):
                    block_turn(*at(0))

            run_steps(pe, NB, blocks, 3, LANES)


_OUTS = [((B, T, C), "float32")]


def kernel(**inputs):
    import numpy as np
    import concourse.bacc as bacc
    from concourse.bass_utils import run_bass_kernel_spmd as run

    g = {k: np.asarray(v) for k, v in inputs.items()}
    L1 = "L1_attn_"
    F = "L1_ffn_"
    turned = np.arange(C).reshape(H, 2, D // 2)[:, ::-1].reshape(-1)
    wq, wk, wv = (g[F + "attn_w"][:, k * C:(k + 1) * C] for k in range(3))
    columns = [g["L0_attn_w_norm"], g["L0_attn_lambda_log"], g[L1 + "time_mix_k"], g[L1 + "time_mix_v"],
               g[L1 + "time_mix_r"], g[L1 + "time_decay"], g[L1 + "time_first"], g[L1 + "ln_w"], g[L1 + "ln_b"],
               g[F + "ln1_w"], g[F + "ln1_b"], g[F + "ln2_w"], g[F + "ln2_b"],
               g[F + "conv_w"][:, 0, 0], g[F + "conv_w"][:, 0, 1], g[F + "conv_w"][:, 0, 2]]
    freq = (1.0 / np.float32(10000.0) ** (np.arange(0, D, 2, dtype=np.float32) / np.float32(D))).astype(np.float32)
    angle = np.arange(T, dtype=np.float32)[:, None] * freq[None, :]
    angle = np.concatenate([angle, angle], 1).T
    sign = np.where(np.arange(D) < D // 2, -1.0, 1.0)[:, None]
    rope = np.stack([np.tile(np.cos(angle), (H, 1)), np.tile(np.sin(angle) * sign, (H, 1))], 1).astype(np.float32)
    q, k = np.arange(P)[:, None], np.arange(P)[None, :]
    before = (q < k).astype(np.float32)
    mask = np.stack([np.where(k > q, -1e30, 0.0), np.where(q > k, -1e30, 0.0)], 1).astype(np.float32)
    arrays = {
        "x": g["L0_attn_x"].reshape(TOK, C),
        "params": np.stack(columns, 1),
        "w_in": g["L0_attn_W_in"], "w_out": g["L0_attn_W_out"], "w_ffn": g["L0_ffn_weight"].T,
        "disha2": np.concatenate([g["L0_ffn_disha"], g["L0_ffn_disha"]], 0),
        "w_kvr": np.concatenate([g[L1 + "Wk"].T, g[L1 + "Wv"].T, g[L1 + "Wr"].T], 1), "w_o": g[L1 + "Wo"].T,
        "w_qk": np.concatenate([wq, wq[:, turned], wk, wk[:, turned]], 1), "w_v": wv, "w_proj": g[F + "proj_w"],
        "w_router": g[F + "router_w"], "w_up": g[F + "expert_wv"].transpose(1, 0, 2).reshape(C, E * 2 * FF),
        "w_down": g[F + "expert_proj"].reshape(E, FB, P, C).transpose(2, 0, 1, 3).reshape(P, E * FF),
        "ident": np.eye(P, dtype=np.float32), "rope": rope, "mask": mask,
        "pick": np.tile(np.arange(E, 0, -1, dtype=np.float32), (P, 1)),
        "before": before, "block": np.tile(np.arange(GB, dtype=np.float32) * P, (P, 1)),
    }
    nc = bacc.Bacc("TRN2", target_bir_lowering=False, num_devices=1)
    data, args = {}, []
    for name, a in arrays.items():
        a = np.ascontiguousarray(a)
        data[f"in_{name}"] = a
        args.append(nc.dram_tensor(f"in_{name}", a.shape, mybir.dt.from_np(a.dtype), kind="ExternalInput").ap())
    o = nc.dram_tensor("out_0", [TOK, C], F32, kind="ExternalOutput").ap()
    model_kernel(nc, *args, o)
    r = run(nc, [data], core_ids=[0])
    return r.results[0]["out_0"].reshape(B, T, C)
```

```python
from contextlib import ExitStack

import concourse.bass as bass
from concourse import mybir

F32 = mybir.dt.float32
BF16 = mybir.dt.bfloat16
I32 = mybir.dt.int32
U32 = mybir.dt.uint32
ALU = mybir.AluOpType
ACT = mybir.ActivationFunctionType
AX_X = mybir.AxisListType.X
ds = bass.ds

P = 128
B, T, C = 16, 256, 128
TOK = B * T
NT = TOK // P
CH = 512
NCH = TOK // CH
TPC = CH // P
SPC = CH // T
H, D = 16, 8
E, FF = 4, 512
FB = FF // P
GROUPS_G = 2
GT = NT // GROUPS_G
GB = GT + E - 1
NB = GROUPS_G * GB
LN_EPS, RMS_EPS = 1e-5, 1e-6
SCALE = float(D) ** -0.5
Q_PART = (0, 0, 0, 1, 1, 2)
K_PART = (0, 1, 2, 0, 1, 0)
MAX_ROW = 96
LANES = 4
PARAMS = ["w_norm", "lambda_log", "mix_k", "mix_v", "mix_r", "decay", "first", "ln_w", "ln_b",
          "ln1_w", "ln1_b", "ln2_w", "ln2_b", "conv0", "conv1", "conv2"]
GROUPS = ((0, 0, 4), (0, 4, 4), (1, 0, 8), (0, 8, 4), (0, 12, 4), (1, 8, 8))
NG = len(GROUPS)
NS = 12


class Signal:

    def __init__(self, sem, per=1):
        self.sem, self.per = sem, per

    def start(self, eng):
        eng.sem_inc(self.sem, 2 * self.per)

    def done(self, c, n=None):
        return (c + 2) * self.per + (self.per if n is None else n)

    def freed(self, c):
        return (c + 1) * self.per


class Fixed:

    def __init__(self, sem):
        self.sem = sem


class Lanes:

    def __init__(self, sems, per):
        self.sems, self.per = sems, per

    def start(self, eng):
        for s in self.sems:
            eng.sem_inc(s, self.per)

    def wait_done(self, eng, u, turn):
        eng.wait_ge(self.sems[u], (turn + 2) * self.per)

    def wait_freed(self, eng, u, turn):
        eng.wait_ge(self.sems[u], (turn + 1) * self.per)


def run_steps(eng, n, step, lag, period=2, peel=1):
    lo = max((lag + period - 1) // period, peel) * period
    hi = lo + (n - lo) // period * period

    def fixed(s):
        step(s, lambda l: (s - l, (s - l) % period, (s - l) // period), lambda l: 0 <= s - l < n)

    for s in range(lo):
        fixed(s)
    if hi > lo:
        with eng.Fori(0, (hi - lo) // period) as i:
            for w in range(lo, lo + period):
                step(i * period + w,
                     lambda l: (i * period + (w - l), (w - l) % period, i + (w - l) // period),
                     lambda l: True)
    for s in range(hi, n + lag):
        fixed(s)


START = {k: [n * NCH + (n > 0) + c for c in range(NCH)] for n, k in enumerate("ABCD")}
START["F"] = list(range(NCH))
START["G"] = [c // 4 * 4 + 6 + c % 4 // 2 for c in range(NCH)]


def dense(parts):
    steps = {}
    for n, (stage, lag, part) in enumerate(parts):
        for c in range(NCH):
            steps.setdefault(START[stage][c] + lag, []).append((n, c, part))
    for s in sorted(steps):
        for _, c, part in sorted(steps[s], key=lambda a: a[:2]):
            part(c, c % 2, c // 2)


def in_turn(eng, n, parts, period=2, peel=1):
    def step(s, at, live):
        for lag, part in parts:
            if live(lag):
                part(*at(lag))
    run_steps(eng, n, step, max(lag for lag, _ in parts), period, peel)


def model_kernel(nc, x_in, params_in, w_in, w_out, w_ffn, disha2, w_kvr, w_o, w_qk, w_v, w_proj,
                 w_router, w_up, w_down, ident_in, rope_in, mask_in, pick_in, before_in, block_in, code_in, out):
    x_tiles = x_in.rearrange("(n p) c -> p n c", p=P)
    qk_dram = nc.dram_tensor("qk_parts", [2, 3, P, TOK], BF16, kind="Internal").ap()

    sorted_in, sorted_res = ([nc.dram_tensor(f"{name}{g}", [GB * P, w], F32, kind="Internal").ap()
                              for g in range(GROUPS_G)] for name, w in (("sorted_in", C), ("sorted_res", C + 1)))

    with ExitStack() as ctx:
        def sb(name, shape, dt=F32):
            return ctx.enter_context(nc.sbuf_tensor(name, shape, dt))

        def sem(name):
            return ctx.enter_context(nc.semaphore(name))

        def signal(name, per=1):
            return Signal(sem(name), per)

        X = sb("X", [P, NT, C])
        XR = sb("XR", [P, NT, C + 1])
        XRES = XR[:, :, 0:C]
        codes = sb("codes", [P, NT])
        Y = sb("Y", [P, NT, C])
        V = sb("V", [P, NT, C])
        XA = V
        bn = sb("bn", [P, NT, 6])
        mean, var = (sb(k, [P, NT]) for k in ("mean", "var"))
        tv, rsq, nt = (sb(k, [P, 2, NT]) for k in ("tv", "rsq", "nt"))
        r1, rs = rsq[:, 0, :], rsq[:, 1, :]
        half = nt[:, 0, :]
        rp1, mr, ms = (sb(k, [P, NT]) for k in ("rp1", "mr", "ms"))
        params = sb("params", [P, len(PARAMS)])
        W_in = sb("W_in", [P, 3 * C])
        W_out = sb("W_out", [P, C])
        W_ffn = sb("W_ffn", [P, C])
        DISHA = sb("DISHA", [P, C])
        W_kvr = sb("W_kvr", [P, 3 * C])
        W_o = sb("W_o", [P, C])
        W_qk = sb("W_qk", [P, 4 * C])
        W_v = sb("W_v", [P, C])
        W_proj = sb("W_proj", [P, C])
        W_router = sb("W_router", [P, E])
        ident = sb("ident", [P, P])
        ident_b = sb("ident_b", [P, P], BF16)
        rope = sb("rope", [P, 2, T])
        masks = sb("masks", [P, 2, P])
        masks_b = sb("masks_b", [P, 2, 4, P], BF16)
        pick = sb("pick", [P, E])
        lam = sb("lam", [P, 2])
        dec = sb("dec", [P, 2])
        first = sb("first", [P, 1])
        decay_row = sb("decay_row", [P, T])
        ones = sb("ones", [P, T])
        xs = sb("xs", [P, 2, TPC, C])
        xT = sb("xT", [P, 2, CH])
        ta, tr, gv, ga, rv, uu, y = (sb(k, [P, 2, CH]) for k in ("ta", "tr", "gv", "ga", "rv", "uu", "y"))
        hp = sb("hp", [P, 2, SPC, T + 2])
        dif, sk, rg = ta, tr, gv
        mix = sb("mix", [P, 2, 3, CH])
        hc = ga
        rot = mix
        full, rem = rv, uu
        kq = Y[:].rearrange("p n c -> p (n c)").bitcast(BF16)[:, 0:2 * 2 * 3 * CH].rearrange(
            "p (u n a t) -> p u n a t", u=2, n=2, a=3)
        stack_q = sb("stack_q", [P, LANES * H * T // 2])
        QS = stack_q[:].bitcast(BF16).rearrange("p (l h t) -> p l h t", l=LANES, h=H)
        W_up = stack_q[:, 0:E * 2 * FF]
        W_down = stack_q[:, E * 2 * FF:E * 3 * FF]
        stack_k = sb("stack_k", [P, LANES * H * T // 2])
        KS = stack_k[:].bitcast(BF16).rearrange("p (l h t) -> p l h t", l=LANES, h=H)
        Vx = sb("Vx", [P, 2, 2, H, 32])
        Pt = mix[:].rearrange("p u n t -> p (u n t)")[:, 0:2048].rearrange("p (u n) -> p u n", u=2)
        M = sb("M", [P, 2, 2, H])
        mp = hp[:].rearrange("p u s t -> p (u s t)").bitcast(BF16)[0:H, 0:LANES * 2 * T].rearrange(
            "h (l r t) -> h l r t", l=LANES, r=2)
        yr = xs[:].rearrange("p u t c -> p u (t c)")
        rden = sb("rden", [P, 2, 2, 2, 4])
        HN = Y
        used = [0]

        def late(*shape):
            n = 1
            for k in shape:
                n *= k
            a = stack_k[:, used[0]:used[0] + n]
            used[0] += n
            if len(shape) == 1:
                return a
            names = "abc"[:len(shape)]
            return a.rearrange(f"p ({' '.join(names)}) -> p {' '.join(names)}",
                               **{k: v for k, v in zip(names, shape)})

        hs = late(LANES, C)
        hT, yo = late(2, C), late(LANES, C)
        res = late(LANES, C + 1)
        row = late(LANES).bitcast(U32)
        xTg, sg, glu, gT = ta, tr, gv, ga
        before = sb("before", [P, P])
        before_b, ones_b = (sb(k, [P, P], BF16) for k in ("before_b", "ones_b"))
        block_at = sb("block_at", [P, GB])
        logits, pk, oh, at4 = (late(NT, E) for _ in range(4))
        oh_b = late(NT * E // 2).bitcast(BF16).rearrange("p (t e) -> p t e", e=E)
        lmax, smax, posf = (late(NT) for _ in range(3))
        pos = late(NT).bitcast(U32)
        cum = late(E, GT)
        padded_i = late(E).bitcast(I32)
        padded, ends, starts = (late(E) for _ in range(3))
        expf = late(NB)
        exp_i = late(NB).bitcast(I32)
        ps = ctx.enter_context(nc.psum_tensor("ps", [P, 8, 512], F32))

        def par(name):
            k = PARAMS.index(name)
            return params[:, k:k + 1]

        ld_x = [sem(f"ld_x{c}") for c in range(NCH)]
        ld_w = sem("ld_w")
        N_W, N_W2 = 6, 12
        ld_w2 = sem("ld_w2")
        ld_e = sem("ld_e")
        prep = sem("prep")
        prep_act = sem("prep_act")
        prep_pool = sem("prep_pool")
        N_POOL = 7
        stat_v = sem("stat_v")
        s_xs = signal("s_xs")
        s_new = signal("s_new")
        s_res, s_res2 = signal("s_res"), signal("s_res2")
        s_tr = signal("s_tr")
        s_xT = signal("s_xT")
        s_out = signal("s_out")
        s_mmA = signal("s_mmA", 3)
        s_actA = signal("s_actA", 5)
        s_rv = signal("s_rv")
        s_uu = signal("s_uu")
        s_y = signal("s_y")
        s_dif = signal("s_dif")
        s_mix = signal("s_mix", 3)
        s_mmC = signal("s_mmC", 3)
        s_sig = signal("s_sig")
        s_kvC = signal("s_kvC", 3)
        s_yC = signal("s_yC")
        s_xsC = signal("s_xsC")
        s_conv = signal("s_conv", 2)
        s_mmD = signal("s_mmD", 5)
        s_rot = signal("s_rot", 4)
        s_full = signal("s_full", 2)
        s_hi = signal("s_hi", 4)
        s_rem, s_lo = signal("s_rem", 2), signal("s_lo", 2)
        s_tap = signal("s_tap")
        s_v = signal("s_v")
        s_st = Lanes([sem(f"s_st{u}") for u in range(2)], 32)
        s_ldst = Lanes([sem(f"s_ldst{u}") for u in range(LANES)], 16 * 12)
        s_mrow = Lanes([sem(f"s_mrow{u}") for u in range(LANES)], 32)
        s_S = signal("s_S", NS)
        s_max = signal("s_max", NS)
        s_mT = signal("s_mT")
        s_mp = signal("s_mp", 2)
        s_ST = signal("s_ST", NG)
        s_exp = signal("s_exp", NG)
        s_pv = signal("s_pv", NG)
        s_yr = signal("s_yr", 2)
        s_yT = signal("s_yT", 2)
        s_rden = signal("s_rden", 2)
        s_yn = signal("s_yn", 2)
        s_vx = signal("s_vx")
        summed = sem("summed")
        zeroed = sem("zeroed")
        s_turnG, s_xTG, s_rt, s_lg = (signal(k) for k in ("s_turnG", "s_xTG", "s_rt", "s_lg"))
        s_cnt = sem("s_cnt")
        route_v = sem("route_v")
        scattered = [sem(f"scattered{g}") for g in range(GROUPS_G)]
        scattered_res = [sem(f"scattered_res{g}") for g in range(GROUPS_G)]
        s_hs = Lanes([sem(f"s_hs{u}") for u in range(LANES)], 16)
        s_lres = Lanes([sem(f"s_lres{u}") for u in range(LANES)], 16)
        outputs = [sem(f"outputs{u}") for u in range(LANES)]
        s_bT, s_hT, s_up, s_silu, s_glu, s_gT, s_gTc, s_dn, s_yc = (
            signal(k) for k in ("s_bT", "s_hT", "s_up", "s_silu", "s_glu", "s_gT", "s_gTc", "s_dn", "s_yc"))

        XS0 = {k: NCH * n for n, k in enumerate("ABDG")}
        TR0 = {k: NCH * n for n, k in enumerate("ABCDF")}
        RES0 = {k: NCH * n for n, k in enumerate("ACF")}
        NEW0 = {k: NCH * n for n, k in enumerate("ABCF")}
        TWICE = "ACD"
        source = {"A": X, "B": X, "C": X, "D": X, "G": XA}

        def out_bank(stage, u):
            return 7 - u if stage in "BF" else 7

        def scaled(stage, c):
            s, n = (s_xsC, c) if stage == "C" else (s_xs, XS0[stage] + c)
            return s.sem, s.done(n)

        FACTORS = {"A": 15, "B": 14, "C": 15, "D": 15, "G": 14}
        factors_c = [2 * (FACTORS["A"] + FACTORS["B"]) + (h + 1) * FACTORS["C"] for h in range(2)]

        ONE_HOT = [6 + g * (17 + E) for g in range(GROUPS_G)]
        ROUTED = [17 + g * (17 + E) for g in range(GROUPS_G)]

        block = ctx.enter_context(nc.Block())

        @block.sync
        def _(sp):
            for s in (s_st, s_ldst, s_mrow, s_hs, s_lres):
                s.start(sp)
            for c in range(NCH):
                sp.dma_start(X[:, c * TPC:(c + 1) * TPC, :], x_tiles[:, c * TPC:(c + 1) * TPC, :])\
                  .then_inc(ld_x[c], 16)

            def store_parts(c, u, turn):
                for n in range(2):
                    sp.wait_ge(s_lo.sem, s_lo.done(c, n + 1))
                    sp.dma_start(qk_dram[n, :, :, ds(c * CH, CH)].rearrange("a p t -> p a t"),
                                 kq[:, u, n, :, :]).then_inc(s_st.sems[u], 16)

            sp.wait_ge(prep_pool, 3)
            for g in range(GROUPS_G):
                for to, w in ((sorted_in, C), (sorted_res, C + 1)):
                    sp.dma_start(to[g].rearrange("(p n) c -> p (n c)", p=P), stack_q[:, 0:GB * w]).then_inc(zeroed, 16)

            def load_stack(b, u, turn):
                if not isinstance(b, int) or b >= LANES:
                    sp.wait_ge(s_ST.sem, s_ST.done(b - LANES))
                for n, (dst, split) in enumerate(((QS, Q_PART), (KS, K_PART))):
                    for k, part in enumerate(split):
                        sp.dma_start(
                            dst[D * k:D * (k + 1), u, :, :],
                            qk_dram[n, part, :, ds(b * T, T)].rearrange("(h d) t -> d h t", d=D),
                        ).then_inc(s_ldst.sems[u], 16)

            def first_stacks(c, u, turn):
                if c * SPC >= LANES:
                    return
                if c == 0:
                    sp.wait_ge(prep_pool, N_POOL)
                    sp.wait_ge(zeroed, 32 * GROUPS_G)
                s_st.wait_done(sp, u, turn)
                for b in range(c * SPC, (c + 1) * SPC):
                    load_stack(b, b % LANES, b // LANES)

            def other_stacks(b, u, turn):
                if not isinstance(b, int) or b >= LANES:
                    load_stack(b, u, turn)

            def max_rows(b, u, turn):
                sp.wait_ge(s_mp.sem, s_mp.done(b))
                for r in range(2):
                    sp.dma_start(QS[MAX_ROW + r:MAX_ROW + r + 1, u, :, :], mp[:, u, r, :])\
                      .then_inc(s_mrow.sems[u], 16)

            dense([("D", 3, store_parts), ("D", 4, first_stacks)])
            for u in range(2):
                s_st.wait_done(sp, u, NCH // 2 - 1)
            in_turn(sp, B, [(0, other_stacks), (2, max_rows)], LANES)

            sp.wait_ge(s_ST.sem, s_ST.done(B - 1))
            sp.dma_start(W_up, w_up).then_inc(ld_e, 16)
            sp.dma_start(W_down, w_down).then_inc(ld_e, 16)

            def block_rows(tensors, k):
                return tensors[k // GB][k % GB * P:(k % GB + 1) * P, :]

            for s in range(NB + 2):
                if s < NB:
                    u = s % LANES
                    if s % GB == 0:
                        sp.wait_ge(scattered[s // GB], 16 * GT)
                    sp.wait_ge(s_bT.sem, s_bT.done(s - LANES) if s >= LANES else 2)
                    sp.dma_start(hs[:, u, :], block_rows(sorted_in, s)).then_inc(s_hs.sems[u], 16)
                if s >= 2:
                    k = s - 2
                    if k % GB == 0:
                        sp.wait_ge(scattered_res[k // GB], 16 * GT)
                    sp.wait_ge(s_yc.sem, s_yc.done(k - LANES) if k >= LANES else 2)
                    sp.dma_start(res[:, k % LANES, :], block_rows(sorted_res, k)).then_inc(s_lres.sems[k % LANES], 16)
            for u in range(LANES):
                sp.wait_ge(outputs[u], 16 * ((NB - u + LANES - 1) // LANES))

        @block.gpsimd
        def _(pool):
            for s in (s_rv, s_dif, s_vx, s_full, s_res, s_lo, s_yC):
                s.start(pool)
            fills = ((ones[:], 1.0), (hp[:], 0.0), (stack_q[:], 0.0), (stack_k[:], 0.0), (Vx[:], 0.0),
                     (KS[MAX_ROW:MAX_ROW + 2, :, :, :], 1.0), (Vx[:, :, :, :, D:D + 1], 1.0))

            def fill(n):
                if n:
                    pool.wait_ge(prep_pool, n)
                pool.memset(fills[n][0], fills[n][1]).then_inc(prep_pool, 1)

            fill(0)
            fill(1)

            def fill_stacks(c, u, turn):
                if c + 2 < len(fills):
                    fill(c + 2)

            def gates(c, u, turn):
                pool.wait_ge(s_actA.sem, s_actA.done(c, 5))
                pool.wait_ge(s_uu.sem, s_uu.freed(c))
                pool.tensor_tensor(rv[:, u, :], tr[:, u, :], gv[:, u, :], ALU.mult).then_inc(s_rv.sem, 1)

            def shift(c, u, turn):
                pool.wait_ge(s_xT.sem, s_xT.done(TR0["C"] + c))
                pool.wait_ge(s_mix.sem, s_mix.freed(c))
                pool.tensor_tensor(dif[:, u, :].rearrange("p (s t) -> p s t", s=SPC), hp[:, u, :, 2:T + 2],
                                   hp[:, u, :, 1:T + 1], ALU.subtract).then_inc(s_dif.sem, 1)

            def receive(c, u, turn):
                pool.wait_ge(s_kvC.sem, s_kvC.done(c))
                pool.wait_ge(s_sig.sem, s_sig.done(c))
                pool.wait_ge(s_out.sem, s_out.freed(NEW0["C"] + c))
                pool.tensor_tensor(y[:, u, :], sk[:, u, :], rg[:, u, :], ALU.mult).then_inc(s_yC.sem, 1)

            def rotate(c, u, turn):
                for n in range(2):
                    pool.wait_ge(s_rot.sem, s_rot.done(c, 2 * n + 2))
                    pool.wait_ge(s_rem.sem, s_rem.done(c - 1, n + 1))
                    pool.tensor_tensor(full[:, n, :], rot[:, n, 0, :], rot[:, n, 1, :], ALU.add)\
                        .then_inc(s_full.sem, 1)

            def low_parts(c, u, turn):
                s_st.wait_freed(pool, u, turn)
                for n in range(2):
                    pool.wait_ge(s_hi.sem, s_hi.done(c, n + 3))
                    pool.tensor_tensor(kq[:, u, n, 2, :], rem[:, n, :], kq[:, u, n, 1, :], ALU.subtract)\
                        .then_inc(s_lo.sem, 1)

            def keep(stage):
                def part(c, u, turn):
                    pool.wait_ge(*scaled(stage, c))
                    f = r1 if stage == "D" else rp1
                    for n in range(c * TPC, c * TPC + TPC // 2):
                        ins = pool.tensor_scalar(XRES[:, n, :], X[:, n, :], f[:, n:n + 1], mr[:, n:n + 1],
                                                 ALU.mult, ALU.add)
                    ins.then_inc(s_res.sem, 1)
                return part

            dense([("A", 1, gates), ("A", 0, keep("A")), ("B", 0, fill_stacks), ("C", 1, shift), ("C", 0, keep("C")), ("C", 3, receive),
                   ("D", 3, rotate), ("D", 0, keep("D")), ("D", 3, low_parts)])

            def spread_values(b, u, turn):
                pool.wait_ge(s_pv.sem, s_pv.freed(b))
                for kb in range(2):
                    ins = pool.tensor_copy(
                        Vx[:, u % 2, kb, :, 0:D],
                        V[:, ds(b * 2 + kb, 1), :].rearrange("p o (h d) -> p (o h) d", h=H))
                ins.then_inc(s_vx.sem, 1)

            pool.wait_ge(s_v.sem, s_v.done(NCH - 1))
            in_turn(pool, B, [(0, spread_values)])

            def scatter(rows, to, g, t, done):
                pool.indirect_dma_start(
                    out=to[g], out_offset=bass.IndirectOffsetOnAxis(ap=pos[:, t:t + 1], axis=0),
                    in_=rows[:, t, :], in_offset=None).then_inc(done[g], 16)

            def add_streams(c):
                pool.wait_ge(s_new.sem, s_new.done(NEW0["F"] + c))
                t = slice(c * TPC, (c + 1) * TPC)
                pool.tensor_tensor(XRES[:, t, :], X[:, t, :], XA[:, t, :], ALU.add).then_inc(summed, 1)
                pool.wait_ge(summed, c + 1)

            pool.wait_ge(zeroed, 32 * GROUPS_G)
            for c in range(GT // TPC):
                add_streams(c)
            pool.wait_ge(route_v, ROUTED[0])
            for t in range(GT):
                scatter(HN, sorted_in, 0, t, scattered)
            for t in range(GT):
                scatter(XR, sorted_res, 0, t, scattered_res)
            pool.wait_ge(route_v, ROUTED[1])
            for k in range(NB):
                if k < GT:
                    if k % TPC == 0:
                        add_streams((GT + k) // TPC)
                    scatter(HN, sorted_in, 1, GT + k, scattered)
                    scatter(XR, sorted_res, 1, GT + k, scattered_res)
                pool.wait_ge(s_yc.sem, s_yc.done(k))
                pool.indirect_dma_start(
                    out=out, out_offset=bass.IndirectOffsetOnAxis(ap=row[:, k % LANES:k % LANES + 1], axis=0),
                    in_=yo[:, k % LANES, :], in_offset=None, bounds_check=TOK - 1, oob_is_err=False)\
                    .then_inc(outputs[k % LANES], 16)

        @block.scalar
        def _(act):
            for s in (s_xsC, s_tap, s_res2, s_xT, s_actA, s_sig, s_hi, s_v, s_exp, s_yr, s_xTG, s_lg, s_hT, s_silu, s_gTc):
                s.start(act)
            for n, (dst, src) in enumerate((
                    (params[:], params_in), (W_in[:], w_in), (ident[:], ident_in), (W_out[:], w_out),
                    (W_ffn[:], w_ffn), (DISHA[:], disha2), (W_kvr[:], w_kvr), (W_o[:], w_o),
                    (W_qk[:], w_qk), (W_v[:], w_v), (W_proj[:], w_proj), (W_router[:], w_router),
                    (rope[:], rope_in), (masks[:], mask_in), (pick[:], pick_in),
                    (before[:], before_in), (block_at[:], block_in), (codes[:], code_in))):
                act.dma_start(dst, src).then_inc(ld_w if n < N_W else ld_w2, 16)
            act.wait_ge(ld_w, 16 * N_W)
            nc.scalar.activation(first[:], par("first"), ACT.Exp).then_inc(prep_act, 1)
            nc.scalar.activation(lam[:, 0:1], par("lambda_log"), ACT.Tanh, scale=0.5).then_inc(prep_act, 1)
            nc.scalar.activation(dec[:, 0:1], par("decay"), ACT.Tanh, scale=0.5).then_inc(prep_act, 1)

            def constants(c, u, turn):
                copies = [(masks_b[:, :, k, :], masks[:]) for k in range(4)]
                copies += [(before_b[:], before[:]), (ones_b[:], ones[:, 0:P]), (XR[:, :, C], codes[:])]
                if c == 0:
                    act.wait_ge(ld_w2, 16 * N_W2)
                    act.wait_ge(prep_pool, 1)
                if c < len(copies):
                    nc.scalar.copy(*copies[c]).then_inc(prep_act, 1)

            def copy_turned(stage, users):
                def part(c, u, turn):
                    act.wait_ge(s_tr.sem, s_tr.done(TR0[stage] + c))
                    for sig, value in users:
                        act.wait_ge(sig.sem, value(c))
                    nc.scalar.copy(xT[:, u, :], ps[:, 0, :]).then_inc(s_xT.sem, 1)
                return part

            def scale_turned(stage, dst, w, b, users):
                def part(c, u, turn):
                    act.wait_ge(s_tr.sem, s_tr.done(TR0[stage] + c))
                    for sig, value in users:
                        act.wait_ge(sig.sem, value(c))
                    src, to = ps[:, 0, :], dst[:, u]
                    if dst is hp:
                        src, to = src.rearrange("p (s t) -> p s t", s=SPC), hp[:, u, :, 2:T + 2]
                    nc.scalar.activation(to, src, ACT.Identity, bias=par(b), scale=par(w)).then_inc(s_xT.sem, 1)
                return part

            def act_a(c, u, turn):
                act.wait_ge(s_y.sem, s_y.freed(c))
                for n, (dst, fn, scale) in enumerate(((ta, ACT.Tanh, 0.5), (tr, ACT.Tanh, 0.5), (gv, ACT.Gelu, 1.0))):
                    act.wait_ge(s_mmA.sem, s_mmA.done(c, n + 1))
                    nc.scalar.activation(dst[:, u, :], ps[:, 1 + 3 * u + n, :], fn, scale=scale).then_inc(s_actA.sem, 1)
                for dst, src in ((ga, ta), (tr, tr)):
                    act.wait_ge(s_actA.sem, s_actA.done(c, 2))
                    nc.scalar.activation(dst[:, u, :], src[:, u, :], ACT.Copy, bias=0.5, scale=0.5)\
                        .then_inc(s_actA.sem, 1)

            out_b = lambda c: s_out.freed(NEW0["B"] + c)

            def scale_c(c, u, turn):
                act.wait_ge(stat_v, factors_c[c // (NCH // 2)])
                act.wait_ge(s_xs.sem, s_xs.done(XS0["B"] + NCH - 1))
                act.wait_ge(s_tr.sem, s_tr.freed(TR0["C"] + c))
                for j in range(TPC):
                    n = c * TPC + j
                    ins = nc.scalar.activation(xs[:, u, j, :], X[:, n, :], ACT.Identity, bias=ms[:, n:n + 1],
                                               scale=rs[:, n:n + 1])
                ins.then_inc(s_xsC.sem, 1)

            def act_c(c, u, turn):
                act.wait_ge(s_mmC.sem, s_mmC.done(c, 3))
                act.wait_ge(s_yC.sem, s_yC.freed(c))
                nc.scalar.activation(rg[:, u, :], ps[:, 1 + 3 * u + 2, :], ACT.Sigmoid).then_inc(s_sig.sem, 1)

            pads = [(Fixed(prep_pool), lambda c: 2)]

            def first_tap(c, u, turn):
                act.wait_ge(s_xT.sem, s_xT.done(TR0["D"] + c))
                act.wait_ge(s_mmD.sem, s_mmD.freed(c))
                nc.scalar.activation(hc[:, u, :].rearrange("p (s t) -> p s t", s=SPC), hp[:, u, :, 2:T + 2],
                                     ACT.Copy, scale=par("conv2")).then_inc(s_tap.sem, 1)

            def split(c, u, turn):
                s_st.wait_freed(act, u, turn)
                for n in range(2):
                    act.wait_ge(s_full.sem, s_full.done(c, n + 1))
                    nc.scalar.copy(kq[:, u, n, 0, :], full[:, n, :]).then_inc(s_hi.sem, 1)
                for n in range(2):
                    act.wait_ge(s_rem.sem, s_rem.done(c, n + 1))
                    nc.scalar.copy(kq[:, u, n, 1, :], rem[:, n, :]).then_inc(s_hi.sem, 1)

            def keep(stage):
                def part(c, u, turn):
                    act.wait_ge(*scaled(stage, c))
                    f = r1 if stage == "D" else rp1
                    for n in range(c * TPC + TPC // 2, (c + 1) * TPC):
                        ins = nc.scalar.activation(XRES[:, n, :], X[:, n, :], ACT.Identity, bias=mr[:, n:n + 1],
                                                   scale=f[:, n:n + 1])
                    ins.then_inc(s_res2.sem, 1)
                return part

            def copy_values(c, u, turn):
                act.wait_ge(s_mmD.sem, s_mmD.done(c, 5))
                nc.scalar.copy(V[:, ds(c * TPC, TPC), :], ps[:, 5, :].rearrange("p (t c) -> p t c", t=TPC))\
                    .then_inc(s_v.sem, 1)

            dense([("A", 0, copy_turned("A", [(s_mmA, s_mmA.freed)])), ("A", 1, act_a), ("A", 0, keep("A")),
                   ("B", 0, copy_turned("B", [(s_out, out_b)])), ("B", 0, constants),
                   ("C", 0, scale_c), ("C", 2, act_c),
                   ("C", 0, scale_turned("C", hp, "ln_w", "ln_b", pads + [(s_mix, s_mix.freed)])),
                   ("C", 0, keep("C")),
                   ("D", 1, first_tap), ("D", 3, split), ("D", 2, copy_values),
                   ("D", 0, scale_turned("D", hp, "ln1_w", "ln1_b",
                                         [(s_conv, s_conv.freed), (Fixed(s_mix.sem), lambda c: s_mix.done(NCH - 1))])),
                   ("D", 0, keep("D"))])

            def attend(s, at, live):
                if not live(2):
                    return
                b, u, turn = at(2)
                for g in range(NG):
                    act.wait_ge(s_ST.sem, s_ST.done(b, g + 1))
                    act.wait_ge(s_pv.sem, s_pv.done(b, g - 1))
                    nc.scalar.activation(Pt[:, g % 2, :].rearrange("p (k n) -> p k n", k=2),
                                         ps[:, 2 + 2 * (g % 2):4 + 2 * (g % 2), :], ACT.Exp,
                                         scale=SCALE).then_inc(s_exp.sem, 1)
                    if g in (3, 5):
                        half = 0 if g == 3 else 1
                        act.wait_ge(s_pv.sem, s_pv.done(b, 3 * half + 3))
                        act.wait_ge(s_yT.sem, s_yT.done(b, half - 1))
                        nc.scalar.copy(yr[:, half, :], ps[:, 6, :]).then_inc(s_yr.sem, 1)

            run_steps(act, B, attend, 2)
            out_f = lambda c: s_out.freed(NEW0["F"] + c)

            def scale_g(c, u, turn):
                act.wait_ge(s_turnG.sem, s_turnG.done(c))
                act.wait_ge(s_rt.sem, s_rt.freed(c))
                nc.scalar.activation(xTg[:, u, :], ps[:, 1 + 2 * u, :], ACT.Identity, bias=par("ln2_b"),
                                     scale=par("ln2_w")).then_inc(s_xTG.sem, 1)

            def take_logits(c, u, turn):
                act.wait_ge(s_rt.sem, s_rt.done(c))
                nc.scalar.copy(logits[:, c * TPC:(c + 1) * TPC, :],
                               ps[:, 2, 0:TPC * E].rearrange("p (t e) -> p t e", t=TPC)).then_inc(s_lg.sem, 1)

            dense([("G", 1, take_logits), ("F", 0, copy_turned("F", [(s_out, out_f)])), ("G", 0, scale_g)])

            def block_in_(k, u, turn):
                act.wait_ge(s_bT.sem, s_bT.done(k))
                act.wait_ge(s_up.sem, s_up.freed(k))
                nc.scalar.activation(hT[:, u, :], ps[:, 0, 0:P], ACT.Identity, bias=par("ln2_b"),
                                     scale=par("ln2_w")).then_inc(s_hT.sem, 1)

            def block_silu(k, u, turn):
                act.wait_ge(s_up.sem, s_up.done(k))
                act.wait_ge(s_glu.sem, s_glu.freed(k))
                nc.scalar.activation(sg[:, u, :], ps[:, 1 + u, :], ACT.Silu).then_inc(s_silu.sem, 1)

            def block_turned(k, u, turn):
                act.wait_ge(s_gT.sem, s_gT.done(k))
                act.wait_ge(s_dn.sem, s_dn.freed(k))
                nc.scalar.copy(gT[:, u, :], ps[:, 5, :]).then_inc(s_gTc.sem, 1)

            in_turn(act, NB, [(3, block_turned), (1, block_silu), (0, block_in_)])

        @block.vector
        def _(dve):
            for s in (s_xs, s_new, s_uu, s_y, s_mix, s_kvC, s_conv, s_rot, s_rem, s_max,
                      s_mp, s_rden, s_yn, s_glu, s_yc):
                s.start(dve)

            def tiles(c, j):
                return ds(c * TPC + j, 1)

            def take_stats(src, c):
                for j in range(TPC):
                    dve.bn_stats(bn[:, tiles(c, j), :].rearrange("p o s -> p (o s)"),
                                 src[:, tiles(c, j), :].rearrange("p o c -> p (o c)"))

            links = [0]

            def link(*made):
                links[0] += 1
                made[-1].then_inc(stat_v, 1)
                dve.wait_ge(stat_v, links[0])

            def factors(stage, part):
                n0 = links[0]
                t = slice(part * NT // 2, (part + 1) * NT // 2)
                n = 2 if stage in TWICE else 1
                eps2 = RMS_EPS if stage == "A" else LN_EPS
                v, r, w = tv[:, 0:n, t], rsq[:, 0:n, t], nt[:, 0:n, t]
                dve.drain()
                link(dve.tensor_tensor(mean[:, t], bn[:, t, 1], bn[:, t, 4], ALU.add),
                     dve.tensor_tensor(half[:, t], bn[:, t, 1], bn[:, t, 4], ALU.subtract),
                     dve.tensor_tensor(var[:, t], bn[:, t, 2], bn[:, t, 5], ALU.add))
                link(dve.tensor_scalar(mean[:, t], mean[:, t], 0.5, None, ALU.mult),
                     dve.scalar_tensor_tensor(out=half[:, t], in0=half[:, t], scalar=0.25, in1=half[:, t],
                                              op0=ALU.mult, op1=ALU.mult))
                link(dve.scalar_tensor_tensor(out=var[:, t], in0=var[:, t], scalar=1.0 / C, in1=half[:, t],
                                              op0=ALU.mult, op1=ALU.add))
                made = [dve.tensor_scalar(tv[:, 0, t], var[:, t], LN_EPS, None, ALU.add)]
                if n == 2:
                    made.append(dve.tensor_scalar(tv[:, 1, t], var[:, t], 1.0 + eps2, LN_EPS * eps2,
                                                  ALU.mult, ALU.add))
                link(*made)
                link(dve.tensor_scalar(r.bitcast(I32), v.bitcast(I32), -0.5, float(0x5F3759DF), ALU.mult, ALU.add))
                for _ in range(3):
                    link(dve.scalar_tensor_tensor(out=w, in0=r, scalar=-0.5, in1=v, op0=ALU.mult, op1=ALU.mult))
                    link(dve.tensor_tensor(w, w, r, ALU.mult))
                    link(dve.scalar_tensor_tensor(out=r, in0=w, scalar=1.5, in1=r, op0=ALU.add, op1=ALU.mult))
                if stage in "ACD":
                    link(dve.tensor_scalar(rp1[:, t], r1[:, t], 1.0, None, ALU.add),
                         dve.scalar_tensor_tensor(out=ms[:, t], in0=mean[:, t], scalar=-1.0, in1=rs[:, t],
                                                  op0=ALU.mult, op1=ALU.mult),
                         dve.scalar_tensor_tensor(out=mr[:, t], in0=mean[:, t], scalar=-1.0, in1=r1[:, t],
                                                  op0=ALU.mult, op1=ALU.mult))
                assert links[0] - n0 == FACTORS[stage]

            def scale_inputs(stage):
                f = rs if stage in TWICE else r1

                def part(c, u, turn):
                    if stage != "G":
                        dve.wait_ge(s_tr.sem, s_tr.freed(TR0[stage] + c))
                    for j in range(TPC):
                        x = source[stage][:, tiles(c, j), :].rearrange("p o c -> p (o c)")
                        to = HN[:, c * TPC + j, :] if stage == "G" else xs[:, u, j, :]
                        ins = dve.tensor_scalar(to, x, mean[:, tiles(c, j)],
                                                f[:, tiles(c, j)], ALU.subtract, ALU.mult)
                    ins.then_inc(s_xs.sem, 1)
                return part

            def add_product(stage):
                k0 = NEW0[stage]
                to = XA if stage == "F" else X

                def part(c, u, turn):
                    dve.wait_ge(s_out.sem, s_out.done(k0 + c))
                    kept = X if stage == "B" else XRES
                    if stage != "B":
                        dve.wait_ge(s_res.sem, s_res.done(RES0[stage] + c))
                        dve.wait_ge(s_res2.sem, s_res2.done(RES0[stage] + c))
                    dve.tensor_tensor(to[:, ds(c * TPC, TPC), :], ps[:, out_bank(stage, u), :].rearrange("p (t c) -> p t c", t=TPC),
                                      kept[:, ds(c * TPC, TPC), :], ALU.add).then_inc(s_new.sem, 1)
                    dve.drain()
                    take_stats(to, c)
                    if (c + 1) % (NCH // 2) == 0:
                        factors({"A": "B", "B": "C", "C": "D", "F": "G"}[stage], c // (NCH // 2))
                return part

            def take_inputs(c):
                dve.wait_ge(ld_x[c], 16)
                take_stats(X, c)
                if (c + 1) % (NCH // 2) == 0:
                    factors("A", c // (NCH // 2))

            def second_half(c, u, turn):
                if c < NCH // 2:
                    take_inputs(c + NCH // 2)

            for c in range(NCH // 2):
                take_inputs(c)

            def fold_weights(c, u, turn):
                if c > 0:
                    return
                dve.wait_ge(ld_w, 16 * N_W)
                dve.wait_ge(prep_act, 3)
                dve.wait_ge(prep_pool, 1)
                dve.tensor_scalar(W_in[:], W_in[:], par("w_norm"), None, ALU.mult).then_inc(prep, 1)
                dve.tensor_scalar(lam[:, 1:2], lam[:, 0:1], -0.5, -0.5, ALU.mult, ALU.add).then_inc(prep, 1)
                dve.tensor_scalar(dec[:, 1:2], dec[:, 0:1], 0.5, 0.5, ALU.mult, ALU.add).then_inc(prep, 1)
                dve.wait_ge(prep, 3)
                dve.tensor_scalar(W_out[:], W_out[:], lam[:, 1:2], None, ALU.mult).then_inc(prep, 1)
                dve.tensor_scalar(decay_row[:], ones[:], dec[:, 1:2], None, ALU.mult).then_inc(prep, 1)
                dve.tensor_tensor(W_ffn[:], W_ffn[:], DISHA[:], ALU.add).then_inc(prep, 1)
                dve.tensor_copy(ident_b[:], ident[:]).then_inc(prep, 1)

            def recur(c, u, turn):
                dve.wait_ge(s_rv.sem, s_rv.done(c))
                dve.wait_ge(s_y.sem, s_y.freed(c))
                dve.scalar_tensor_tensor(out=uu[:, u, :], in0=ga[:, u, :], scalar=-1.0, in1=rv[:, u, :],
                                         op0=ALU.add, op1=ALU.mult).then_inc(s_uu.sem, 1)
                dve.wait_ge(s_uu.sem, s_uu.done(c))
                dve.wait_ge(s_out.sem, s_out.freed(NEW0["A"] + c))
                for s in range(SPC):
                    t = slice(s * T, (s + 1) * T)
                    ins = dve.tensor_tensor_scan(y[:, u, t], ga[:, u, t], uu[:, u, t], 0.0, ALU.mult, ALU.add)
                ins.then_inc(s_y.sem, 1)

            def mixes(c, u, turn):
                dve.wait_ge(s_dif.sem, s_dif.done(c))
                dve.wait_ge(s_mmC.sem, s_mmC.freed(c))
                for n, name in enumerate(("mix_k", "mix_v", "mix_r")):
                    dve.scalar_tensor_tensor(
                        out=mix[:, u, n, :].rearrange("p (s t) -> p s t", s=SPC),
                        in0=dif[:, u, :].rearrange("p (s t) -> p s t", s=SPC), scalar=par(name),
                        in1=hp[:, u, :, 1:T + 1], op0=ALU.mult, op1=ALU.add).then_inc(s_mix.sem, 1)

            def states(c, u, turn):
                K, Vb = ps[:, 1 + 3 * u, :], ps[:, 2 + 3 * u, :]
                dve.wait_ge(s_mmC.sem, s_mmC.done(c, 2))
                dve.wait_ge(s_yC.sem, s_yC.freed(c))
                for s in range(SPC):
                    t = slice(s * T, (s + 1) * T)
                    ins = dve.tensor_tensor_scan(sk[:, u, t], decay_row[:], K[:, t], 0.0, ALU.mult, ALU.add)
                ins.then_inc(s_kvC.sem, 1)
                dve.wait_ge(s_kvC.sem, s_kvC.done(c, 1))
                dve.scalar_tensor_tensor(out=sk[:, u, :], in0=sk[:, u, :], scalar=first[:], in1=K,
                                         op0=ALU.mult, op1=ALU.add).then_inc(s_kvC.sem, 1)
                dve.wait_ge(s_kvC.sem, s_kvC.done(c, 2))
                dve.tensor_tensor(sk[:, u, :], sk[:, u, :], Vb, ALU.mult).then_inc(s_kvC.sem, 1)

            def convolve(c, u, turn):
                dve.wait_ge(s_tap.sem, s_tap.done(c))
                o = hc[:, u, :].rearrange("p (s t) -> p s t", s=SPC)
                for k, name in ((1, "conv1"), (0, "conv0")):
                    if k == 0:
                        dve.wait_ge(s_conv.sem, s_conv.done(c, 1))
                    dve.scalar_tensor_tensor(out=o, in0=hp[:, u, :, k:k + T], scalar=par(name), in1=o,
                                             op0=ALU.mult, op1=ALU.add).then_inc(s_conv.sem, 1)

            def rotations(c, u, turn):
                for n in range(2):
                    for k in range(2):
                        dve.wait_ge(s_mmD.sem, s_mmD.done(c, 2 * n + k + 1))
                        dve.wait_ge(s_full.sem, s_full.done(c, n - 1))
                        dve.tensor_tensor(
                            rot[:, n, k, :].rearrange("p (s t) -> p s t", s=SPC),
                            ps[:, 1 + 2 * n + k, :].rearrange("p (s t) -> p s t", s=SPC),
                            rope[:, k:k + 1, :].to_broadcast([P, SPC, T]), ALU.mult).then_inc(s_rot.sem, 1)

            def remainder(n):
                def part(c, u, turn):
                    dve.wait_ge(s_hi.sem, s_hi.done(c, n + 1))
                    dve.wait_ge(s_lo.sem, s_lo.done(c - 1, n + 1))
                    dve.tensor_tensor(rem[:, n, :], full[:, n, :], kq[:, u, n, 0, :], ALU.subtract)\
                        .then_inc(s_rem.sem, 1)
                return part

            dense([("A", 0, scale_inputs("A")), ("A", 1, fold_weights), ("A", 2, recur), ("A", 3, add_product("A")), ("A", 0, second_half),
                   ("B", 3, add_product("B")), ("B", 0, scale_inputs("B")),
                   ("C", 2, mixes), ("C", 3, states), ("C", 4, add_product("C")),
                   ("D", 2, convolve), ("D", 3, rotations), ("D", 3, remainder(0)), ("D", 0, scale_inputs("D")),
                   ("D", 3, remainder(1))])

            def maximum(b, u, n):
                dve.wait_ge(s_S.sem, s_S.done(b, n + 1))
                if n == 0:
                    dve.wait_ge(s_mT.sem, s_mT.freed(b))
                if n < 4:
                    to, src = M[:, u, 0, 4 * n:4 * n + 4], ps[:, n % 2, :].rearrange("p (h k) -> p h k", h=4)
                else:
                    h = 2 * (n - 4)
                    to, src = M[:, u, 1, h:h + 2], ps[:, n % 2, :].rearrange("p (h k) -> p h k", h=2)
                dve.tensor_reduce(to, src, AX_X, ALU.max).then_inc(s_max.sem, 1)

            def normalise(b, half):
                u = half
                dve.wait_ge(s_yT.sem, s_yT.done(b, half + 1))
                o = ps[:, 7, :].rearrange("p (g q j c) -> p g q j c", g=2, q=2, j=4)
                dve.reciprocal(rden[:, u], o[:, :, :, :, D]).then_inc(s_rden.sem, 1)
                dve.wait_ge(s_rden.sem, s_rden.done(b, half + 1))
                for q in range(2):
                    to = Y[:, ds(b * 2 + q, 1), half * 64:half * 64 + 64]
                    ins = dve.tensor_tensor(
                        to.rearrange("p o (g j d) -> p (o g) j d", g=2, j=4), o[:, :, q, :, 0:D],
                        rden[:, u, :, q, :].rearrange("p g (j d) -> p g j d", d=1).to_broadcast([P, 2, 4, D]),
                        ALU.mult)
                ins.then_inc(s_yn.sem, 1)

            def minus_max(b, u, turn):
                dve.wait_ge(s_mT.sem, s_mT.done(b))
                s_mrow.wait_freed(dve, u, turn)
                dve.tensor_scalar(mp[:, u, 0, :], ps[0:H, 7, 0:T], -1.0, None, ALU.mult).then_inc(s_mp.sem, 1)
                dve.wait_ge(s_mp.sem, s_mp.done(b, 1))
                dve.scalar_tensor_tensor(out=mp[:, u, 1, :], in0=ps[0:H, 7, 0:T], scalar=-1.0,
                                         in1=mp[:, u, 0, :], op0=ALU.mult, op1=ALU.subtract)\
                    .then_inc(s_mp.sem, 1)

            def attend(s, at, live):
                for n in range(NS):
                    if live(0):
                        b, u, _ = at(0)
                        maximum(b, u % 2, n)
                    if n == 1 and live(1):
                        minus_max(*at(1))
                    if n == 5 and live(3):
                        normalise(at(3)[0], 1)
                    if n == 9 and live(2):
                        normalise(at(2)[0], 0)

            run_steps(dve, B, attend, 3, LANES)

            def route(c, u, turn):
                if (c + 1) % (NCH // GROUPS_G):
                    return
                g = c // (NCH // GROUPS_G)
                t = slice(g * GT, (g + 1) * GT)
                k = slice(g * GB, (g + 1) * GB)
                wide = lambda a: a.rearrange("p (t e) -> p t e", e=1).to_broadcast([P, GT, E])
                over = lambda a: a.rearrange("p (t e) -> p t e", t=1).to_broadcast([P, GT, E])

                def link(*made):
                    routes[0] += 1
                    made[-1].then_inc(route_v, 1)
                    dve.wait_ge(route_v, routes[0])

                dve.wait_ge(s_lg.sem, s_lg.done(c))
                link(dve.tensor_reduce(lmax[:, t], logits[:, t, :], AX_X, ALU.max))
                link(dve.tensor_tensor(pk[:, t, :], logits[:, t, :], wide(lmax[:, t]), ALU.is_equal))
                link(dve.tensor_tensor(pk[:, t, :], pk[:, t, :], over(pick[:]), ALU.mult))
                link(dve.tensor_reduce(smax[:, t], pk[:, t, :], AX_X, ALU.max))
                link(dve.tensor_tensor(oh[:, t, :], pk[:, t, :], wide(smax[:, t]), ALU.is_equal))
                link(dve.tensor_copy(oh_b[:, t, :], oh[:, t, :]))
                assert routes[0] == ONE_HOT[g]
                dve.wait_ge(s_cnt, g + 1)
                tile_n = ps[:, 5 + 2 * g, 0:GT * E].rearrange("p (t e) -> p t e", t=GT)
                link(*(dve.tensor_tensor_scan(cum[:, e, :], ones[:, 0:GT], tile_n[:, :, e], 0.0, ALU.mult, ALU.add)
                       for e in range(E)))
                link(dve.tensor_scalar(padded_i, cum[:, :, GT - 1], float(P - 1), None, ALU.add))
                shift = P.bit_length() - 1
                link(dve.tensor_scalar(padded_i, padded_i, shift, shift, ALU.logical_shift_right,
                                       ALU.logical_shift_left))
                link(dve.tensor_copy(padded, padded_i))
                link(dve.tensor_tensor_scan(ends, ones[:, 0:E], padded, 0.0, ALU.mult, ALU.add))
                link(dve.tensor_tensor(starts, ends, padded, ALU.subtract),
                     dve.tensor_tensor(at4[:, t, :], cum[:].rearrange("p e t -> p t e"), tile_n, ALU.subtract))
                link(dve.tensor_tensor(at4[:, t, :], at4[:, t, :],
                                       ps[:, 4 + 2 * g, 0:GT * E].rearrange("p (t e) -> p t e", t=GT), ALU.add))
                link(dve.tensor_tensor(at4[:, t, :], at4[:, t, :], over(starts), ALU.add))
                link(dve.tensor_tensor(at4[:, t, :], at4[:, t, :], oh[:, t, :], ALU.mult))
                link(dve.tensor_reduce(posf[:, t], at4[:, t, :], AX_X, ALU.add))
                link(dve.tensor_copy(pos[:, t], posf[:, t]))
                assert routes[0] == ROUTED[g]
                link(dve.tensor_scalar(expf[:, k], block_at[:], starts[:, 1:2], None, ALU.is_ge))
                for e in range(2, E):
                    link(dve.scalar_tensor_tensor(out=expf[:, k], in0=block_at[:], scalar=starts[:, e:e + 1],
                                                  in1=expf[:, k], op0=ALU.is_ge, op1=ALU.add))
                link(dve.tensor_scalar(exp_i[:, k], expf[:, k], float(FF), None, ALU.mult))

            routes = [0]
            dense([("G", 1, route), ("F", 2, add_product("F")), ("G", -1, scale_inputs("G"))])

            def block_glu(k, u, turn):
                dve.wait_ge(s_silu.sem, s_silu.done(k))
                dve.wait_ge(s_gT.sem, s_gT.freed(k))
                dve.tensor_tensor(glu[:, u % 2, :], sg[:, u % 2, :], ps[:, 3 + u % 2, :], ALU.mult)\
                    .then_inc(s_glu.sem, 1)

            def block_out(k, u, turn):
                s_lres.wait_done(dve, u, turn)
                if not isinstance(k, int) or k >= LANES:
                    dve.wait_ge(outputs[u], 16 * turn)
                dve.tensor_scalar(row[:, u:u + 1], res[:, u, C:C + 1], -1.0, float(TOK), ALU.mult, ALU.add)
                dve.wait_ge(s_dn.sem, s_dn.done(k))
                dve.tensor_tensor(yo[:, u, :], res[:, u, 0:C], ps[:, 6 + u % 2, 0:C], ALU.add).then_inc(s_yc.sem, 1)

            in_turn(dve, NB, [(1, block_glu), (3, block_out)], LANES, peel=2)

        @block.tensor
        def _(pe):
            for s in (s_tr, s_out, s_mmA, s_mmC, s_mmD, s_S, s_mT, s_ST, s_pv, s_yT, s_turnG, s_rt, s_bT, s_up,
                      s_gT, s_dn):
                s.start(pe)

            def turn(stage):
                def part(c, u, turn_):
                    pe.wait_ge(s_xT.sem, s_xT.done(TR0[stage] + c - 1))
                    if stage == "F":
                        pe.wait_ge(s_yn.sem, s_yn.done(B - 1))
                    else:
                        pe.wait_ge(*scaled(stage, c))
                    for j in range(TPC):
                        src = Y[:, c * TPC + j, :] if stage == "F" else xs[:, u, j, :]
                        ins = pe.transpose(ps[:, 0, j * P:(j + 1) * P], src, ident[:])
                    ins.then_inc(s_tr.sem, 1)
                return part

            def product(stage, a, w, ready):
                k0 = NEW0[stage]

                def part(c, u, turn_):
                    ready(c)
                    pe.wait_ge(s_new.sem, s_new.freed(k0 + c) if stage in "BF" and c > 0 else s_new.done(k0 + c - 1))
                    for j in range(TPC):
                        ins = pe.matmul(ps[:, out_bank(stage, u), j * C:(j + 1) * C], a[:, u, j * P:(j + 1) * P], w[:],
                                        start=(j == 0), stop=True, skip_group_check=True)
                    ins.then_inc(s_out.sem, 1)
                return part

            pe.wait_ge(ld_w, 16 * N_W)

            def project_a(c, u, turn_):
                if c == 0:
                    pe.wait_ge(prep, 7)
                pe.wait_ge(s_xT.sem, s_xT.done(TR0["A"] + c))
                pe.wait_ge(s_actA.sem, s_actA.freed(c))
                for n in range(3):
                    pe.matmul(ps[:, 1 + 3 * u + n, :], W_in[:, n * C:(n + 1) * C], xT[:, u, :],
                              start=True, stop=True).then_inc(s_mmA.sem, 1)

            def project_c(c, u, turn_):
                pe.wait_ge(s_kvC.sem, s_kvC.freed(c))
                pe.wait_ge(s_sig.sem, s_sig.freed(c))
                if c == 1:
                    pe.wait_ge(s_new.sem, s_new.done(NEW0["B"] + NCH - 1))
                for n in range(3):
                    pe.wait_ge(s_mix.sem, s_mix.done(c, n + 1))
                    pe.matmul(ps[:, 1 + 3 * u + n, :], W_kvr[:, n * C:(n + 1) * C], mix[:, u, n, :],
                              start=True, stop=True).then_inc(s_mmC.sem, 1)

            def project_d(c, u, turn_):
                pe.wait_ge(s_conv.sem, s_conv.done(c))
                if c == 0:
                    pe.wait_ge(s_kvC.sem, s_kvC.done(NCH - 1))
                for n in range(4):
                    pe.wait_ge(s_rot.sem, s_rot.done(c - 1, n + 1))
                    pe.matmul(ps[:, 1 + n, :], W_qk[:, n * C:(n + 1) * C], hc[:, u, :],
                              start=True, stop=True).then_inc(s_mmD.sem, 1)
                pe.wait_ge(s_v.sem, s_v.done(c - 1))
                for j in range(TPC):
                    ins = pe.matmul(ps[:, 5, j * C:(j + 1) * C], hc[:, u, j * P:(j + 1) * P], W_v[:],
                                    start=(j == 0), stop=True, skip_group_check=True)
                ins.then_inc(s_mmD.sem, 1)

            def weights_there(c, u, turn_):
                if c == 0:
                    pe.wait_ge(ld_w2, 16 * N_W2)

            dense([("A", 3, product("A", y, W_out, lambda c: pe.wait_ge(s_y.sem, s_y.done(c)))),
                   ("A", 0, turn("A")), ("A", 1, project_a),
                   ("B", 2, product("B", xT, W_ffn, lambda c: pe.wait_ge(s_xT.sem, s_xT.done(TR0["B"] + c)))),
                   ("B", 0, turn("B")), ("C", 0, weights_there),
                   ("C", 4, product("C", y, W_o, lambda c: pe.wait_ge(s_yC.sem, s_yC.done(c)))),
                   ("C", 2, project_c), ("C", 0, turn("C")), ("D", 2, project_d), ("D", 0, turn("D"))])
            pe.wait_ge(prep_act, 10)
            pe.wait_ge(s_rot.sem, s_rot.done(NCH - 1))
            pe.wait_ge(s_v.sem, s_v.done(NCH - 1))

            def scores(b, lane, n):
                pe.wait_ge(s_max.sem, s_max.done(b, n - 1))
                bank = ps[:, n % 2, :]
                if n < 4:
                    pe.matmul(bank, ident_b[:], masks_b[:, 0].rearrange("p k c -> p (k c)"), start=True, stop=False,
                              skip_group_check=True)
                    for k in range(4):
                        ins = pe.matmul(bank[:, k * P:(k + 1) * P], QS[0:MAX_ROW, lane, 4 * n + k, 0:P],
                                        KS[0:MAX_ROW, lane, 4 * n + k, 0:P], start=False, stop=True,
                                        skip_group_check=True)
                else:
                    h = 2 * (n - 4)
                    pe.matmul(bank.rearrange("p (h k c) -> p h k c", h=2, k=2)[:, :, 1, :], ident_b[:],
                              masks_b[:, 0, 0:2, :], start=True, stop=False, skip_group_check=True)
                    for k in range(2):
                        ins = pe.matmul(bank[:, k * T:(k + 1) * T], QS[0:MAX_ROW, lane, h + k, P:T],
                                        KS[0:MAX_ROW, lane, h + k, :], start=False, stop=True,
                                        skip_group_check=True)
                ins.then_inc(s_S.sem, 1)

            def turned_scores(b, lane, g):
                kb, h0, nh = GROUPS[g]
                pe.wait_ge(s_exp.sem, s_exp.done(b, g - 1))
                for half in range(2):
                    bank = ps[:, 2 + 2 * (g % 2) + half, :]
                    if kb == 0:
                        pe.matmul(bank.rearrange("p (h k c) -> p h k c", h=2, k=2)[:, :, 0, :], ident_b[:],
                                  masks_b[:, 1, 0:2, :], start=True, stop=False, skip_group_check=True)
                    else:
                        pe.matmul(bank, ident_b[:], masks_b[:, 1].rearrange("p k c -> p (k c)"), start=True,
                                  stop=False, skip_group_check=True)
                    w = T - kb * P
                    for k in range(nh // 2):
                        h = h0 + half * nh // 2 + k
                        ins = pe.matmul(bank[:, k * w:(k + 1) * w], KS[:, lane, h, kb * P:(kb + 1) * P],
                                        QS[:, lane, h, kb * P:T], start=False, stop=True, skip_group_check=True)
                ins.then_inc(s_ST.sem, 1)

            def weigh(b, u, g):
                kb, h0, nh = GROUPS[g]
                pe.wait_ge(s_exp.sem, s_exp.done(b, g + 1))
                if g in (0, 3):
                    pe.wait_ge(s_yr.sem, s_yr.done(b, g // 3))
                w = T - kb * P
                for k in range(nh):
                    h = h0 + k
                    j, q = h % 4, h // 4 % 2
                    ins = pe.matmul(ps[32 * j:32 * j + 32, 6, q * T + kb * P:(q + 1) * T], Vx[:, u, kb, h, :],
                                    Pt[:, g % 2, k * w:(k + 1) * w], start=(g % 3 == 0), stop=(kb == 1),
                                    skip_group_check=True)
                ins.then_inc(s_pv.sem, 1)

            def turn_outputs(b, half):
                pe.wait_ge(s_yn.sem, s_yn.done(b, half))
                pe.wait_ge(s_yr.sem, s_yr.done(b, half + 1))
                for k in range(4):
                    ins = pe.transpose(ps[:, 7, k * P:(k + 1) * P], yr[:, half, k * P:(k + 1) * P], ident[:])
                ins.then_inc(s_yT.sem, 1)

            def turn_maxima(b, u):
                pe.wait_ge(s_max.sem, s_max.done(b))
                for q in range(2):
                    ins = pe.transpose(ps[0:H, 7, q * P:(q + 1) * P], M[:, u, q, :], ident[:])
                ins.then_inc(s_mT.sem, 1)

            def attend(s, at, live):
                if live(0):
                    b0, lane0, turn0 = at(0)
                    s_ldst.wait_done(pe, lane0, turn0)
                if live(2):
                    b2, lane2, turn2 = at(2)
                    pe.wait_ge(s_vx.sem, s_vx.done(b2))
                    s_mrow.wait_done(pe, lane2, turn2)
                for g in range(NG):
                    if live(0):
                        scores(b0, lane0, 2 * g)
                    if live(2):
                        turned_scores(b2, lane2, g)
                    if live(0):
                        scores(b0, lane0, 2 * g + 1)
                    if live(2) and g > 0:
                        weigh(b2, lane2 % 2, g - 1)
                    if g == 0 and live(1):
                        if live(3):
                            pe.wait_ge(s_yn.sem, s_yn.done(at(3)[0], 1))
                        turn_maxima(at(1)[0], at(1)[1] % 2)
                    if g == 2 and live(3):
                        pe.wait_ge(s_mp.sem, s_mp.done(at(1)[0] if live(1) else B - 1))
                        turn_outputs(at(3)[0], 1)
                    if g == 4 and live(2):
                        pe.wait_ge(s_mp.sem, s_mp.done(at(1)[0] if live(1) else B - 1))
                        turn_outputs(b2, 0)
                if live(2):
                    weigh(b2, lane2 % 2, NG - 1)

            run_steps(pe, B, attend, 3, LANES)

            def turn_g(c, u, turn_):
                pe.wait_ge(s_xTG.sem, s_xTG.freed(c))
                pe.wait_ge(s_xs.sem, s_xs.done(XS0["G"] + c))
                for j in range(TPC):
                    ins = pe.transpose(ps[:, 1 + 2 * u, j * P:(j + 1) * P], HN[:, c * TPC + j, :], ident[:])
                ins.then_inc(s_turnG.sem, 1)

            def logits_g(c, u, turn_):
                pe.wait_ge(s_xTG.sem, s_xTG.done(c))
                pe.wait_ge(s_lg.sem, s_lg.done(c - 1))
                for j in range(TPC):
                    ins = pe.matmul(ps[:, 2, j * E:(j + 1) * E], xTg[:, u, j * P:(j + 1) * P], W_router[:],
                                    start=(j == 0), stop=True, skip_group_check=True)
                ins.then_inc(s_rt.sem, 1)

            def count_g(c, u, turn_):
                if (c + 1) % (NCH // GROUPS_G):
                    return
                g = c // (NCH // GROUPS_G)
                pe.wait_ge(route_v, ONE_HOT[g])
                o = oh_b[:, g * GT:(g + 1) * GT, :].rearrange("p t e -> p (t e)")
                pe.matmul(ps[:, 4 + 2 * g, 0:GT * E], before_b[:], o, start=True, stop=True)
                pe.matmul(ps[:, 5 + 2 * g, 0:GT * E], ones_b[:], o, start=True, stop=True).then_inc(s_cnt, 1)

            dense([("G", 1, logits_g),
                   ("F", 1, product("F", xT, W_proj, lambda c: pe.wait_ge(s_xT.sem, s_xT.done(TR0["F"] + c)))),
                   ("F", 0, turn("F")), ("G", 1, count_g), ("G", 0, turn_g)])

            pe.wait_ge(ld_e, 32)
            pe.wait_ge(route_v, ROUTED[0] + E)

            def block_turn(k, u, turn_):
                s_hs.wait_done(pe, u, turn_)
                pe.wait_ge(s_hT.sem, s_hT.done(k - 1))
                pe.transpose(ps[:, 0, 0:P], hs[:, u, :], ident[:]).then_inc(s_bT.sem, 1)

            def block_up(k, u, turn_, e):
                pe.wait_ge(s_hT.sem, s_hT.done(k))
                pe.wait_ge(s_glu.sem, s_glu.freed(k))
                for n in range(2):
                    ins = pe.matmul(ps[:, 1 + 2 * n + u % 2, :], hT[:, u % 2, :], W_up[:, ds(e * 2 + n * FF, FF)],
                                    start=True, stop=True)
                ins.then_inc(s_up.sem, 1)

            def block_back(k, u, turn_):
                pe.wait_ge(s_glu.sem, s_glu.done(k))
                pe.wait_ge(s_gTc.sem, s_gTc.done(k - 1))
                for f in range(FB):
                    ins = pe.transpose(ps[:, 5, f * P:(f + 1) * P], glu[:, u % 2, f * P:(f + 1) * P], ident[:])
                ins.then_inc(s_gT.sem, 1)

            def block_down(k, u, turn_, e):
                pe.wait_ge(s_gTc.sem, s_gTc.done(k))
                pe.wait_ge(s_yc.sem, s_yc.freed(k))
                for f in range(FB):
                    ins = pe.matmul(ps[:, 6 + u % 2, 0:C], gT[:, u % 2, f * P:(f + 1) * P],
                                    W_down[:, ds(e + f * C, C)], start=(f == 0), stop=(f == FB - 1))
                ins.then_inc(s_dn.sem, 1)

            def blocks(s, at, live):
                def expert(l):
                    return pe.value_load(exp_i[0:1, ds(at(l)[0], 1)], min_val=0, max_val=(E - 1) * FF)

                if isinstance(s, int) and s == 3:
                    pe.wait_ge(route_v, ROUTED[-1] + E)
                if live(3):
                    block_back(*at(3))
                if live(1):
                    block_up(*at(1), expert(1))
                if live(3):
                    block_down(*at(3), expert(3))
                if live(0):
                    block_turn(*at(0))

            run_steps(pe, NB, blocks, 3, LANES)


_OUTS = [((B, T, C), "float32")]


def kernel(**inputs):
    import numpy as np
    import concourse.bacc as bacc
    from concourse.bass_utils import run_bass_kernel_spmd as run

    g = {k: np.asarray(v) for k, v in inputs.items()}
    L1 = "L1_attn_"
    F = "L1_ffn_"
    turned = np.arange(C).reshape(H, 2, D // 2)[:, ::-1].reshape(-1)
    wq, wk, wv = (g[F + "attn_w"][:, k * C:(k + 1) * C] for k in range(3))
    columns = [g["L0_attn_w_norm"], g["L0_attn_lambda_log"], g[L1 + "time_mix_k"], g[L1 + "time_mix_v"],
               g[L1 + "time_mix_r"], g[L1 + "time_decay"], g[L1 + "time_first"], g[L1 + "ln_w"], g[L1 + "ln_b"],
               g[F + "ln1_w"], g[F + "ln1_b"], g[F + "ln2_w"], g[F + "ln2_b"],
               g[F + "conv_w"][:, 0, 0], g[F + "conv_w"][:, 0, 1], g[F + "conv_w"][:, 0, 2]]
    freq = (1.0 / np.float32(10000.0) ** (np.arange(0, D, 2, dtype=np.float32) / np.float32(D))).astype(np.float32)
    angle = np.arange(T, dtype=np.float32)[:, None] * freq[None, :]
    angle = np.concatenate([angle, angle], 1).T
    sign = np.where(np.arange(D) < D // 2, -1.0, 1.0)[:, None]
    rope = np.stack([np.tile(np.cos(angle), (H, 1)), np.tile(np.sin(angle) * sign, (H, 1))], 1).astype(np.float32)
    q, k = np.arange(P)[:, None], np.arange(P)[None, :]
    before = (q < k).astype(np.float32)
    mask = np.stack([np.where(k > q, -1e30, 0.0), np.where(q > k, -1e30, 0.0)], 1).astype(np.float32)
    arrays = {
        "x": g["L0_attn_x"].reshape(TOK, C),
        "params": np.stack(columns, 1),
        "w_in": g["L0_attn_W_in"], "w_out": g["L0_attn_W_out"], "w_ffn": g["L0_ffn_weight"].T,
        "disha2": np.concatenate([g["L0_ffn_disha"], g["L0_ffn_disha"]], 0),
        "w_kvr": np.concatenate([g[L1 + "Wk"].T, g[L1 + "Wv"].T, g[L1 + "Wr"].T], 1), "w_o": g[L1 + "Wo"].T,
        "w_qk": np.concatenate([wq, wq[:, turned], wk, wk[:, turned]], 1), "w_v": wv, "w_proj": g[F + "proj_w"],
        "w_router": g[F + "router_w"], "w_up": g[F + "expert_wv"].transpose(1, 0, 2).reshape(C, E * 2 * FF),
        "w_down": g[F + "expert_proj"].reshape(E, FB, P, C).transpose(2, 0, 1, 3).reshape(P, E * FF),
        "ident": np.eye(P, dtype=np.float32), "rope": rope, "mask": mask,
        "pick": np.tile(np.arange(E, 0, -1, dtype=np.float32), (P, 1)),
        "before": before, "block": np.tile(np.arange(GB, dtype=np.float32) * P, (P, 1)),
        "code": (TOK - np.arange(TOK)).reshape(NT, P).T.astype(np.float32),
    }
    nc = bacc.Bacc("TRN2", target_bir_lowering=False, num_devices=1)
    data, args = {}, []
    for name, a in arrays.items():
        a = np.ascontiguousarray(a)
        data[f"in_{name}"] = a
        args.append(nc.dram_tensor(f"in_{name}", a.shape, mybir.dt.from_np(a.dtype), kind="ExternalInput").ap())
    o = nc.dram_tensor("out_0", [TOK, C], F32, kind="ExternalOutput").ap()
    model_kernel(nc, *args, o)
    r = run(nc, [data], core_ids=[0])
    return r.results[0]["out_0"].reshape(B, T, C)
```
